# Optimizing a Trainium2 kernel written in Bass

```python
import numpy as np
import jax
import jax.numpy as jnp

def _softmax(x, axis=-1):
    return jax.nn.softmax(x, axis=axis)

def _gelu(x):
    return jax.nn.gelu(x, approximate=True)

def _silu(x):
    return jax.nn.silu(x)

def _sigmoid(x):
    return jax.nn.sigmoid(x)

def _layernorm(x, axis=-1, eps=1e-05):
    m = jnp.mean(x, axis=axis, keepdims=True)
    v = jnp.var(x, axis=axis, keepdims=True)
    return (x - m) / jnp.sqrt(v + eps)

def _scatter_add(tgt, idx, src, axis=0):
    return tgt.at[idx].add(src)

def _segment_sum(src, seg, n):
    return jax.ops.segment_sum(src, seg, n)
kernel_name = 'mk_gnn_resnorm_d4_gnn_r32_3d9787'

def setup_inputs(seed: int=0):
    np.random.seed(seed)
    _w = jnp.asarray

    def _rec_inputs():
        import jax
        import jax.numpy as jnp
        _gk = jax.random.key(seed)
        x = -0.0005121 + 1.001 * jax.random.normal(jax.random.fold_in(_gk, 1), (3125, 32), jnp.float32)
        src = jax.random.randint(jax.random.fold_in(_gk, 2), (100000,), 0, 3125, jnp.int32)
        dst = jnp.minimum((3125 * jax.random.uniform(jax.random.fold_in(_gk, 3), (100000,)) ** 2.0).astype(jnp.int32), 99999)
        _o = jnp.argsort(dst, stable=True)
        src = src[_o]
        dst = dst[_o]
        edge_type_86 = jax.random.randint(jax.random.fold_in(_gk, 13), (100000,), 0, 86, jnp.int32)
        edge_weight = jax.random.uniform(jax.random.fold_in(_gk, 14), (100000,), jnp.float32, 0.0, 1)
        edge_weight1 = 0.000614103 + 0.999867 * jax.random.normal(jax.random.fold_in(_gk, 15), (100000, 1), jnp.float32)
        return (x, src, dst, edge_type_86, edge_weight, edge_weight1)
    x, src, dst, edge_type_86, edge_weight, edge_weight1 = _rec_inputs()

    def _L0_gnn_setup():
        import jax, jax.numpy as jnp
        import numpy as np
        N_NODES = 3125
        N_EDGES = 100000
        D_IN = 32
        N_HEADS = 4
        D_HEAD = 8
        key = jax.random.key(seed)
        k1, k2, k3, k4, k5, k6, k7 = jax.random.split(key, 7)
        scale = 1.0 / np.sqrt(D_IN)
        x = jax.random.normal(k1, (N_NODES, D_IN), dtype=jnp.float32)
        Wq = jax.random.normal(k2, (D_IN, N_HEADS * D_HEAD), dtype=jnp.float32) * scale
        Wk = jax.random.normal(k3, (D_IN, N_HEADS * D_HEAD), dtype=jnp.float32) * scale
        Wv = jax.random.normal(k4, (D_IN, N_HEADS * D_HEAD), dtype=jnp.float32) * scale
        Wo = jax.random.normal(k5, (N_HEADS * D_HEAD, D_IN), dtype=jnp.float32) * scale
        src = jax.random.randint(k6, (N_EDGES,), 0, N_NODES)
        dst = jax.random.randint(k7, (N_EDGES,), 0, N_NODES)
        edge_index = jnp.stack([src, dst], axis=0).astype(jnp.int64)
        return {'x': x, 'Wq': Wq, 'Wk': Wk, 'Wv': Wv, 'Wo': Wo, 'edge_index': edge_index}
    _L0_gnn_all = _L0_gnn_setup()
    _L0_gnn_in = {k: v for k, v in _L0_gnn_all.items() if k in ('Wq', 'Wk', 'Wv', 'Wo')}
    del _L0_gnn_all

    def _L1_gnn_setup():
        import jax, jax.numpy as jnp
        import numpy as np
        N_NODES = 50000
        N_EDGES = 25000
        INP_DIM = 32
        OUT_DIM = 32
        ATTN_DIM = 32
        NUM_RELS = 86
        NUM_BASES = 16
        GAMMA = 0.0
        key = jax.random.key(seed)
        ks = jax.random.split(key, 12)
        return {'h': jax.random.normal(ks[0], (N_NODES, INP_DIM), jnp.float32), 'weight': jax.random.normal(ks[1], (NUM_BASES, INP_DIM, OUT_DIM), jnp.float32), 'w_comp': jax.random.normal(ks[2], (NUM_RELS, NUM_BASES), jnp.float32), 'self_loop_weight': jax.random.normal(ks[3], (INP_DIM, OUT_DIM), jnp.float32), 'A1_w': jax.random.normal(ks[4], (ATTN_DIM, INP_DIM), jnp.float32), 'A1_b': jax.random.normal(ks[5], (ATTN_DIM,), jnp.float32), 'A2_w': jax.random.normal(ks[6], (ATTN_DIM, INP_DIM), jnp.float32), 'A2_b': jax.random.normal(ks[7], (ATTN_DIM,), jnp.float32), 'rel_emb': jax.random.normal(ks[8], (NUM_RELS, ATTN_DIM), jnp.float32), 'src': jax.random.randint(ks[9], (N_EDGES,), 0, N_NODES, jnp.int32), 'dst': jax.random.randint(ks[10], (N_EDGES,), 0, N_NODES, jnp.int32), 'etype': jax.random.randint(ks[11], (N_EDGES,), 0, NUM_RELS, jnp.int32)}
    _L1_gnn_all = _L1_gnn_setup()
    _L1_gnn_in = {k: v for k, v in _L1_gnn_all.items() if k in ('weight', 'w_comp', 'self_loop_weight', 'A1_w', 'A1_b', 'A2_w', 'A2_b', 'rel_emb')}
    del _L1_gnn_all

    def _L2_gnn_setup():
        import jax, jax.numpy as jnp
        import numpy as np
        N_NODES = 3125
        N_EDGES = 50000
        EMB_DIM = 32
        NUM_LAYERS = 3
        key = jax.random.key(seed)
        k_emb, k_w, k_row, k_col = jax.random.split(key, 4)
        emb = jax.random.normal(k_emb, (N_NODES, EMB_DIM), dtype=jnp.float32)
        edge_weight = jax.random.uniform(k_w, (N_EDGES,), dtype=jnp.float32)
        row = jax.random.randint(k_row, (N_EDGES,), 0, N_NODES, dtype=jnp.int32)
        col = jax.random.randint(k_col, (N_EDGES,), 0, N_NODES, dtype=jnp.int32)
        return {'emb': emb, 'edge_weight': edge_weight, 'row': row, 'col': col, 'num_layers': NUM_LAYERS}
    _L2_gnn_all = _L2_gnn_setup()
    _L2_gnn_in = {k: v for k, v in _L2_gnn_all.items() if k in ()}
    del _L2_gnn_all

    def _L3_gnn_setup():
        import jax, jax.numpy as jnp
        import numpy as np
        N = 50000
        E = 25000
        H = 8
        C = 32
        L = 3
        NEG_SLOPE = 0.2
        BN_EPS = 1e-05

        def gatv2_layer(x, Wl, bl, Wr, br, att, bias, src, dst, n):
            xl = (x @ Wl + bl).reshape(n, H, C)
            xr = (x @ Wr + br).reshape(n, H, C)
            e = jax.nn.leaky_relu(xl[src] + xr[dst], NEG_SLOPE)
            logits = jnp.einsum('ehc,hc->eh', e, att)
            m = jax.ops.segment_max(logits, dst, num_segments=n)
            m = jnp.where(jnp.isfinite(m), m, 0.0)
            p = jnp.exp(logits - jax.lax.stop_gradient(m)[dst])
            denom = jax.ops.segment_sum(p, dst, num_segments=n)
            alpha = p / (denom[dst] + 1e-16)
            out = jax.ops.segment_sum(xl[src] * alpha[:, :, None], dst, num_segments=n)
            return out.mean(axis=1) + bias

        def batchnorm_train(x, gamma, beta):
            mu = x.mean(axis=0)
            var = x.var(axis=0)
            return (x - mu) * jax.lax.rsqrt(var + BN_EPS) * gamma + beta
        key = jax.random.key(seed)
        ks = jax.random.split(key, 8)
        s = 1.0 / np.sqrt(C)
        return {'patch_embs': jax.random.normal(ks[0], (N, C), jnp.float32), 'edge_index': jax.random.randint(ks[1], (2, E), 0, N, dtype=jnp.int32), 'edge_attr': jax.random.normal(ks[2], (E, 1), jnp.float32), 'Wl': jax.random.normal(ks[3], (L, C, H * C), jnp.float32) * s, 'bl': jnp.zeros((L, H * C), jnp.float32), 'Wr': jax.random.normal(ks[4], (L, C, H * C), jnp.float32) * s, 'br': jnp.zeros((L, H * C), jnp.float32), 'att': jax.random.normal(ks[5], (L, H, C), jnp.float32) * s, 'conv_bias': jnp.zeros((L, C), jnp.float32), 'bn_gamma': jnp.ones((L, C), jnp.float32), 'bn_beta': jnp.zeros((L, C), jnp.float32)}
    _L3_gnn_all = _L3_gnn_setup()
    _L3_gnn_in = {k: v for k, v in _L3_gnn_all.items() if k in ('Wl', 'bl', 'Wr', 'br', 'att', 'conv_bias', 'bn_gamma', 'bn_beta')}
    del _L3_gnn_all
    return {'x': x, 'src': src, 'dst': dst, 'edge_type_86': edge_type_86, 'edge_weight': edge_weight, 'edge_weight1': edge_weight1, 'L0_gnn_Wq': _L0_gnn_in['Wq'], 'L0_gnn_Wk': _L0_gnn_in['Wk'], 'L0_gnn_Wv': _L0_gnn_in['Wv'], 'L0_gnn_Wo': _L0_gnn_in['Wo'], 'L1_gnn_weight': _L1_gnn_in['weight'], 'L1_gnn_w_comp': _L1_gnn_in['w_comp'], 'L1_gnn_self_loop_weight': _L1_gnn_in['self_loop_weight'], 'L1_gnn_A1_w': _L1_gnn_in['A1_w'], 'L1_gnn_A1_b': _L1_gnn_in['A1_b'], 'L1_gnn_A2_w': _L1_gnn_in['A2_w'], 'L1_gnn_A2_b': _L1_gnn_in['A2_b'], 'L1_gnn_rel_emb': _L1_gnn_in['rel_emb'], 'L3_gnn_Wl': _L3_gnn_in['Wl'], 'L3_gnn_bl': _L3_gnn_in['bl'], 'L3_gnn_Wr': _L3_gnn_in['Wr'], 'L3_gnn_br': _L3_gnn_in['br'], 'L3_gnn_att': _L3_gnn_in['att'], 'L3_gnn_conv_bias': _L3_gnn_in['conv_bias'], 'L3_gnn_bn_gamma': _L3_gnn_in['bn_gamma'], 'L3_gnn_bn_beta': _L3_gnn_in['bn_beta']}

def reference(x, src, dst, edge_type_86, edge_weight, edge_weight1, L0_gnn_Wq, L0_gnn_Wk, L0_gnn_Wv, L0_gnn_Wo, L1_gnn_weight, L1_gnn_w_comp, L1_gnn_self_loop_weight, L1_gnn_A1_w, L1_gnn_A1_b, L1_gnn_A2_w, L1_gnn_A2_b, L1_gnn_rel_emb, L3_gnn_Wl, L3_gnn_bl, L3_gnn_Wr, L3_gnn_br, L3_gnn_att, L3_gnn_conv_bias, L3_gnn_bn_gamma, L3_gnn_bn_beta):
    import jax
    import jax.numpy as jnp

    def _L0_gnn_ref(x, Wq, Wk, Wv, Wo, edge_index):
        import jax, jax.numpy as jnp
        import numpy as np
        N_NODES = 3125
        N_EDGES = 100000
        D_IN = 32
        N_HEADS = 4
        D_HEAD = 8
        N = x.shape[0]
        src, dst = (edge_index[0], edge_index[1])
        q = (x @ Wq).reshape(N, N_HEADS, D_HEAD)
        k = (x @ Wk).reshape(N, N_HEADS, D_HEAD)
        v = (x @ Wv).reshape(N, N_HEADS, D_HEAD)
        inv_sqrt_d = jnp.asarray(1.0 / np.sqrt(D_HEAD), dtype=x.dtype)
        scores = jnp.einsum('ehd,ehd->eh', q[dst], k[src]) * inv_sqrt_d
        m = jax.ops.segment_max(scores, dst, num_segments=N)
        m = jnp.where(jnp.isfinite(m), m, jnp.zeros_like(m))
        e = jnp.exp(scores - m[dst])
        denom = jax.ops.segment_sum(e, dst, num_segments=N)
        msg = jax.ops.segment_sum(e[:, :, None] * v[src], dst, num_segments=N)
        attn_out = msg / jnp.maximum(denom, 1e-16)[:, :, None]
        out = attn_out.reshape(N, N_HEADS * D_HEAD) @ Wo
        return x + out

    def _L1_gnn_ref(h, weight, w_comp, self_loop_weight, A1_w, A1_b, A2_w, A2_b, rel_emb, src, dst, etype):
        import jax, jax.numpy as jnp
        import numpy as np
        N_NODES = 50000
        N_EDGES = 25000
        INP_DIM = 32
        OUT_DIM = 32
        ATTN_DIM = 32
        NUM_RELS = 86
        NUM_BASES = 16
        GAMMA = 0.0
        E = src.shape[0]
        N = h.shape[0]
        x = h[src]
        y = h[dst]
        c = w_comp[etype]
        xb = jnp.einsum('ei,bio->ebo', x, weight)
        msg = jnp.einsum('eb,ebo->eo', c, xb)
        x_hat = x @ A1_w.T + A1_b
        y_hat = y @ A2_w.T + A2_b + rel_emb[etype]
        scale = jnp.sqrt(jnp.asarray(INP_DIM, h.dtype))
        a = jnp.tanh(jax.nn.relu(jnp.sum(x_hat * y_hat, axis=-1) / scale))
        a = jnp.where(a > GAMMA, a, jnp.zeros_like(a))
        nei = jax.ops.segment_sum(a[:, None] * msg, dst, num_segments=N)
        last_e = jax.ops.segment_max(jnp.arange(E, dtype=jnp.int32), dst, num_segments=N)
        last_e = jnp.clip(last_e, 0, E - 1)
        curr = h[src[last_e]] @ self_loop_weight
        in_deg = jax.ops.segment_sum(jnp.ones((E,), h.dtype), dst, num_segments=N)
        h_new = jnp.where((in_deg > 0)[:, None], nei + curr, jnp.zeros_like(nei))
        return jax.nn.relu(h_new)

    def _L2_gnn_ref(emb, edge_weight, row, col, num_layers):
        import jax, jax.numpy as jnp
        import numpy as np
        N_NODES = 3125
        N_EDGES = 50000
        EMB_DIM = 32
        NUM_LAYERS = 3
        n = emb.shape[0]
        w = edge_weight[:, None]
        X = emb
        for _ in range(num_layers):
            msgs = w * X[col]
            X = jax.ops.segment_sum(msgs, row, num_segments=n)
        return X

    def _L3_gnn_ref(patch_embs, edge_index, edge_attr, Wl, bl, Wr, br, att, conv_bias, bn_gamma, bn_beta):
        import jax, jax.numpy as jnp
        import numpy as np
        N = 50000
        E = 25000
        H = 8
        C = 32
        L = 3
        NEG_SLOPE = 0.2
        BN_EPS = 1e-05

        def gatv2_layer(x, Wl, bl, Wr, br, att, bias, src, dst, n):
            xl = (x @ Wl + bl).reshape(n, H, C)
            xr = (x @ Wr + br).reshape(n, H, C)
            e = jax.nn.leaky_relu(xl[src] + xr[dst], NEG_SLOPE)
            logits = jnp.einsum('ehc,hc->eh', e, att)
            m = jax.ops.segment_max(logits, dst, num_segments=n)
            m = jnp.where(jnp.isfinite(m), m, 0.0)
            p = jnp.exp(logits - jax.lax.stop_gradient(m)[dst])
            denom = jax.ops.segment_sum(p, dst, num_segments=n)
            alpha = p / (denom[dst] + 1e-16)
            out = jax.ops.segment_sum(xl[src] * alpha[:, :, None], dst, num_segments=n)
            return out.mean(axis=1) + bias

        def batchnorm_train(x, gamma, beta):
            mu = x.mean(axis=0)
            var = x.var(axis=0)
            return (x - mu) * jax.lax.rsqrt(var + BN_EPS) * gamma + beta
        n = patch_embs.shape[0]
        loops = jnp.arange(n, dtype=edge_index.dtype)
        src = jnp.concatenate([edge_index[0], loops])
        dst = jnp.concatenate([edge_index[1], loops])
        x = patch_embs
        h1 = gatv2_layer(x, Wl[0], bl[0], Wr[0], br[0], att[0], conv_bias[0], src, dst, n)
        x = batchnorm_train(jax.nn.leaky_relu(h1, 0.01) + x, bn_gamma[0], bn_beta[0])
        h2 = gatv2_layer(x, Wl[1], bl[1], Wr[1], br[1], att[1], conv_bias[1], src, dst, n)
        x = batchnorm_train(jax.nn.leaky_relu(h2, 0.01) + x, bn_gamma[1], bn_beta[1])
        h3 = gatv2_layer(x, Wl[2], bl[2], Wr[2], br[2], att[2], conv_bias[2], src, dst, n)
        x = batchnorm_train(h3 + x, bn_gamma[2], bn_beta[2])
        return x
    edge_index = jnp.stack([src, dst])
    x = _layernorm(x + _L0_gnn_ref(x, L0_gnn_Wq, L0_gnn_Wk, L0_gnn_Wv, L0_gnn_Wo, edge_index), axis=-1)
    x = _layernorm(x + _L1_gnn_ref(x, L1_gnn_weight, L1_gnn_w_comp, L1_gnn_self_loop_weight, L1_gnn_A1_w, L1_gnn_A1_b, L1_gnn_A2_w, L1_gnn_A2_b, L1_gnn_rel_emb, src, dst, edge_type_86), axis=-1)
    x = _layernorm(x + _L2_gnn_ref(x, edge_weight, src, dst, 3), axis=-1)
    x = _layernorm(x + _L3_gnn_ref(x, edge_index, edge_weight1, L3_gnn_Wl, L3_gnn_bl, L3_gnn_Wr, L3_gnn_br, L3_gnn_att, L3_gnn_conv_bias, L3_gnn_bn_gamma, L3_gnn_bn_beta), axis=-1)
    return x

_drawn_inputs = setup_inputs


def setup_inputs(seed=0):
    import zlib

    import numpy as np

    out = dict(_drawn_inputs(seed))
    spreads = {'L3_gnn_bl': (0.0, 1.396),
     'L3_gnn_br': (0.0, 2.0),
     'L3_gnn_conv_bias': (0.0, 0.326),
     'L3_gnn_bn_gamma': (1.0, 0.2),
     'L3_gnn_bn_beta': (0.0, 0.1)}
    factors = {'L3_gnn_Wr': 2.698}
    for name, (base, spread) in spreads.items():
        noise = np.random.default_rng([zlib.crc32(name.encode()), seed]).standard_normal(out[name].shape)
        drawn = base * np.exp(spread * noise) if base else spread * noise
        out[name] = jnp.asarray(drawn.astype(out[name].dtype))
    for name, factor in factors.items():
        out[name] = (out[name] * factor).astype(out[name].dtype)
    return out
```

```python
from contextlib import ExitStack

import concourse.bass as bass
from concourse import mybir

F32 = mybir.dt.float32
I32 = mybir.dt.int32
U32 = mybir.dt.uint32
ALU = mybir.AluOpType
ACT = mybir.ActivationFunctionType
AX = mybir.AxisListType

P = 128
D = 32
N, E = 3125, 100000
K = 4
GE = K * P
NB = -(-N // P)
NP = NB * P
TAIL = N - (NB - 1) * P
RING = 4
G = -(-((E + NB * (GE - 1)) // GE) // RING) * RING
SL = G * GE
RUN = SL // P
EP = 125
EF = E // EP
NREL, NBASE = 86, 16
TILES = -(-E // (P * K * RING)) * K * RING
H0 = 4
H3 = 8
W3 = H3 * D
TAB3 = W3 + D
ACC0 = D + H0
ACC1 = NBASE * D + D
ACC3 = W3 + 2 * H3 + 1
BIG = 1e30
LN_EPS = 1e-5
assert EP * EF == E and RUN * P == SL and EF == RUN - 80


class Stage:

    def __init__(self, nc, tag):
        self.nc, self.tag, self.made = nc, tag, {}

    def __call__(self, name):
        if name not in self.made:
            self.made[name] = self.nc.alloc_semaphore(name=f"{self.tag}_{name}")
        return self.made[name]


def need(eng, sem, value):
    if not isinstance(value, int) or value > 0:
        eng.wait_ge(sem, value)


def groups(eng, body, turns=G // RING):
    for i in range(2):
        for u in range(RING):
            body(i, u)
    with eng.Fori(2, turns, 1) as i:
        for u in range(RING):
            body(i, u)


class Mem:
    pass


def allocate(nc, ctx):
    m = Mem()

    def sb(name, shape, dt=F32):
        t = ctx.enter_context(nc.sbuf_tensor(name, shape, dt))
        return t

    m.ident = sb("ident", [P, P])
    m.iota_row = sb("iota_row", [P, P])
    m.ones = sb("ones", [P, P])
    m.upper = sb("upper", [NB, NB])
    m.src_i = sb("src_i", [P, G + 1, K], I32)
    m.rel = sb("rel", [P, G + 1, K])
    m.et_f = sb("et_f", [P, G + 1, K])
    m.first_t = sb("first_t", [P, G, K])
    m.last_t = sb("last_t", [P, G, K])
    m.new_seg = sb("new_seg", [P, RUN])
    m.end_seg = sb("end_seg", [P, RUN])
    m.blk_i = sb("blk_i", [1, G + 1], I32)
    m.X = sb("X", [P, NB, D])
    m.Y = sb("Y", [P, NB, D])
    m.Z = sb("Z", [P, NB, D])
    m.XT = sb("XT", [D + 1, NP])
    rows = sb("rows", [P, NB * W3])
    m.R = rows[:, :].rearrange("p (b w) -> p b w", b=NB)
    wr = D + NBASE
    m.Rr = rows[:, 0:NB * wr].rearrange("p (b w) -> p b w", b=NB)
    at = NB * wr
    m.typ = rows[:, at:at + 2 * K * NREL].rearrange("p (n k r) -> p n k r", n=2, k=K)
    at += 2 * K * NREL
    m.typT = rows[0:NREL, at:at + 2 * K * P].rearrange("p (n w) -> p n w", n=2)
    m.big = sb("big", [P, 2 * RUN * H3])
    at = K * NB * D
    m.w_e = m.big[:, at:at + TILES]
    at += TILES
    m.dst_i = m.big[:, at:at + TILES + K].bitcast(I32)
    at += TILES + K
    m.src_low = m.big[:, at:at + TILES + K]
    at += TILES + K
    m.src_blk = m.big[:, at:at + TILES]
    m.gx = sb("gx", [P, RING, K, TAB3])
    m.gi = sb("gi", [P, RING, K], I32)
    m.oh = sb("oh", [P, 2, K, P])
    m.ohT = sb("ohT", [P, 2, K * P])
    m.work = sb("work", [P, 2, K * NBASE * D])
    m.lg = sb("lg", [P, RING, K * H3])
    m.pr = sb("pr", [P, RING, 2, K * H3])
    m.xl = sb("xl", [P, RING, K, D])
    m.a1 = sb("a1", [P, 2, 4, K])
    m.sblk = m.work[:, 0, 0:2 * K * NB].rearrange("p (n k b) -> p n k b", n=2, k=K)
    m.zeros = m.work[:, 1, 0:512]
    m.ac = sb("ac", [P, 2, K, NBASE])
    m.lx = sb("lx", [P, 2, K, D])
    m.self3 = sb("self3", [P, NB, H3])
    m.small = sb("small", [P, 5, NB, H3])
    m.line = sb("line", [P, 4, NB])
    m.c8 = sb("c8", [P, 6, H3])
    m.r8 = sb("r8", [H3, 4, P])
    m.bnv = sb("bnv", [P, 4, D])
    m.w3 = sb("w3", [D + 1, 3, 2 * W3])
    m.w3o = sb("w3o", [P, 3, 2, D])
    m.att3 = sb("att3", [P, 3, W3])
    m.bn = sb("bn", [P, 3, 2, D])
    m.brow = sb("brow", [1, 3, W3 + 2 * D])
    m.w0 = sb("w0", [D, 3 * D])
    m.wo0 = sb("wo0", [D, D])
    m.w1 = sb("w1", [D + 1, 2 * D])
    m.w1b = sb("w1b", [P, 4, D])
    m.w1s = sb("w1s", [D, D])
    m.relt = sb("relt", [NREL, D + NBASE])
    m.col = sb("col", [P, 8])
    m.coli = sb("coli", [P, 1], I32)
    m.eps = sb("eps", [P, 1])
    m.guard = sb("guard", [1, 1])
    m.psA = ctx.enter_context(nc.psum_tensor("psA", [P, 2, 1024], F32))
    m.psT = ctx.enter_context(nc.psum_tensor("psT", [P, 2, 512], F32))
    m.psC = ctx.enter_context(nc.psum_tensor("psC", [P, 2, 512], F32))

    def dram(name, shape):
        return nc.dram_tensor(name, shape, F32, kind="Internal").ap()

    m.key_d = dram("key_d", [SL + 2])
    m.first_d = dram("first_d", [SL])
    m.last_d = dram("last_d", [SL])
    m.table_d = {n: dram(f"table_{n}", [NP, w]) for n, w in
                 (("t", 2 * D), ("r", 2 * D), ("s0", D), ("s1", D), ("s2", D), ("g0", TAB3), ("g1", TAB3), ("g2", TAB3))}
    soft = (("t", H0), ("g0", H3), ("g1", H3), ("g2", H3))
    m.xs_d = {n: dram(f"xs_{n}", [SL, D]) for n, _ in soft}
    m.logit_d = {n: dram(f"logit_{n}", [SL, h]) for n, h in soft}
    m.prob_d = {n: dram(f"prob_{n}", [SL, h]) for n, h in soft}
    m.max_d = {n: dram(f"max_{n}", [SL, h]) for n, h in soft}
    return m



def constants(nc, m, a):
    with ExitStack() as ctx:
        s = Stage(nc, "const")
        block = ctx.enter_context(nc.Block())
        LOADS = []
        bias = D
        LOADS.append((m.X[:, 0:NB - 1, :], a["x"][0:(NB - 1) * P, :].rearrange("(b p) d -> p b d", p=P)))
        LOADS.append((m.X[0:TAIL, NB - 1, :], a["x"][(NB - 1) * P:N, :]))
        for n, w in enumerate(("L0_gnn_Wk", "L0_gnn_Wv", "L0_gnn_Wq")):
            LOADS.append((m.w0[:, n * D:(n + 1) * D], a[w]))
        LOADS.append((m.wo0[:, :], a["L0_gnn_Wo"]))
        for n, (w, b) in enumerate((("L1_gnn_A1_w", "L1_gnn_A1_b"), ("L1_gnn_A2_w", "L1_gnn_A2_b"))):
            LOADS.append((m.w1[0:D, n * D:(n + 1) * D], a[w].rearrange("o i -> i o")))
            LOADS.append((m.w1[bias:bias + 1, n * D:(n + 1) * D], a[b].rearrange("(a o) -> a o", a=1)))
        LOADS.append((m.w1b[:, :, :], a["L1_gnn_weight"].rearrange("(t q) i o -> (q i) t o", q=4)))
        LOADS.append((m.w1s[:, :], a["L1_gnn_self_loop_weight"]))
        LOADS.append((m.relt[:, 0:D], a["L1_gnn_rel_emb"]))
        LOADS.append((m.relt[:, D:D + NBASE], a["L1_gnn_w_comp"]))
        for l in range(3):
            for n, (w, b) in enumerate((("L3_gnn_Wl", "L3_gnn_bl"), ("L3_gnn_Wr", "L3_gnn_br"))):
                LOADS.append((m.w3[0:D, l, n * W3:(n + 1) * W3], a[w][l]))
                LOADS.append((m.w3[bias:bias + 1, l, n * W3:(n + 1) * W3], a[b][l:l + 1]))
            for h in range(H3):
                LOADS.append((m.w3o[(h % 4) * D:(h % 4 + 1) * D, l, h // 4, :],
                              a["L3_gnn_Wl"][l, :, h * D:(h + 1) * D]))
            LOADS.append((m.att3[:, l, :], a["L3_gnn_att"][l].rearrange("(a h) c -> a (h c)", a=1).to_broadcast([P, W3])))
            for n, w in enumerate(("L3_gnn_bn_gamma", "L3_gnn_bn_beta")):
                LOADS.append((m.bn[:, l, n, :], a[w][l:l + 1].to_broadcast([P, D])))
            LOADS.append((m.brow[:, l, 0:W3], a["L3_gnn_bl"][l:l + 1]))
            LOADS.append((m.brow[:, l, W3:W3 + D], a["L3_gnn_conv_bias"][l:l + 1]))

        @block.vector
        def _(dve):
            nc.vector.memset(m.X[:, NB - 1, :], 0.0).then_inc(s("xzero"), 1)
            nc.vector.memset(m.ones[:, :], 1.0).then_inc(s("ones"), 1)
            nc.vector.memset(m.XT[D:D + 1, :], 1.0)
            nc.vector.memset(m.rel[:, G, :], -1.0)
            nc.vector.memset(m.et_f[:, G, :], -1.0)
            nc.vector.memset(m.eps[:, :], LN_EPS)
            nc.vector.memset(m.guard[:, :], -5.0)
            dve.wait_ge(s("loads"), 16 * len(LOADS))
            nc.vector.tensor_scalar(m.w3o[:, :, :, :], m.w3o[:, :, :, :], 1.0 / H3, None, ALU.mult)
            nc.vector.tensor_reduce(m.brow[:, :, W3 + D:W3 + 2 * D],
                                    m.brow[:, :, 0:W3].rearrange("p l (h c) -> p l c h", h=H3), AX.X, ALU.add
                                    ).then_inc(s("brow"), 1)
            dve.wait_ge(s("brow"), 1)
            nc.vector.tensor_scalar(m.brow[:, :, 0:D], m.brow[:, :, W3 + D:W3 + 2 * D], 1.0 / H3, None,
                                    ALU.mult).then_inc(s("brow"), 1)
            dve.wait_ge(s("brow"), 2)
            nc.vector.tensor_tensor(m.brow[:, :, W3:W3 + D], m.brow[:, :, W3:W3 + D], m.brow[:, :, 0:D], ALU.add)

        @block.gpsimd
        def _(pool):
            pool.wait_ge(s("ones"), 1)
            nc.gpsimd.affine_select(out=m.ident[:, :], in_=m.ones[:, :], compare_op=ALU.is_equal, fill=0.0,
                                    base=0, pattern=[[-1, P]], channel_multiplier=1)
            nc.gpsimd.affine_select(out=m.upper[:, :], in_=m.ones[0:NB, 0:NB], compare_op=ALU.is_gt, fill=0.0,
                                    base=0, pattern=[[1, NB]], channel_multiplier=-1)
            nc.gpsimd.iota(m.iota_row[:, :], [[1, P]], base=0, channel_multiplier=0,
                           allow_small_or_imprecise_dtypes=True)
            nc.gpsimd.memset(m.src_i[:, G, :], 0)
            nc.gpsimd.memset(m.blk_i[:, G:G + 1], 0)

        @block.sync
        def _(sp):
            sp.wait_ge(s("xzero"), 1)
            for n, (dst, src) in enumerate(LOADS):
                sp.dma_start(dst, src, allow_slow_non_contiguous=True).then_inc(s("loads"), 16)
            sp.wait_ge(s("loads"), 16 * len(LOADS))


def cut(nc, m, a):
    b = m.big
    dst_i = b[0:EP, 0:EF].bitcast(I32)
    dst_f = b[0:EP, EF:2 * EF]
    below = b[0:EP, 2 * EF:3 * EF]
    counts = b[0:EP, 3 * EF:3 * EF + NB + 1]
    at = 3 * EF + 32
    g_no, mask, val = (b[0:NB, at + n * G:at + (n + 1) * G] for n in range(3))
    at += 3 * G
    blk128 = b[:, at:at + G]
    row1 = b[0:1, at + G:at + 2 * G]
    row2 = b[0:1, at + 2 * G:at + 3 * G]
    start_i = b[0:1, at + 3 * G:at + 4 * G].bitcast(I32)
    at += 4 * G

    def slots(n):
        return b[:, at + n * G * K:at + (n + 1) * G * K].rearrange("p (g k) -> p g k", k=K)
    slot_dst, slot_et, slot_f, valid = slots(0).bitcast(I32), slots(1).bitcast(I32), slots(2), slots(3)
    col = m.col
    first, nxt, t1, ng, g0, g1, off, num = (col[0:NB, n:n + 1] for n in range(8))
    bcol = b[0:NB, at + 4 * G * K:at + 4 * G * K + P]

    with ExitStack() as ctx:
        s = Stage(nc, "cut")
        block = ctx.enter_context(nc.Block())

        @block.vector
        def _(dve):
            n = [0]

            def step(ins):
                n[0] += 1
                ins.then_inc(s("v"), 1)
                dve.wait_ge(s("v"), n[0])
            dve.wait_ge(s("dst"), 16)
            step(nc.vector.tensor_copy(dst_f, dst_i))
            for j in range(NB + 1):
                step(nc.vector.tensor_scalar(below, dst_f, float(j * P), None, ALU.is_lt))
                step(nc.vector.tensor_reduce(counts[:, j:j + 1], below, AX.X, ALU.add))
            dve.sem_inc(s("counts"), 1)
            dve.wait_ge(s("sums"), 1)
            nc.vector.tensor_copy(first, m.psC[0:NB, 0, 0:1])
            step(nc.vector.tensor_copy(nxt, m.psC[0:NB, 0, 1:2]))
            step(nc.vector.tensor_tensor(t1, nxt, first, ALU.subtract))
            step(nc.vector.tensor_scalar(t1, t1, float(GE - 1), None, ALU.add))
            step(nc.vector.tensor_copy(m.coli[0:NB, :], t1))
            step(nc.vector.tensor_scalar(m.coli[0:NB, :], m.coli[0:NB, :], GE.bit_length() - 1, None,
                                         ALU.arith_shift_right))
            step(nc.vector.tensor_copy(ng, m.coli[0:NB, :]))
            dve.sem_inc(s("ng"), 1)
            dve.wait_ge(s("sums"), 2)
            step(nc.vector.tensor_copy(g0, m.psC[0:NB, 0, 2:3]))
            step(nc.vector.tensor_tensor(g1, g0, ng, ALU.add))
            step(nc.vector.tensor_scalar(off, g0, float(-GE), None, ALU.mult))
            step(nc.vector.tensor_tensor(off, off, first, ALU.add))
            dve.wait_ge(s("iota"), 1)
            step(nc.vector.tensor_scalar(mask, g_no, g1, None, ALU.is_lt))
            step(nc.vector.tensor_scalar(val, g_no, g0, None, ALU.is_ge))
            step(nc.vector.tensor_tensor(mask, mask, val, ALU.mult))
            step(nc.vector.tensor_scalar(val, g_no, float(GE), off, ALU.mult, ALU.add))
            step(nc.vector.tensor_tensor(val, val, mask, ALU.mult))
            step(nc.vector.tensor_scalar(bcol, m.ones[0:NB, :], num, None, ALU.mult))
            dve.sem_inc(s("masks"), 1)
            dve.wait_ge(s("sums"), 3)
            step(nc.vector.tensor_scalar(row1, m.psC[0:1, 0, G:2 * G], float(-E), float(E), ALU.mult, ALU.add))
            step(nc.vector.tensor_tensor(row1, row1, m.psC[0:1, 0, 0:G], ALU.add))
            nc.vector.tensor_copy(start_i, row1).then_inc(s("starts"), 1)
            step(nc.vector.tensor_copy(m.blk_i[:, 0:G], m.psC[0:1, 1, 0:G]))
            step(nc.vector.tensor_scalar(blk128, m.psC[:, 1, 0:G], float(P), None, ALU.mult))
            dve.wait_ge(s("slot_sp"), 16 * 2 * G)
            dve.wait_ge(s("slot_act"), 16 * G)
            nc.vector.tensor_copy(m.et_f[:, 0:G, :], slot_et)
            step(nc.vector.tensor_copy(slot_f, slot_dst))
            rel = m.rel[:, 0:G, :]
            step(nc.vector.tensor_tensor(rel, slot_f, blk128.unsqueeze(2).to_broadcast([P, G, K]), ALU.subtract))
            step(nc.vector.tensor_scalar(valid, rel, float(P), None, ALU.is_lt))
            step(nc.vector.tensor_scalar(slot_f, slot_f, 1.0, None, ALU.add))
            step(nc.vector.tensor_tensor(slot_f, slot_f, valid, ALU.mult))
            step(nc.vector.tensor_scalar(slot_f, slot_f, -1.0, None, ALU.add))
            dve.sem_inc(s("keys"), 1)

        @block.gpsimd
        def _(pool):
            nc.gpsimd.iota(g_no, [[1, G]], base=0, channel_multiplier=0, allow_small_or_imprecise_dtypes=True)
            nc.gpsimd.iota(num, [[0, 1]], base=0, channel_multiplier=1,
                           allow_small_or_imprecise_dtypes=True).then_inc(s("iota"), 1)

        @block.tensor
        def _(pe):
            pe.wait_ge(s("counts"), 1)
            nc.tensor.matmul(m.psC[0:NB, 0, 0:1], counts[:, 0:NB], m.ones[0:EP, 0:1], start=True, stop=True)
            nc.tensor.matmul(m.psC[0:NB, 0, 1:2], counts[:, 1:NB + 1], m.ones[0:EP, 0:1], start=True,
                             stop=True).then_inc(s("sums"), 1)
            pe.wait_ge(s("ng"), 1)
            nc.tensor.matmul(m.psC[0:NB, 0, 2:3], m.upper[:, :], ng, start=True, stop=True).then_inc(s("sums"), 1)
            pe.wait_ge(s("masks"), 1)
            nc.tensor.matmul(m.psC[0:1, 0, 0:G], m.ones[0:NB, 0:1], val, start=True, stop=True)
            nc.tensor.matmul(m.psC[0:1, 0, G:2 * G], m.ones[0:NB, 0:1], mask, start=True, stop=True)
            nc.tensor.matmul(m.psC[:, 1, 0:G], bcol, mask, start=True, stop=True).then_inc(s("sums"), 1)

        def loads(eng, name, pairs):
            def body(g):
                start = eng.value_load(start_i[0:1, bass.ds(g, 1)], min_val=0, max_val=E)
                for dst, src in pairs:
                    eng.dma_start(dst[:, bass.ds(g, 1), :].rearrange("p a k -> p (a k)"),
                                  src[bass.ds(start, GE)].rearrange("(p k) -> p k", k=K)).then_inc(s(name), 16)
            eng.wait_ge(s("starts"), 1)
            with eng.Fori(0, G, 1) as g:
                body(g)

        @block.sync
        def _(sp):
            sp.dma_start(dst_i, a["dst"][0:E].rearrange("(p f) -> p f", p=EP)).then_inc(s("dst"), 16)
            loads(sp, "slot_sp", ((slot_dst, a["dst"]), (m.src_i, a["src"])))
            sp.wait_ge(s("keys"), 1)
            sp.dma_start(m.key_d[1:SL + 1].rearrange("(g p k) -> p g k", p=P, k=K), slot_f).then_inc(s("out"), 16)
            sp.dma_start(m.key_d[0:1].rearrange("(a k) -> a k", a=1), m.guard[:, :]).then_inc(s("out"), 16)
            sp.dma_start(m.key_d[SL + 1:SL + 2].rearrange("(a k) -> a k", a=1), m.guard[:, :]).then_inc(s("out"), 16)
            sp.wait_ge(s("out"), 48)

        @block.scalar
        def _(act):
            loads(act, "slot_act", ((slot_et, a["edge_type_86"]),))

    prev, own, nxt_k, f1, f2 = (b[:, n * RUN:(n + 1) * RUN] for n in range(5))
    with ExitStack() as ctx:
        s = Stage(nc, "runs")
        block = ctx.enter_context(nc.Block())

        @block.sync
        def _(sp):
            for n, t in enumerate((prev, own, nxt_k)):
                sp.dma_start(t, m.key_d[n:n + SL].rearrange("(p f) -> p f", p=P)).then_inc(s("keys"), 16)
            sp.wait_ge(s("flags"), 1)
            for t, d in ((f1, m.first_d), (f2, m.last_d)):
                sp.dma_start(d.rearrange("(p f) -> p f", p=P), t).then_inc(s("out"), 16)
            sp.wait_ge(s("out"), 32)
            for t, d in ((m.first_t, m.first_d), (m.last_t, m.last_d)):
                sp.dma_start(t[:, :, :], d.rearrange("(g p k) -> p g k", p=P, k=K)).then_inc(s("in"), 16)
            sp.wait_ge(s("in"), 32)

        @block.vector
        def _(dve):
            dve.wait_ge(s("keys"), 48)
            nc.vector.tensor_tensor(f1, own, prev, ALU.not_equal)
            nc.vector.tensor_tensor(f2, own, nxt_k, ALU.not_equal).then_inc(s("flags"), 1)
            dve.wait_ge(s("flags"), 1)
            nc.vector.tensor_scalar(m.new_seg[:, :], f1, -BIG, None, ALU.mult)
            nc.vector.tensor_scalar(m.end_seg[:, :], f2, -BIG, None, ALU.mult)



def transposed(nc, m, name):
    with ExitStack() as ctx:
        s = Stage(nc, f"xt_{name}")
        block = ctx.enter_context(nc.Block())
        steps = [range(b, min(b + 4, NB)) for b in range(0, NB, 4)]

        @block.tensor
        def _(pe):
            for n, bs in enumerate(steps):
                need(pe, s("copied"), n - 1)
                for b in bs:
                    ins = nc.tensor.transpose(m.psT[0:D, n % 2, (b - bs[0]) * P:(b - bs[0] + 1) * P], m.X[:, b, :],
                                              m.ident[:, :])
                ins.then_inc(s("turned"), 1)

        @block.scalar
        def _(act):
            for n, bs in enumerate(steps):
                act.wait_ge(s("turned"), n + 1)
                nc.scalar.copy(m.XT[0:D, bs[0] * P:(bs[-1] + 1) * P], m.psT[0:D, n % 2, 0:len(bs) * P]
                               ).then_inc(s("copied"), 1)


def tables(nc, m, name, weights, keep, width, tab, side):
    w = m.table_d[name].shape[1]
    out = m.big[:, 0:NB * w].rearrange("p (b w) -> p b w", b=NB)
    rows = D + 1 if keep else D
    with ExitStack() as ctx:
        s = Stage(nc, f"tab_{name}")
        block = ctx.enter_context(nc.Block())

        @block.tensor
        def _(pe):
            for b in range(NB):
                need(pe, s("side"), b - 1)
                nc.tensor.matmul(m.psA[:, b % 2, 0:width], m.XT[0:rows, b * P:(b + 1) * P], weights, start=True,
                                 stop=True).then_inc(s("made"), 1)

        @block.scalar
        def _(act):
            for b in range(NB):
                act.wait_ge(s("made"), b + 1)
                tab(out[:, b, :], m.psA[:, b % 2, :]).then_inc(s("tab"), 1)

        @block.vector
        def _(dve):
            if w > W3 or name == "r":
                lo = W3 if w > W3 else 0
                nc.vector.tensor_copy(out[:, :, lo:lo + D], m.X[:, :, :]).then_inc(s("x"), 1)
            else:
                dve.sem_inc(s("x"), 1)
            for b in range(NB):
                dve.wait_ge(s("tab"), b + 1)
                side(b, m.psA[:, b % 2, :]).then_inc(s("side"), 1)

        @block.sync
        def _(sp):
            sp.wait_ge(s("x"), 1)
            sp.wait_ge(s("tab"), NB)
            sp.dma_start(m.table_d[name].rearrange("(b p) w -> p b w", p=P), out).then_inc(s("out"), 16)
            sp.wait_ge(s("out"), 16)



def normalised(nc, m, tag, addends, relu=False):
    with ExitStack() as ctx:
        s = Stage(nc, f"ln_{tag}")
        block = ctx.enter_context(nc.Block())
        mean, var = m.line[:, 0, :], m.line[:, 1, :]
        wide = [P, NB, D]

        @block.vector
        def _(dve):
            n = [0]

            def step(ins):
                n[0] += 1
                ins.then_inc(s("v"), 1)
                dve.wait_ge(s("v"), n[0])
            total = addends[0]
            for t in addends[1:]:
                step(nc.vector.tensor_tensor(m.Z[:, :, :], total[:, :, :], t[:, :, :], ALU.add))
                total = m.Z
            step(nc.vector.tensor_reduce(mean, m.Z[:, :, :], AX.X, ALU.add))
            step(nc.vector.tensor_scalar(mean, mean, 1.0 / D, None, ALU.mult))
            step(nc.vector.tensor_tensor(m.Z[:, :, :], m.Z[:, :, :], mean.unsqueeze(2).to_broadcast(wide),
                                         ALU.subtract))
            step(nc.vector.tensor_tensor(m.X[:, :, :], m.Z[:, :, :], m.Z[:, :, :], ALU.mult))
            step(nc.vector.tensor_reduce(var, m.X[:, :, :], AX.X, ALU.add))
            dve.sem_inc(s("var"), 1)
            dve.wait_ge(s("root"), 1)
            step(nc.vector.reciprocal(var, var))
            nc.vector.tensor_tensor(m.X[:, :, :], m.Z[:, :, :], var.unsqueeze(2).to_broadcast(wide), ALU.mult)

        @block.scalar
        def _(act):
            act.wait_ge(s("var"), 1)
            nc.scalar.activation(var, var, ACT.Sqrt, bias=m.eps[:, 0:1], scale=1.0 / D).then_inc(s("root"), 1)



def gather(nc, m, s, pool, table, w, used, stored=False, index=None, tiles=G * K):
    def indices(g, slot):
        at = m.src_i[:, bass.ds(g, 1), :].rearrange("p a k -> p (a k)") if index is None else \
            index[:, bass.ds(g * K, K)]
        nc.gpsimd.tensor_copy(m.gi[:, slot, :], at).then_inc(s("indices"), 1)

    def body(i, u):
        g = i * RING + u
        ahead = (u + 1) % RING
        need(pool, s(f"rows{ahead}"), 16 * K * (i if ahead else i + 1))
        indices(g + 1, ahead)
        need(pool, used, g - RING + 1)
        if stored:
            need(pool, s(f"xs{u}"), 16 * i)
        pool.wait_ge(s("indices"), g + 1)
        pool.sem_inc(s("ticket"), 1)
        for k in range(K):
            pool.indirect_dma_start(m.gx[:, u, k, 0:w], None, table,
                                    bass.IndirectOffsetOnAxis(m.gi[:, u, k:k + 1].bitcast(U32), 0)
                                    ).then_inc(s(f"rows{u}"), 16)
    indices(0, 0)
    groups(pool, body, tiles // (K * RING))


def one_hot(nc, m, g, half):
    return nc.vector.tensor_tensor(
        m.oh[:, half, :, :], m.iota_row[:, :].unsqueeze(1).to_broadcast([P, K, P]),
        m.rel[:, bass.ds(g, 1), :].rearrange("p a k -> p (a k)").unsqueeze(2).to_broadcast([P, K, P]),
        ALU.is_equal)


def add_up(nc, m, dve, g, w, ps):
    blk = dve.value_load(m.blk_i[0:1, bass.ds(g, 1)], min_val=0, max_val=NB - 1)
    acc = m.big[:, 0:NB * w].rearrange("p (b w) -> p b w", b=NB)[:, bass.ds(blk, 1), :].rearrange(
        "p a w -> p (a w)")
    return nc.vector.tensor_tensor(acc, acc, ps, ALU.add)


def logits(nc, m, name, heads, cols, layer):
    w = m.table_d[name].shape[1]
    dh = cols // heads
    gat = layer is not None

    def prod(half):
        return m.work[:, half, 0:K * cols]

    with ExitStack() as ctx:
        s = Stage(nc, f"log_{name}")
        block = ctx.enter_context(nc.Block())

        @block.gpsimd
        def _(pool):
            gather(nc, m, s, pool, m.table_d[name], w, s("summed"), True)

        @block.vector
        def _(dve):
            def reduce(i, u):
                g = i * RING + u
                half = u % 2
                if gat:
                    dve.wait_ge(s("summed"), g + 1)
                    nc.vector.scalar_tensor_tensor(out=prod(half), in0=prod(half), scalar=0.2, in1=prod(half),
                                                   op0=ALU.mult, op1=ALU.max).then_inc(s("leaky"), 1)
                    dve.wait_ge(s("leaky"), g + 1)
                    t = prod(half).rearrange("p (k c) -> p k c", k=K)
                    nc.vector.tensor_tensor(t, t, m.att3[:, layer, :].unsqueeze(1).to_broadcast([P, K, cols]),
                                            ALU.mult).then_inc(s("weighted"), 1)
                    dve.wait_ge(s("weighted"), g + 1)
                else:
                    dve.wait_ge(s("summed"), g + 1)
                need(dve, s(f"lg{u}"), 16 * i)
                nc.vector.tensor_reduce(m.lg[:, u, 0:K * heads],
                                        prod(half).rearrange("p (k c) -> p k c", c=dh), AX.X, ALU.add
                                        ).then_inc(s("logits"), 1)

            def body(i, u):
                g = i * RING + u
                need(dve, s("turned"), g)
                one_hot(nc, m, g + 1, (u + 1) % 2).then_inc(s("one_hot"), 1)
                dve.wait_ge(s(f"rows{u}"), 16 * K * (i + 1))
                dve.wait_ge(s("projected"), g + 1)
                need(dve, s("logits"), g - 1)
                nc.vector.tensor_tensor(prod(u % 2).rearrange("p (k c) -> p k c", k=K), m.gx[:, u, :, 0:cols],
                                        m.psA[:, u % 2, 0:K * cols].rearrange("p (k c) -> p k c", k=K),
                                        ALU.add if gat else ALU.mult).then_inc(s("summed"), 1)
                if u:
                    reduce(i, u - 1)
                elif not isinstance(i, int) or i:
                    reduce(i - 1, RING - 1)
            one_hot(nc, m, 0, 0).then_inc(s("one_hot"), 1)
            groups(dve, body)
            reduce(G // RING - 1, RING - 1)

        @block.scalar
        def _(act):
            def turn(g, half):
                act.wait_ge(s("turned"), g + 1)
                need(act, s("projected"), g - 1)
                nc.scalar.copy(m.ohT[:, half, :], m.psT[:, half, :]).then_inc(s("ohT"), 1)

            def body(i, u):
                g = i * RING + u
                turn(g + 1, (u + 1) % 2)
            turn(0, 0)
            groups(act, body)

        @block.tensor
        def _(pe):
            def turn(g, half):
                pe.wait_ge(s("one_hot"), g + 1)
                need(pe, s("ohT"), g - 1)
                for k in range(K):
                    ins = nc.tensor.transpose(m.psT[:, half, k * P:(k + 1) * P], m.oh[:, half, k, :], m.ident[:, :])
                ins.then_inc(s("turned"), 1)

            def body(i, u):
                g = i * RING + u
                turn(g + 1, (u + 1) % 2)
                blk = pe.value_load(m.blk_i[0:1, bass.ds(g, 1)], min_val=0, max_val=NB - 1)
                pe.wait_ge(s("ohT"), g + 1)
                need(pe, s("summed"), g - 1)
                rows = m.R[:, bass.ds(blk, 1), 0:cols].rearrange("p a c -> p (a c)")
                for k in range(K):
                    ins = nc.tensor.matmul(m.psA[:, u % 2, k * cols:(k + 1) * cols], m.ohT[:, u % 2, k * P:(k + 1) * P],
                                           rows, start=True, stop=True)
                ins.then_inc(s("projected"), 1)
            turn(0, 0)
            groups(pe, body)

        @block.sync
        def _(sp):
            lview = m.logit_d[name].rearrange("(g p k) h -> g p (k h)", p=P, k=K)
            xview = m.xs_d[name].rearrange("(g p k) d -> g p k d", p=P, k=K)

            def store(i, u):
                g = i * RING + u
                sp.wait_ge(s("logits"), g + 1)
                sp.dma_start(lview[bass.ds(g, 1)].rearrange("a p w -> (a p) w"), m.lg[:, u, 0:K * heads]
                             ).then_inc(s(f"lg{u}"), 16)

            def body(i, u):
                g = i * RING + u
                sp.wait_ge(s(f"rows{u}"), 16 * K * (i + 1))
                sp.dma_start(xview[bass.ds(g, 1)].rearrange("a p k d -> (a p) k d"), m.gx[:, u, :, w - D:w]
                             ).then_inc(s(f"xs{u}"), 16)
                if u:
                    store(i, u - 1)
                elif not isinstance(i, int) or i:
                    store(i - 1, RING - 1)
            groups(sp, body)
            store(G // RING - 1, RING - 1)
            for u in range(RING):
                sp.wait_ge(s(f"xs{u}"), 16 * (G // RING))
                sp.wait_ge(s(f"lg{u}"), 16 * (G // RING))


def softmax_parts(nc, m, name, heads):
    wide = RUN * heads
    L, F = m.big[:, 0:wide], m.big[:, wide:2 * wide]
    by_head = [t.rearrange("p (f h) -> p h f", h=heads) for t in (L, F)]
    tail, flag, carry = (m.c8[:, n, 0:heads] for n in range(3))
    tail_r, flag_r, out_r, carry_r = (m.r8[0:heads, n, :] for n in range(4))

    with ExitStack() as ctx:
        s = Stage(nc, f"soft_{name}")
        block = ctx.enter_context(nc.Block())

        @block.sync
        def _(sp):
            sp.dma_start(L, m.logit_d[name].rearrange("(p f) h -> p (f h)", p=P)).then_inc(s("in"), 16)
            outs = 1
            if name in m.max_d and name != "t":
                sp.wait_ge(s("maxima"), 1)
                sp.dma_start(m.max_d[name].rearrange("(p f) h -> p (f h)", p=P), F).then_inc(s("out"), 16)
                outs = 2
            sp.wait_ge(s("exp"), 1)
            sp.dma_start(m.prob_d[name].rearrange("(p f) h -> p (f h)", p=P), L).then_inc(s("out"), 16)
            sp.wait_ge(s("out"), 16 * outs)

        @block.vector
        def _(dve):
            n = [0]

            def step(ins):
                n[0] += 1
                ins.then_inc(s("v"), 1)
                dve.wait_ge(s("v"), n[0])
            dve.wait_ge(s("in"), 16)
            for back in range(2):
                way = slice(None, None, -1) if back else slice(None)
                cuts = m.end_seg if back else m.new_seg
                edge = 0 if back else RUN - 1
                source = by_head[1 if back else 0]
                for h in range(heads):
                    ins = nc.vector.tensor_tensor_scan(by_head[1][:, h, way], cuts[:, way], source[:, h, way],
                                                       -BIG, ALU.add, ALU.max)
                step(ins)
                nc.vector.tensor_copy(tail, by_head[1][:, :, edge])
                step(nc.vector.tensor_reduce(m.c8[:, 3, 0:1], cuts[:, :], AX.X, ALU.min))
                step(nc.vector.tensor_copy(flag, m.c8[:, 3, 0:1].to_broadcast([P, heads])))
                dve.sem_inc(s("tails"), 1)
                dve.wait_ge(s("rows"), back + 1)
                nc.vector.tensor_copy(tail_r, m.psT[0:heads, 0, 0:P])
                step(nc.vector.tensor_copy(flag_r, m.psT[0:heads, 0, P:2 * P]))
                step(nc.vector.tensor_tensor_scan(out_r[:, way], flag_r[:, way], tail_r[:, way], -BIG,
                                                  ALU.add, ALU.max))
                if back:
                    nc.vector.memset(carry_r[:, P - 1:P], -BIG)
                    step(nc.vector.tensor_copy(carry_r[:, 0:P - 1], out_r[:, 1:P]))
                else:
                    nc.vector.memset(carry_r[:, 0:1], -BIG)
                    step(nc.vector.tensor_copy(carry_r[:, 1:P], out_r[:, 0:P - 1]))
                dve.sem_inc(s("carries"), 1)
                dve.wait_ge(s("cols"), back + 1)
                step(nc.vector.tensor_copy(carry, m.psT[:, 1, 0:heads]))
                for h in range(heads):
                    ins = nc.vector.tensor_tensor_scan(by_head[1][:, h, way], cuts[:, way], by_head[1][:, h, way],
                                                       carry[:, h:h + 1], ALU.add, ALU.max)
                step(ins)
            step(nc.vector.tensor_tensor(L, L, F, ALU.subtract))
            dve.sem_inc(s("shifted"), 1)
            if name != "t":
                f3 = F.rearrange("p (f h) -> p f h", h=heads)
                nc.vector.scalar_tensor_tensor(out=f3, in0=m.new_seg[:, :].unsqueeze(2).to_broadcast([P, RUN, heads]),
                                               scalar=-1.0, in1=f3, op0=ALU.is_lt, op1=ALU.mult
                                               ).then_inc(s("maxima"), 1)

        @block.scalar
        def _(act):
            act.wait_ge(s("shifted"), 1)
            nc.scalar.activation(L, L, ACT.Exp).then_inc(s("exp"), 1)

        @block.tensor
        def _(pe):
            for back in range(2):
                pe.wait_ge(s("tails"), back + 1)
                nc.tensor.transpose(m.psT[0:heads, 0, 0:P], tail, m.ident[:, :])
                nc.tensor.transpose(m.psT[0:heads, 0, P:2 * P], flag, m.ident[:, :]).then_inc(s("rows"), 1)
                pe.wait_ge(s("carries"), back + 1)
                nc.tensor.transpose(m.psT[:, 1, 0:heads], carry_r, m.ident[0:heads, 0:heads]).then_inc(s("cols"), 1)


def weighted_sums(nc, m, name, heads, acc_w):
    gat = name != "t"
    cols = heads * D if gat else D
    extras = 3 if gat else 1
    n_loads = 3 if gat else 2

    def rhs(half):
        return m.work[:, half, 0:K * acc_w].rearrange("p (k w) -> p k w", k=K)

    with ExitStack() as ctx:
        s = Stage(nc, f"sum_{name}")
        block = ctx.enter_context(nc.Block())

        @block.sync
        def _(sp):
            xview = m.xs_d[name].rearrange("(g p k) d -> g p (k d)", p=P, k=K)
            pview = m.prob_d[name].rearrange("(g p k) h -> g p (k h)", p=P, k=K)
            mview = m.max_d[name].rearrange("(g p k) h -> g p (k h)", p=P, k=K)

            def body(i, u):
                g = i * RING + u
                need(sp, s("added"), g - RING + 1)
                sp.dma_start(m.xl[:, u, :, :].rearrange("p k d -> p (k d)"),
                             xview[bass.ds(g, 1)].rearrange("a p w -> (a p) w")).then_inc(s(f"in{u}"), 16)
                for n, view in enumerate((pview, mview)[:n_loads - 1]):
                    sp.dma_start(m.pr[:, u, n, 0:K * heads],
                                 view[bass.ds(g, 1)].rearrange("a p w -> (a p) w")).then_inc(s(f"in{u}"), 16)
            groups(sp, body)

        @block.vector
        def _(dve):
            def collect(g, half):
                dve.wait_ge(s("added"), g + 1)
                need(dve, s("acc"), g + 1)
                add_up(nc, m, dve, g, acc_w, m.psC[:, half, 0:acc_w]).then_inc(s("acc"), 1)

            def body(i, u):
                g = i * RING + u
                need(dve, s("added"), g)
                one_hot(nc, m, g + 1, (u + 1) % 2).then_inc(s("one_hot"), 1)
                dve.wait_ge(s(f"in{u}"), 16 * n_loads * (i + 1))
                need(dve, s("added"), g - 1)
                if gat:
                    shape = [P, K, heads, D]
                    p = m.pr[:, u, 0, :].rearrange("p (k h) -> p k h", k=K).unsqueeze(3).to_broadcast(shape)
                    x = m.xl[:, u, :, :].unsqueeze(2).to_broadcast(shape)
                    o = rhs(u % 2)[:, :, 0:cols].rearrange("p k (h c) -> p k h c", h=heads)
                else:
                    shape = [P, K, heads, D // heads]
                    p = m.pr[:, u, 0, 0:K * heads].rearrange("p (k h) -> p k h", k=K).unsqueeze(3).to_broadcast(shape)
                    x = m.xl[:, u, :, :].rearrange("p k (h c) -> p k h c", h=heads)
                    o = rhs(u % 2)[:, :, 0:cols].rearrange("p k (h c) -> p k h c", h=heads)
                nc.vector.tensor_tensor(o, p, x, ALU.mult).then_inc(s("rhs"), 1)
                if u:
                    collect(g - 1, (u - 1) % 2)
                elif not isinstance(i, int) or i:
                    collect(g - 1, 1)
            nc.vector.memset(m.big[:, 0:NB * acc_w], 0.0).then_inc(s("acc"), 1)
            one_hot(nc, m, 0, 0).then_inc(s("one_hot"), 1)
            groups(dve, body)
            collect(G - 1, 1)

        @block.scalar
        def _(act):
            def body(i, u):
                g = i * RING + u
                act.wait_ge(s(f"in{u}"), 16 * n_loads * (i + 1))
                need(act, s("added"), g - 1)
                r = rhs(u % 2)
                for n in range(n_loads - 1):
                    nc.scalar.copy(r[:, :, cols + n * heads:cols + (n + 1) * heads],
                                   m.pr[:, u, n, 0:K * heads].rearrange("p (k h) -> p k h", k=K)
                                   ).then_inc(s("extra"), 1)
                if gat:
                    nc.scalar.copy(r[:, :, cols + 2 * heads:cols + 2 * heads + 1],
                                   m.first_t[:, bass.ds(g, 1), :].rearrange("p a k -> p k a")
                                   ).then_inc(s("extra"), 1)
            groups(act, body)

        @block.tensor
        def _(pe):
            def body(i, u):
                g = i * RING + u
                pe.wait_ge(s("one_hot"), g + 1)
                pe.wait_ge(s("rhs"), g + 1)
                pe.wait_ge(s("extra"), extras * (g + 1))
                need(pe, s("acc"), g)
                for k in range(K):
                    ins = nc.tensor.matmul(m.psC[:, u % 2, 0:acc_w], m.oh[:, u % 2, k, :], rhs(u % 2)[:, k, :],
                                           start=(k == 0), stop=(k == K - 1))
                ins.then_inc(s("added"), 1)
            groups(pe, body)


def transformer_out(nc, m):
    acc = m.big[:, 0:NB * ACC0].rearrange("p (b w) -> p b w", b=NB)
    msg = acc[:, :, 0:D].rearrange("p b (h c) -> p b h c", h=H0)
    den = m.small[:, 0, :, 0:H0]
    steps = [range(b, min(b + 4, NB)) for b in range(0, NB, 4)]
    with ExitStack() as ctx:
        s = Stage(nc, "out_t")
        block = ctx.enter_context(nc.Block())

        @block.vector
        def _(dve):
            nc.vector.tensor_scalar(den, acc[:, :, D:D + H0], 1e-16, None, ALU.max).then_inc(s("den"), 1)
            dve.wait_ge(s("den"), 1)
            nc.vector.reciprocal(den, den).then_inc(s("den"), 1)
            dve.wait_ge(s("den"), 2)
            nc.vector.tensor_tensor(msg, msg, den.unsqueeze(3).to_broadcast([P, NB, H0, D // H0]), ALU.mult
                                    ).then_inc(s("msg"), 1)
            for b in range(NB):
                dve.wait_ge(s("made"), b + 1)
                nc.vector.tensor_copy(m.Y[:, b, :], m.psC[:, b % 2, 0:D]).then_inc(s("y"), 1)

        @block.scalar
        def _(act):
            for n, bs in enumerate(steps):
                act.wait_ge(s("turned"), n + 1)
                nc.scalar.copy(m.XT[0:D, bs[0] * P:(bs[-1] + 1) * P], m.psT[0:D, n % 2, 0:len(bs) * P]
                               ).then_inc(s("copied"), 1)

        @block.tensor
        def _(pe):
            pe.wait_ge(s("msg"), 1)
            for n, bs in enumerate(steps):
                need(pe, s("copied"), n - 1)
                for b in bs:
                    ins = nc.tensor.transpose(m.psT[0:D, n % 2, (b - bs[0]) * P:(b - bs[0] + 1) * P],
                                              acc[:, b, 0:D], m.ident[:, :])
                ins.then_inc(s("turned"), 1)
            pe.wait_ge(s("copied"), len(steps))
            for b in range(NB):
                need(pe, s("y"), b - 1)
                nc.tensor.matmul(m.psC[:, b % 2, 0:D], m.XT[0:D, b * P:(b + 1) * P], m.wo0[:, :], start=True,
                                 stop=True).then_inc(s("made"), 1)


def relation_walk(nc, m):
    name = "r"
    wq = D + NBASE

    def xs(u):
        return m.gx[:, u, :, 0:D]

    def outer(half):
        return m.work[:, half, :].rearrange("p (k w) -> p k w", k=K)

    with ExitStack() as ctx:
        s = Stage(nc, "rel")
        block = ctx.enter_context(nc.Block())

        @block.gpsimd
        def _(pool):
            gather(nc, m, s, pool, m.table_d[name], 2 * D, s("rhs"))

        @block.vector
        def _(dve):
            def one_hots(g, half):
                one_hot(nc, m, g, half).then_inc(s("one_hot"), 1)
                nc.vector.tensor_tensor(
                    m.typ[:, half, :, :], m.iota_row[:, 0:NREL].unsqueeze(1).to_broadcast([P, K, NREL]),
                    m.et_f[:, bass.ds(g, 1), :].rearrange("p a k -> p (a k)").unsqueeze(2).to_broadcast([P, K, NREL]),
                    ALU.is_equal).then_inc(s("one_hot"), 1)

            def collect(g, half):
                dve.wait_ge(s("added"), g + 1)
                need(dve, s("acc"), g + 1)
                add_up(nc, m, dve, g, ACC1, m.psA[:, half, 0:ACC1]).then_inc(s("acc"), 1)

            def body(i, u):
                g = i * RING + u
                half = u % 2
                need(dve, s("added"), g)
                one_hots(g + 1, (u + 1) % 2)
                dve.wait_ge(s(f"rows{u}"), 16 * K * (i + 1))
                dve.wait_ge(s("fetched"), g + 1)
                fetched = m.psC[:, half, 0:K * wq].rearrange("p (k w) -> p k w", k=K)
                dots = m.lx[:, half, :, :]
                nc.vector.tensor_tensor(dots, m.gx[:, u, :, D:2 * D], fetched[:, :, 0:D], ALU.mult
                                        ).then_inc(s("dots"), 1)
                dve.wait_ge(s("dots"), g + 1)
                nc.vector.tensor_reduce(m.a1[:, half, 0, :], dots, AX.X, ALU.add).then_inc(s("score"), 1)
                dve.wait_ge(s("score"), g + 1)
                nc.vector.tensor_scalar(m.a1[:, half, 1, :], m.a1[:, half, 0, :], D ** -0.5, 0.0, ALU.mult, ALU.max
                                        ).then_inc(s("relu"), 1)
                if u:
                    collect(g - 1, (u - 1) % 2)
                elif not isinstance(i, int) or i:
                    collect(g - 1, 1)
                dve.wait_ge(s("tanh"), g + 1)
                nc.vector.tensor_tensor(m.ac[:, half, :, :], fetched[:, :, D:wq],
                                        m.a1[:, half, 2, :].unsqueeze(2).to_broadcast([P, K, NBASE]), ALU.mult
                                        ).then_inc(s("ac"), 1)
                nc.vector.tensor_tensor(m.lx[:, half, :, :], xs(u),
                                        m.last_t[:, bass.ds(g, 1), :].rearrange("p a k -> p (a k)").unsqueeze(2)
                                        .to_broadcast([P, K, D]), ALU.mult).then_inc(s("lastx"), 1)
                dve.wait_ge(s("ac"), g + 1)
                shape = [P, K, NBASE, D]
                nc.vector.tensor_tensor(outer(half).rearrange("p k (b c) -> p k b c", b=NBASE),
                                        m.ac[:, half, :, :].unsqueeze(3).to_broadcast(shape),
                                        xs(u).unsqueeze(2).to_broadcast(shape), ALU.mult).then_inc(s("rhs"), 1)
            nc.vector.memset(m.big[:, 0:NB * ACC1], 0.0).then_inc(s("acc"), 1)
            one_hots(0, 0)
            groups(dve, body)
            collect(G - 1, 1)

        @block.scalar
        def _(act):
            def turn(g, half):
                act.wait_ge(s("turned"), g + 1)
                need(act, s("fetched"), g - 1)
                nc.scalar.copy(m.ohT[:, half, :], m.psT[:, 0, :]).then_inc(s("ohT"), 1)
                nc.scalar.copy(m.typT[:, half, :], m.psT[0:NREL, 1, :]).then_inc(s("ohT"), 1)

            def body(i, u):
                g = i * RING + u
                turn(g + 1, (u + 1) % 2)
                act.wait_ge(s("relu"), g + 1)
                nc.scalar.activation(m.a1[:, u % 2, 2, :], m.a1[:, u % 2, 1, :], ACT.Tanh).then_inc(s("tanh"), 1)
            turn(0, 0)
            groups(act, body)

        @block.tensor
        def _(pe):
            def turn(g, half):
                pe.wait_ge(s("one_hot"), 2 * (g + 1))
                need(pe, s("ohT"), 2 * g)
                for k in range(K):
                    nc.tensor.transpose(m.psT[:, 0, k * P:(k + 1) * P], m.oh[:, half, k, :], m.ident[:, :])
                    ins = nc.tensor.transpose(m.psT[0:NREL, 1, k * P:(k + 1) * P], m.typ[:, half, k, :],
                                              m.ident[:, :])
                ins.then_inc(s("turned"), 1)

            def add(g, half):
                pe.wait_ge(s("rhs"), g + 1)
                pe.wait_ge(s("lastx"), g + 1)
                need(pe, s("acc"), g)
                for k in range(K):
                    nc.tensor.matmul(m.psA[:, half, 0:NBASE * D], m.oh[:, half, k, :], outer(half)[:, k, :],
                                     start=(k == 0), stop=(k == K - 1))
                    ins = nc.tensor.matmul(m.psA[:, half, NBASE * D:ACC1], m.oh[:, half, k, :], m.lx[:, half, k, :],
                                           start=(k == 0), stop=(k == K - 1))
                ins.then_inc(s("added"), 1)

            def body(i, u):
                g = i * RING + u
                half = u % 2
                blk = pe.value_load(m.blk_i[0:1, bass.ds(g, 1)], min_val=0, max_val=NB - 1)
                turn(g + 1, (u + 1) % 2)
                pe.wait_ge(s("ohT"), 2 * (g + 1))
                need(pe, s("ac"), g - 1)
                rows = m.Rr[:, bass.ds(blk, 1), :].rearrange("p a c -> p (a c)")
                for k in range(K):
                    to = m.psC[:, half, k * wq:(k + 1) * wq]
                    nc.tensor.matmul(to, m.ohT[:, half, k * P:(k + 1) * P], rows, start=True, stop=False)
                    ins = nc.tensor.matmul(to, m.typT[:, half, k * P:(k + 1) * P], m.relt[:, :], start=False,
                                           stop=True)
                ins.then_inc(s("fetched"), 1)
                add(g, half)
            turn(0, 0)
            groups(pe, body)


def relational_out(nc, m):
    acc = m.big[:, 0:NB * ACC1].rearrange("p (b w) -> p b w", b=NB)
    nq = NBASE * D // P
    with ExitStack() as ctx:
        s = Stage(nc, "out_r")
        block = ctx.enter_context(nc.Block())

        @block.tensor
        def _(pe):
            def turn(b):
                need(pe, s("copied"), 2 * (b - 1))
                for q in range(nq):
                    nc.tensor.transpose(m.psA[:, b % 2, q * P:(q + 1) * P], acc[:, b, q * P:(q + 1) * P],
                                        m.ident[:, :])
                nc.tensor.transpose(m.psA[0:D, b % 2, 512:512 + P], acc[:, b, NBASE * D:ACC1], m.ident[:, :]
                                    ).then_inc(s("turned"), 1)
            turn(0)
            for b in range(NB):
                if b + 1 < NB:
                    turn(b + 1)
                pe.wait_ge(s("copied"), 2 * (b + 1))
                need(pe, s("y"), b - 1)
                zt = m.work[:, b % 2, :]
                for q in range(nq):
                    nc.tensor.matmul(m.psC[:, b % 2, 0:D], zt[:, q * P:(q + 1) * P], m.w1b[:, q, :], start=(q == 0),
                                     stop=False)
                nc.tensor.matmul(m.psC[:, b % 2, 0:D], zt[0:D, 512:512 + P], m.w1s[:, :], start=False, stop=True
                                 ).then_inc(s("made"), 1)

        @block.scalar
        def _(act):
            for b in range(NB):
                act.wait_ge(s("turned"), b + 1)
                need(act, s("made"), b - 1)
                zt = m.work[:, b % 2, :]
                nc.scalar.copy(zt[:, 0:512], m.psA[:, b % 2, 0:512]).then_inc(s("copied"), 1)
                nc.scalar.copy(zt[0:D, 512:512 + P], m.psA[0:D, b % 2, 512:512 + P]).then_inc(s("copied"), 1)

        @block.vector
        def _(dve):
            for b in range(NB):
                dve.wait_ge(s("made"), b + 1)
                nc.vector.tensor_scalar(m.Y[:, b, :], m.psC[:, b % 2, 0:D], 0.0, None, ALU.max).then_inc(s("y"), 1)


def relational(nc, m):
    transposed(nc, m, "r")

    def side(b, ps):
        return nc.vector.tensor_copy(m.Rr[:, b, 0:D], ps[:, D:2 * D])

    with ExitStack() as ctx:
        block = ctx.enter_context(nc.Block())

        @block.vector
        def _(dve):
            nc.vector.memset(m.Rr[:, :, D:D + NBASE], 0.0)
    tables(nc, m, "r", m.w1[:, :], True, 2 * D, lambda o, ps: nc.scalar.copy(o[:, D:2 * D], ps[:, 0:D]), side)
    relation_walk(nc, m)
    relational_out(nc, m)
    normalised(nc, m, "r", (m.X, m.Y))


def edge_tiles(nc, m, a):
    src_i, low_i, blk_i = (m.big[:, n * TILES:(n + 1) * TILES].bitcast(I32) for n in range(3))
    with ExitStack() as ctx:
        s = Stage(nc, "tiles")
        block = ctx.enter_context(nc.Block())

        @block.sync
        def _(sp):
            for dst, name in ((src_i, "src"), (m.dst_i[:, 0:TILES], "dst"), (m.w_e[:, :], "edge_weight")):
                sp.dma_start(dst, a[name][0:P * TILES].rearrange("(p t) -> p t", p=P)).then_inc(s("in"), 16)
            sp.wait_ge(s("in"), 48)

        @block.vector
        def _(dve):
            nc.vector.memset(m.src_low[:, TILES:TILES + K], -1.0)
            nc.vector.memset(m.dst_i[:, TILES:TILES + K], 0)
            dve.wait_ge(s("in"), 48)
            nc.vector.tensor_scalar(m.dst_i[:, 0:TILES], m.dst_i[:, 0:TILES], N - 1, None, ALU.min)
            nc.vector.tensor_scalar(low_i, src_i, P - 1, None, ALU.bitwise_and).then_inc(s("v"), 1)
            nc.vector.tensor_scalar(blk_i, src_i, P.bit_length() - 1, None, ALU.arith_shift_right
                                    ).then_inc(s("v"), 1)
            dve.wait_ge(s("v"), 2)
            nc.vector.tensor_copy(m.src_low[:, 0:TILES], low_i)
            nc.vector.tensor_copy(m.src_blk[:, :], blk_i)


def smoothing_walk(nc, m, name, source):
    wide = NB * D
    turns = TILES // (K * RING)
    with ExitStack() as ctx:
        s = Stage(nc, f"put_{name}")
        block = ctx.enter_context(nc.Block())

        @block.sync
        def _(sp):
            sp.dma_start(m.table_d[name].rearrange("(b p) d -> p b d", p=P), source[:, :, :]).then_inc(s("out"), 16)
            sp.wait_ge(s("out"), 16)

    def rhs(k):
        return m.big[:, k * wide:(k + 1) * wide]

    with ExitStack() as ctx:
        s = Stage(nc, f"smooth_{name}")
        block = ctx.enter_context(nc.Block())

        @block.gpsimd
        def _(pool):
            gather(nc, m, s, pool, m.table_d[name], D, s("scaled"), index=m.dst_i, tiles=TILES)

        @block.vector
        def _(dve):
            def low_hot(g, half):
                nc.vector.tensor_tensor(
                    m.oh[:, half, :, :], m.iota_row[:, :].unsqueeze(1).to_broadcast([P, K, P]),
                    m.src_low[:, bass.ds(g * K, K)].unsqueeze(2).to_broadcast([P, K, P]),
                    ALU.is_equal).then_inc(s("one_hot"), 1)

            def body(i, u):
                g = i * RING + u
                half = u % 2
                need(dve, s("added"), K * g)
                low_hot(g + 1, (u + 1) % 2)
                need(dve, s("rhs"), K * (g - 1))
                nc.vector.tensor_tensor(
                    m.sblk[:, half, :, :], m.iota_row[:, 0:NB].unsqueeze(1).to_broadcast([P, K, NB]),
                    m.src_blk[:, bass.ds(g * K, K)].unsqueeze(2).to_broadcast([P, K, NB]),
                    ALU.is_equal).then_inc(s("blk_hot"), 1)
                dve.wait_ge(s(f"rows{u}"), 16 * K * (i + 1))
                nc.vector.tensor_tensor(m.lx[:, half, :, :], m.gx[:, u, :, 0:D],
                                        m.w_e[:, bass.ds(g * K, K)].unsqueeze(2).to_broadcast([P, K, D]), ALU.mult
                                        ).then_inc(s("scaled"), 1)
                dve.wait_ge(s("blk_hot"), g + 1)
                dve.wait_ge(s("scaled"), g + 1)
                for k in range(K):
                    need(dve, s("added"), K * (g - 1) + k + 1)
                    nc.vector.tensor_tensor(
                        rhs(k).rearrange("p (b d) -> p b d", b=NB),
                        m.sblk[:, half, k, :].unsqueeze(2).to_broadcast([P, NB, D]),
                        m.lx[:, half, k, :].unsqueeze(1).to_broadcast([P, NB, D]), ALU.mult).then_inc(s("rhs"), 1)
            nc.vector.memset(m.zeros[:, :], 0.0).then_inc(s("zeros"), 1)
            low_hot(0, 0)
            groups(dve, body, turns)
            dve.wait_ge(s("total"), 1)
            nc.vector.tensor_copy(m.Y[:, :, :].rearrange("p b d -> p (b d)")[:, 0:512], m.psA[:, 0, 0:512])
            nc.vector.tensor_copy(m.Y[:, :, :].rearrange("p b d -> p (b d)")[:, 512:wide], m.psA[:, 0, 512:wide])

        @block.tensor
        def _(pe):
            cols = ((0, 512), (512, wide))
            pe.wait_ge(s("zeros"), 1)
            for lo, hi in cols:
                nc.tensor.matmul(m.psA[:, 0, lo:hi], m.zeros[:, 0:P], m.zeros[:, 0:hi - lo], start=True, stop=False)

            def body(i, u):
                g = i * RING + u
                pe.wait_ge(s("one_hot"), g + 1)
                for k in range(K):
                    pe.wait_ge(s("rhs"), K * g + k + 1)
                    for lo, hi in cols:
                        ins = nc.tensor.matmul(m.psA[:, 0, lo:hi], m.oh[:, u % 2, k, :], rhs(k)[:, lo:hi],
                                               start=False, stop=False)
                    ins.then_inc(s("added"), 1)
            groups(pe, body, turns)
            for lo, hi in cols:
                ins = nc.tensor.matmul(m.psA[:, 0, lo:hi], m.zeros[:, 0:P], m.zeros[:, 0:hi - lo], start=False,
                                       stop=True)
            ins.then_inc(s("total"), 1)


def smoothing(nc, m, a):
    edge_tiles(nc, m, a)
    smoothing_walk(nc, m, "s0", m.X)
    smoothing_walk(nc, m, "s1", m.Y)
    smoothing_walk(nc, m, "s2", m.Y)
    normalised(nc, m, "s", (m.X, m.Y))


def self_logits(nc, m, l):
    xl = m.big[:, 0:NB * TAB3].rearrange("p (b w) -> p b w", b=NB)
    steps = [range(b, min(b + 4, NB)) for b in range(0, NB, 4)]
    with ExitStack() as ctx:
        s = Stage(nc, f"self{l}")
        block = ctx.enter_context(nc.Block())

        def part(n):
            return m.work[:, n % 2, 0:len(steps[n]) * W3].rearrange("p (b w) -> p b w", w=W3)

        @block.vector
        def _(dve):
            def reduce(n):
                bs = steps[n]
                dve.wait_ge(s("summed"), n + 1)
                nc.vector.scalar_tensor_tensor(out=part(n), in0=part(n), scalar=0.2, in1=part(n), op0=ALU.mult,
                                               op1=ALU.max).then_inc(s("leaky"), 1)
                dve.wait_ge(s("leaky"), n + 1)
                nc.vector.tensor_tensor(part(n), part(n), m.att3[:, l, :].unsqueeze(1)
                                        .to_broadcast([P, len(bs), W3]), ALU.mult).then_inc(s("weighted"), 1)
                dve.wait_ge(s("weighted"), n + 1)
                nc.vector.tensor_reduce(m.self3[:, bs[0]:bs[-1] + 1, :].rearrange("p b h -> p (b h)"),
                                        part(n).rearrange("p b (h c) -> p (b h) c", c=D), AX.X, ALU.add
                                        ).then_inc(s("logits"), 1)
            for n, bs in enumerate(steps):
                need(dve, s("logits"), n - 1)
                nc.vector.tensor_tensor(part(n), xl[:, bs[0]:bs[-1] + 1, 0:W3], m.R[:, bs[0]:bs[-1] + 1, :], ALU.add
                                        ).then_inc(s("summed"), 1)
                if n:
                    reduce(n - 1)
            reduce(len(steps) - 1)


def attention_out(nc, m, l):
    acc = m.big[:, 0:NB * ACC3].rearrange("p (b w) -> p b w", b=NB)
    sums = acc[:, :, 0:W3].rearrange("p b (h c) -> p b h c", h=H3)
    own = m.big[:, NB * ACC3:NB * (ACC3 + W3)].rearrange("p (b h c) -> p b h c", b=NB, h=H3)
    den, top, flag = acc[:, :, W3:W3 + H3], acc[:, :, W3 + H3:W3 + 2 * H3], acc[:, :, ACC3 - 1:ACC3]
    most, e_self, e_edge, total, none = (m.small[:, n, :, :] for n in range(5))
    wide = [P, NB, H3, D]
    with ExitStack() as ctx:
        s = Stage(nc, f"out_g{l}")
        block = ctx.enter_context(nc.Block())

        @block.vector
        def _(dve):
            n = [0]

            def step(ins):
                n[0] += 1
                ins.then_inc(s("v"), 1)
                dve.wait_ge(s("v"), n[0])
            step(nc.vector.tensor_scalar(none, flag.to_broadcast([P, NB, H3]), -1.0, BIG, ALU.add, ALU.mult))
            step(nc.vector.tensor_tensor(top, top, none, ALU.add))
            step(nc.vector.tensor_tensor(most, top, m.self3[:, :, :], ALU.max))
            step(nc.vector.tensor_tensor(e_self, m.self3[:, :, :], most, ALU.subtract))
            step(nc.vector.tensor_tensor(e_edge, top, most, ALU.subtract))
            dve.sem_inc(s("shifted"), 1)
            dve.wait_ge(s("exp"), 2)
            step(nc.vector.tensor_tensor(total, den, e_edge, ALU.mult))
            step(nc.vector.tensor_tensor(total, total, e_self, ALU.add))
            step(nc.vector.tensor_scalar(total, total, 1e-16, None, ALU.add))
            step(nc.vector.reciprocal(total, total))
            nc.vector.tensor_tensor(e_self, e_self, total, ALU.mult)
            step(nc.vector.tensor_tensor(e_edge, e_edge, total, ALU.mult))
            step(nc.vector.tensor_tensor(sums, sums, e_edge.unsqueeze(3).to_broadcast(wide), ALU.mult))
            step(nc.vector.tensor_tensor(own, m.X[:, :, :].unsqueeze(2).to_broadcast(wide),
                                         e_self.unsqueeze(3).to_broadcast(wide), ALU.mult))
            step(nc.vector.tensor_tensor(sums, sums, own, ALU.add))
            dve.sem_inc(s("sums"), 1)
            for b in range(NB):
                dve.wait_ge(s("made"), b + 1)
                nc.vector.tensor_copy(m.Z[:, b, :], m.psC[:, b % 2, 0:D]).then_inc(s("z"), 1)

        @block.scalar
        def _(act):
            act.wait_ge(s("shifted"), 1)
            nc.scalar.activation(e_self, e_self, ACT.Exp).then_inc(s("exp"), 1)
            nc.scalar.activation(e_edge, e_edge, ACT.Exp).then_inc(s("exp"), 1)
            for b in range(NB):
                act.wait_ge(s("turned"), b + 1)
                need(act, s("made"), b - 1)
                nc.scalar.copy(m.work[:, b % 2, 0:W3], m.psT[:, b % 2, 0:W3]).then_inc(s("copied"), 1)

        @block.tensor
        def _(pe):
            def turn(b):
                need(pe, s("copied"), b - 1)
                nc.tensor.transpose(m.psT[:, b % 2, 0:P], acc[:, b, 0:P], m.ident[:, :])
                nc.tensor.transpose(m.psT[:, b % 2, P:2 * P], acc[:, b, P:2 * P], m.ident[:, :]
                                    ).then_inc(s("turned"), 1)
            pe.wait_ge(s("sums"), 1)
            turn(0)
            for b in range(NB):
                if b + 1 < NB:
                    turn(b + 1)
                pe.wait_ge(s("copied"), b + 1)
                need(pe, s("z"), b - 1)
                to = m.psC[:, b % 2, 0:D]
                for q in range(2):
                    nc.tensor.matmul(to, m.work[:, b % 2, q * P:(q + 1) * P], m.w3o[:, l, q, :], start=(q == 0),
                                     stop=False)
                nc.tensor.matmul(to, m.ones[0:1, :], m.brow[:, l, W3:W3 + D], start=False, stop=True
                                 ).then_inc(s("made"), 1)


def batch_normalised(nc, m, l, tag, leaky):
    mean, var, scale = (m.bnv[:, n, :] for n in range(3))
    wide = [P, NB, D]
    with ExitStack() as ctx:
        s = Stage(nc, f"bn{tag}")
        block = ctx.enter_context(nc.Block())

        def over_nodes(t):
            return t.unsqueeze(1).to_broadcast(wide)

        @block.vector
        def _(dve):
            n = [0]

            def step(ins):
                n[0] += 1
                ins.then_inc(s("v"), 1)
                dve.wait_ge(s("v"), n[0])
            if leaky:
                step(nc.vector.scalar_tensor_tensor(out=m.Z[:, :, :], in0=m.Z[:, :, :], scalar=0.01,
                                                    in1=m.Z[:, :, :], op0=ALU.mult, op1=ALU.max))
            step(nc.vector.tensor_tensor(m.X[:, :, :], m.Z[:, :, :], m.X[:, :, :], ALU.add))
            dve.sem_inc(s("ready"), 1)
            dve.wait_ge(s("sums"), 1)
            step(nc.vector.tensor_scalar(mean, m.psC[:, 0, 0:D], 1.0 / N, None, ALU.mult))
            step(nc.vector.tensor_tensor(m.X[:, :, :], m.X[:, :, :], over_nodes(mean), ALU.subtract))
            step(nc.vector.tensor_tensor(m.Z[:, :, :], m.X[:, :, :], m.X[:, :, :], ALU.mult))
            dve.sem_inc(s("ready"), 1)
            dve.wait_ge(s("root"), 1)
            step(nc.vector.reciprocal(scale, var))
            step(nc.vector.tensor_tensor(scale, scale, m.bn[:, l, 0, :], ALU.mult))
            step(nc.vector.tensor_tensor(m.X[:, :, :], m.X[:, :, :], over_nodes(scale), ALU.mult))
            nc.vector.tensor_tensor(m.X[:, :, :], m.X[:, :, :], over_nodes(m.bn[:, l, 1, :]), ALU.add)

        @block.tensor
        def _(pe):
            for n, t in enumerate((m.X, m.Z)):
                pe.wait_ge(s("ready"), n + 1)
                for b in range(NB):
                    rows = P if b < NB - 1 else TAIL
                    ins = nc.tensor.matmul(m.psC[:, n, 0:D], m.ones[0:rows, :], t[0:rows, b, :], start=(b == 0),
                                           stop=(b == NB - 1))
                ins.then_inc(s("sums"), 1)

        @block.scalar
        def _(act):
            act.wait_ge(s("sums"), 2)
            nc.scalar.activation(var, m.psC[:, 1, 0:D], ACT.Sqrt, bias=m.eps[:, 0:1], scale=1.0 / N
                                 ).then_inc(s("root"), 1)


def attention(nc, m):
    with ExitStack() as ctx:
        block = ctx.enter_context(nc.Block())

        @block.vector
        def _(dve):
            nc.vector.tensor_copy(m.Y[:, :, :], m.X[:, :, :])
    for l in range(3):
        name = f"g{l}"
        with nc.cleanup_on_exit():
            transposed(nc, m, name)
            tables(nc, m, name, m.w3[:, l, :], True, 2 * W3,
                   lambda o, ps: nc.scalar.copy(o[:, 0:W3], ps[:, 0:W3]),
                   lambda b, ps: nc.vector.tensor_copy(m.R[:, b, :], ps[:, W3:2 * W3]))
            self_logits(nc, m, l)
            logits(nc, m, name, H3, W3, l)
            softmax_parts(nc, m, name, H3)
            weighted_sums(nc, m, name, H3, ACC3)
            attention_out(nc, m, l)
            batch_normalised(nc, m, l, name, l < 2)
    normalised(nc, m, "g", (m.X, m.Y))


def transformer(nc, m):
    transposed(nc, m, "t")
    tables(nc, m, "t", m.w0[:, :], False, 3 * D,
           lambda o, ps: nc.scalar.copy(o, ps[:, 0:2 * D]),
           lambda b, ps: nc.vector.tensor_scalar(m.R[:, b, 0:D], ps[:, 2 * D:3 * D], (D // H0) ** -0.5, None,
                                                 ALU.mult))
    logits(nc, m, "t", H0, D, None)
    softmax_parts(nc, m, "t", H0)
    weighted_sums(nc, m, "t", H0, ACC0)
    transformer_out(nc, m)
    normalised(nc, m, "t", (m.X, m.X, m.Y))


def program(nc, a, out):
    with ExitStack() as ctx:
        m = allocate(nc, ctx)
        with nc.cleanup_on_exit():
            constants(nc, m, a)
            cut(nc, m, a)
        with nc.cleanup_on_exit():
            transformer(nc, m)
        with nc.cleanup_on_exit():
            relational(nc, m)
        with nc.cleanup_on_exit():
            smoothing(nc, m, a)
        attention(nc, m)
        store(nc, m, out)


def store(nc, m, out):
    with ExitStack() as ctx:
        s = Stage(nc, "store")
        block = ctx.enter_context(nc.Block())

        @block.sync
        def _(sp):
            sp.dma_start(out[0:(NB - 1) * P, :].rearrange("(b p) d -> p b d", p=P), m.X[:, 0:NB - 1, :]
                         ).then_inc(s("out"), 16)
            sp.dma_start(out[(NB - 1) * P:N, :], m.X[0:TAIL, NB - 1, :]).then_inc(s("out"), 16)
            sp.wait_ge(s("out"), 32)



_INS = ["x", "src", "dst", "edge_type_86", "edge_weight", "L0_gnn_Wq", "L0_gnn_Wk", "L0_gnn_Wv", "L0_gnn_Wo",
        "L1_gnn_weight", "L1_gnn_w_comp", "L1_gnn_self_loop_weight", "L1_gnn_A1_w", "L1_gnn_A1_b", "L1_gnn_A2_w",
        "L1_gnn_A2_b", "L1_gnn_rel_emb", "L3_gnn_Wl", "L3_gnn_bl", "L3_gnn_Wr", "L3_gnn_br", "L3_gnn_att",
        "L3_gnn_conv_bias", "L3_gnn_bn_gamma", "L3_gnn_bn_beta"]
_PAD = {"src": 0, "dst": 1 << 20, "edge_type_86": 0, "edge_weight": 0}


def kernel(**inputs):
    import numpy as _np
    import concourse.bacc as _bacc
    from concourse import mybir as _mybir
    from concourse.bass_utils import run_bass_kernel_spmd as _run

    nc = _bacc.Bacc("TRN2", target_bir_lowering=False, num_devices=1)
    arrays, args = {}, {}
    for name in _INS:
        x = _np.ascontiguousarray(inputs[name])
        if name in _PAD:
            x = _np.concatenate([x, _np.full(GE, _PAD[name], x.dtype)])
        arrays[f"in_{name}_dram"] = x
        args[name] = nc.dram_tensor(f"in_{name}_dram", x.shape, _mybir.dt.from_np(x.dtype), kind="ExternalInput").ap()
    out = nc.dram_tensor("out_0_dram", (N, D), F32, kind="ExternalOutput").ap()
    program(nc, args, out)
    r = _run(nc, [arrays], core_ids=[0])
    return r.results[0]["out_0_dram"]
```

```python
from contextlib import ExitStack

import concourse.bass as bass
from concourse import mybir

F32 = mybir.dt.float32
BF16 = mybir.dt.bfloat16
I32 = mybir.dt.int32
U32 = mybir.dt.uint32
ALU = mybir.AluOpType
ACT = mybir.ActivationFunctionType
AX = mybir.AxisListType

P = 128
D = 32
N, E = 3125, 100000
K = 4
GE = K * P
NB = -(-N // P)
NP = NB * P
TAIL = N - (NB - 1) * P
RING = 4
G = -(-((E + NB * (GE - 1)) // GE) // RING) * RING
SL = G * GE
RUN = SL // P
EP = 125
EF = E // EP
NREL, NBASE = 86, 16
TILES = -(-E // (P * K * RING)) * K * RING
H0 = 4
H3 = 8
W3 = H3 * D
TAB3 = W3 + D + H3
ROW3 = W3 + H3
LEAK = 0.2
PE_ADDS = 1
ACC0 = D + H0
ACC1 = NBASE * D + D
ACC3 = W3 + 2 * H3 + 1
BIG = 1e30
LN_EPS = 1e-5
assert EP * EF == E and RUN * P == SL and EF == RUN - 80


class Stage:

    def __init__(self, nc, tag):
        self.nc, self.tag, self.made = nc, tag, {}

    def __call__(self, name):
        if name not in self.made:
            self.made[name] = self.nc.alloc_semaphore(name=f"{self.tag}_{name}")
        return self.made[name]


def need(eng, sem, value):
    if not isinstance(value, int) or value > 0:
        eng.wait_ge(sem, value)


def groups(eng, body, turns=G // RING):
    for i in range(2):
        for u in range(RING):
            body(i, u)
    with eng.Fori(2, turns, 1) as i:
        for u in range(RING):
            body(i, u)


class Mem:
    pass


def allocate(nc, ctx):
    m = Mem()

    def sb(name, shape, dt=F32):
        t = ctx.enter_context(nc.sbuf_tensor(name, shape, dt))
        return t

    m.ident = sb("ident", [P, P])
    m.ident_b = sb("ident_b", [P, P], BF16)
    m.iota_b = sb("iota_b", [P, P], BF16)
    m.iota_row = sb("iota_row", [P, P])
    m.ones = sb("ones", [P, P])
    m.upper = sb("upper", [NB, NB])
    m.src_i = sb("src_i", [P, G + 1, K], I32)
    m.rel = sb("rel", [P, G + 3, K])
    m.et_f = sb("et_f", [P, G + 2, K])
    m.first_t = sb("first_t", [P, G, K])
    m.last_t = sb("last_t", [P, G, K])
    m.new_seg = sb("new_seg", [P, RUN])
    m.end_seg = sb("end_seg", [P, RUN])
    m.blk_i = sb("blk_i", [1, G + 1], I32)
    m.X = sb("X", [P, NB, D])
    m.Y = sb("Y", [P, NB, D])
    m.Z = sb("Z", [P, NB, D])
    m.XT = sb("XT", [D + 1, NP])
    rows = sb("rows", [P, max(NB * ROW3, G * K * H3)])
    m.probs = rows[:, 0:G * K * H3]
    m.R = rows[:, 0:NB * ROW3].rearrange("p (b w) -> p b w", b=NB)
    wr = D + NBASE
    m.Rr = rows[:, 0:NB * wr].rearrange("p (b w) -> p b w", b=NB)
    at = NB * wr
    m.typ = rows[:, at:at + RING * K * NREL].rearrange("p (n k r) -> p n k r", n=RING, k=K)
    at += RING * K * NREL
    m.typT = rows[0:NREL, at:at + 2 * K * P].rearrange("p (n w) -> p n w", n=2)
    m.big = sb("big", [P, 2 * RUN * H3])
    at = K * NB * D
    m.maxima = m.big[:, NB * ACC3:NB * ACC3 + G * K * H3]
    m.w_e = m.big[:, at:at + TILES]
    at += TILES
    m.dst_i = m.big[:, at:at + TILES + K].bitcast(I32)
    at += TILES + K
    m.src_low = m.big[:, at:at + TILES + K]
    at += TILES + K
    m.src_blk = m.big[:, at:at + TILES]
    m.gx = sb("gx", [P, RING, K, TAB3])
    m.gi = sb("gi", [P, RING, K], I32)
    one_hots = sb("oh", [P, RING * K * P])
    m.oh = one_hots[:, :].rearrange("p (n k q) -> p n k q", n=RING, k=K)
    m.oh_b = one_hots[:, 0:RING * K * P // 2].bitcast(BF16).rearrange("p (n k q) -> p n k q", n=RING, k=K)
    m.ohT = sb("ohT", [P, 2, K * P])
    m.work = sb("work", [P, 2, K * NBASE * D])
    m.red = sb("red", [P, 2, K * H3])
    m.lin = sb("lin", [P, 2, K * H3])
    m.lg = sb("lg", [P, RING, K * H3])
    m.xl = sb("xl", [P, RING, K, D])
    m.a1 = sb("a1", [P, 2, 4, K])
    m.sblk = m.work[:, 0, 0:2 * K * NB].rearrange("p (n k b) -> p n k b", n=2, k=K)
    m.zeros = m.work[:, 1, 0:512]
    m.ac = sb("ac", [P, 2, K, NBASE])
    m.lx = sb("lx", [P, 2, K, D])
    m.self3 = sb("self3", [P, NB, H3])
    m.small = sb("small", [P, 5, NB, H3])
    m.line = sb("line", [P, 4, NB])
    m.c8 = sb("c8", [P, 6, H3])
    m.r8 = sb("r8", [H3, 4, P])
    m.bnv = sb("bnv", [P, 4, D])
    m.w3 = sb("w3", [D + 1, 3, 2 * W3])
    m.w3l = sb("w3l", [D + 1, 3, 2 * H3])
    m.w3o = sb("w3o", [P, 3, 2, D])
    m.att3 = sb("att3", [P, 3, W3])
    m.bn = sb("bn", [P, 3, 2, D])
    m.brow = sb("brow", [1, 3, W3 + 2 * D])
    m.w0 = sb("w0", [D, 3 * D])
    m.wo0 = sb("wo0", [D, D])
    m.w1 = sb("w1", [D + 1, 2 * D])
    m.w1b = sb("w1b", [P, 4, D])
    m.w1s = sb("w1s", [D, D])
    m.relt = sb("relt", [NREL, D + NBASE])
    m.col = sb("col", [P, 8])
    m.coli = sb("coli", [P, 1], I32)
    m.eps = sb("eps", [P, 1])
    m.guard = sb("guard", [1, 1])
    m.psA = ctx.enter_context(nc.psum_tensor("psA", [P, 2, 1024], F32))
    m.psT = ctx.enter_context(nc.psum_tensor("psT", [P, 2, 512], F32))
    m.psC = ctx.enter_context(nc.psum_tensor("psC", [P, 2, 512], F32))

    def dram(name, shape):
        return nc.dram_tensor(name, shape, F32, kind="Internal").ap()

    m.key_d = dram("key_d", [SL + 2])
    m.first_d = dram("first_d", [SL])
    m.last_d = dram("last_d", [SL])
    m.table_d = {n: dram(f"table_{n}", [NP, w]) for n, w in
                 (("t", 2 * D), ("r", 2 * D), ("s0", D), ("s1", D), ("s2", D), ("g0", TAB3), ("g1", TAB3), ("g2", TAB3))}
    soft = (("t", H0), ("g0", H3), ("g1", H3), ("g2", H3))
    m.xs_d = {n: dram(f"xs_{n}", [SL, D]) for n, _ in soft}
    m.logit_d = {n: dram(f"logit_{n}", [SL, h]) for n, h in soft}
    m.prob_d = {n: dram(f"prob_{n}", [SL, h]) for n, h in soft}
    m.max_d = {n: dram(f"max_{n}", [SL, h]) for n, h in soft}
    return m



def constants(nc, m, a):
    with ExitStack() as ctx:
        s = Stage(nc, "const")
        block = ctx.enter_context(nc.Block())
        LOADS = []
        bias = D
        LOADS.append((m.X[:, 0:NB - 1, :], a["x"][0:(NB - 1) * P, :].rearrange("(b p) d -> p b d", p=P)))
        LOADS.append((m.X[0:TAIL, NB - 1, :], a["x"][(NB - 1) * P:N, :]))
        for n, w in enumerate(("L0_gnn_Wk", "L0_gnn_Wv", "L0_gnn_Wq")):
            LOADS.append((m.w0[:, n * D:(n + 1) * D], a[w]))
        LOADS.append((m.wo0[:, :], a["L0_gnn_Wo"]))
        for n, (w, b) in enumerate((("L1_gnn_A1_w", "L1_gnn_A1_b"), ("L1_gnn_A2_w", "L1_gnn_A2_b"))):
            LOADS.append((m.w1[0:D, n * D:(n + 1) * D], a[w].rearrange("o i -> i o")))
            LOADS.append((m.w1[bias:bias + 1, n * D:(n + 1) * D], a[b].rearrange("(a o) -> a o", a=1)))
        LOADS.append((m.w1b[:, :, :], a["L1_gnn_weight"].rearrange("(t q) i o -> (q i) t o", q=4)))
        LOADS.append((m.w1s[:, :], a["L1_gnn_self_loop_weight"]))
        LOADS.append((m.relt[:, 0:D], a["L1_gnn_rel_emb"]))
        LOADS.append((m.relt[:, D:D + NBASE], a["L1_gnn_w_comp"]))
        for l in range(3):
            for n, (w, b) in enumerate((("L3_gnn_Wl", "L3_gnn_bl"), ("L3_gnn_Wr", "L3_gnn_br"))):
                LOADS.append((m.w3[0:D, l, n * W3:(n + 1) * W3], a[w][l]))
                LOADS.append((m.w3[bias:bias + 1, l, n * W3:(n + 1) * W3], a[b][l:l + 1]))
            for h in range(H3):
                LOADS.append((m.w3o[(h % 4) * D:(h % 4 + 1) * D, l, h // 4, :],
                              a["L3_gnn_Wl"][l, :, h * D:(h + 1) * D]))
            LOADS.append((m.att3[:, l, :], a["L3_gnn_att"][l].rearrange("(a h) c -> a (h c)", a=1).to_broadcast([P, W3])))
            for n, w in enumerate(("L3_gnn_bn_gamma", "L3_gnn_bn_beta")):
                LOADS.append((m.bn[:, l, n, :], a[w][l:l + 1].to_broadcast([P, D])))
            LOADS.append((m.brow[:, l, 0:W3], a["L3_gnn_bl"][l:l + 1]))
            LOADS.append((m.brow[:, l, W3:W3 + D], a["L3_gnn_conv_bias"][l:l + 1]))

        @block.vector
        def _(dve):
            nc.vector.memset(m.X[:, NB - 1, :], 0.0).then_inc(s("xzero"), 1)
            nc.vector.memset(m.ones[:, :], 1.0).then_inc(s("ones"), 1)
            nc.vector.memset(m.XT[D:D + 1, :], 1.0)
            nc.vector.memset(m.rel[:, G:G + 3, :], -1.0)
            nc.vector.memset(m.et_f[:, G:G + 2, :], -1.0)
            nc.vector.memset(m.eps[:, :], LN_EPS)
            nc.vector.memset(m.guard[:, :], -5.0)
            dve.wait_ge(s("loads"), 16 * len(LOADS))
            weighted = m.big[0:D + 1, 0:3 * 2 * W3].rearrange("p (l n w) -> p l n w", l=3, n=2)
            nc.vector.tensor_tensor(weighted, m.w3[:, :, :].rearrange("p l (n w) -> p l n w", n=2),
                                    m.att3[0:D + 1, :, :].unsqueeze(2).to_broadcast([D + 1, 3, 2, W3]), ALU.mult
                                    ).then_inc(s("weighted"), 1)
            dve.wait_ge(s("weighted"), 1)
            for n in range(2):
                nc.vector.tensor_reduce(m.w3l[:, :, (1 - n) * H3:(2 - n) * H3],
                                        weighted[:, :, n, :].rearrange("p l (h c) -> p l h c", h=H3), AX.X, ALU.add
                                        ).then_inc(s("weighted"), 1)
            dve.wait_ge(s("weighted"), 3)
            nc.vector.tensor_scalar(m.w3l[:, :, :], m.w3l[:, :, :], LEAK, None, ALU.mult)
            nc.vector.tensor_scalar(m.w3o[:, :, :, :], m.w3o[:, :, :, :], 1.0 / H3, None, ALU.mult)
            nc.vector.tensor_reduce(m.brow[:, :, W3 + D:W3 + 2 * D],
                                    m.brow[:, :, 0:W3].rearrange("p l (h c) -> p l c h", h=H3), AX.X, ALU.add
                                    ).then_inc(s("brow"), 1)
            dve.wait_ge(s("brow"), 1)
            nc.vector.tensor_scalar(m.brow[:, :, 0:D], m.brow[:, :, W3 + D:W3 + 2 * D], 1.0 / H3, None,
                                    ALU.mult).then_inc(s("brow"), 1)
            dve.wait_ge(s("brow"), 2)
            nc.vector.tensor_tensor(m.brow[:, :, W3:W3 + D], m.brow[:, :, W3:W3 + D], m.brow[:, :, 0:D], ALU.add)

        @block.gpsimd
        def _(pool):
            pool.wait_ge(s("ones"), 1)
            nc.gpsimd.affine_select(out=m.ident[:, :], in_=m.ones[:, :], compare_op=ALU.is_equal, fill=0.0,
                                    base=0, pattern=[[-1, P]], channel_multiplier=1).then_inc(s("ident"), 1)
            nc.gpsimd.affine_select(out=m.upper[:, :], in_=m.ones[0:NB, 0:NB], compare_op=ALU.is_gt, fill=0.0,
                                    base=0, pattern=[[1, NB]], channel_multiplier=-1)
            nc.gpsimd.iota(m.iota_row[:, :], [[1, P]], base=0, channel_multiplier=0,
                           allow_small_or_imprecise_dtypes=True).then_inc(s("iota"), 1)
            pool.wait_ge(s("ident"), 1)
            pool.wait_ge(s("iota"), 1)
            nc.gpsimd.tensor_copy(m.iota_b[:, :], m.iota_row[:, :])
            nc.gpsimd.tensor_copy(m.ident_b[:, :], m.ident[:, :])
            nc.gpsimd.memset(m.src_i[:, G, :], 0)
            nc.gpsimd.memset(m.blk_i[:, G:G + 1], 0)

        @block.sync
        def _(sp):
            sp.wait_ge(s("xzero"), 1)
            for n, (dst, src) in enumerate(LOADS):
                sp.dma_start(dst, src, allow_slow_non_contiguous=True).then_inc(s("loads"), 16)
            sp.wait_ge(s("loads"), 16 * len(LOADS))


def cut(nc, m, a):
    b = m.big
    dst_i = b[0:EP, 0:EF].bitcast(I32)
    dst_f = b[0:EP, EF:2 * EF]
    below = b[0:EP, 2 * EF:3 * EF]
    counts = b[0:EP, 3 * EF:3 * EF + NB + 1]
    at = 3 * EF + 32
    g_no, mask, val = (b[0:NB, at + n * G:at + (n + 1) * G] for n in range(3))
    at += 3 * G
    blk128 = b[:, at:at + G]
    row1 = b[0:1, at + G:at + 2 * G]
    row2 = b[0:1, at + 2 * G:at + 3 * G]
    start_i = b[0:1, at + 3 * G:at + 4 * G].bitcast(I32)
    at += 4 * G

    def slots(n):
        return b[:, at + n * G * K:at + (n + 1) * G * K].rearrange("p (g k) -> p g k", k=K)
    slot_dst, slot_et, slot_f, valid = slots(0).bitcast(I32), slots(1).bitcast(I32), slots(2), slots(3)
    col = m.col
    first, nxt, t1, ng, g0, g1, off, num = (col[0:NB, n:n + 1] for n in range(8))
    bcol = b[0:NB, at + 4 * G * K:at + 4 * G * K + P]

    with ExitStack() as ctx:
        s = Stage(nc, "cut")
        block = ctx.enter_context(nc.Block())

        @block.vector
        def _(dve):
            n = [0]

            def step(ins):
                n[0] += 1
                ins.then_inc(s("v"), 1)
                dve.wait_ge(s("v"), n[0])
            dve.wait_ge(s("dst"), 16)
            step(nc.vector.tensor_copy(dst_f, dst_i))
            for j in range(NB + 1):
                step(nc.vector.tensor_scalar(below, dst_f, float(j * P), None, ALU.is_lt))
                step(nc.vector.tensor_reduce(counts[:, j:j + 1], below, AX.X, ALU.add))
            dve.sem_inc(s("counts"), 1)
            dve.wait_ge(s("sums"), 1)
            nc.vector.tensor_copy(first, m.psC[0:NB, 0, 0:1])
            step(nc.vector.tensor_copy(nxt, m.psC[0:NB, 0, 1:2]))
            step(nc.vector.tensor_tensor(t1, nxt, first, ALU.subtract))
            step(nc.vector.tensor_scalar(t1, t1, float(GE - 1), None, ALU.add))
            step(nc.vector.tensor_copy(m.coli[0:NB, :], t1))
            step(nc.vector.tensor_scalar(m.coli[0:NB, :], m.coli[0:NB, :], GE.bit_length() - 1, None,
                                         ALU.arith_shift_right))
            step(nc.vector.tensor_copy(ng, m.coli[0:NB, :]))
            dve.sem_inc(s("ng"), 1)
            dve.wait_ge(s("sums"), 2)
            step(nc.vector.tensor_copy(g0, m.psC[0:NB, 0, 2:3]))
            step(nc.vector.tensor_tensor(g1, g0, ng, ALU.add))
            step(nc.vector.tensor_scalar(off, g0, float(-GE), None, ALU.mult))
            step(nc.vector.tensor_tensor(off, off, first, ALU.add))
            dve.wait_ge(s("iota"), 1)
            step(nc.vector.tensor_scalar(mask, g_no, g1, None, ALU.is_lt))
            step(nc.vector.tensor_scalar(val, g_no, g0, None, ALU.is_ge))
            step(nc.vector.tensor_tensor(mask, mask, val, ALU.mult))
            step(nc.vector.tensor_scalar(val, g_no, float(GE), off, ALU.mult, ALU.add))
            step(nc.vector.tensor_tensor(val, val, mask, ALU.mult))
            step(nc.vector.tensor_scalar(bcol, m.ones[0:NB, :], num, None, ALU.mult))
            dve.sem_inc(s("masks"), 1)
            dve.wait_ge(s("sums"), 3)
            step(nc.vector.tensor_scalar(row1, m.psC[0:1, 0, G:2 * G], float(-E), float(E), ALU.mult, ALU.add))
            step(nc.vector.tensor_tensor(row1, row1, m.psC[0:1, 0, 0:G], ALU.add))
            nc.vector.tensor_copy(start_i, row1).then_inc(s("starts"), 1)
            step(nc.vector.tensor_copy(m.blk_i[:, 0:G], m.psC[0:1, 1, 0:G]))
            step(nc.vector.tensor_scalar(blk128, m.psC[:, 1, 0:G], float(P), None, ALU.mult))
            dve.wait_ge(s("slot_sp"), 16 * 2 * G)
            dve.wait_ge(s("slot_act"), 16 * G)
            nc.vector.tensor_copy(m.et_f[:, 0:G, :], slot_et)
            step(nc.vector.tensor_copy(slot_f, slot_dst))
            rel = m.rel[:, 0:G, :]
            step(nc.vector.tensor_tensor(rel, slot_f, blk128.unsqueeze(2).to_broadcast([P, G, K]), ALU.subtract))
            step(nc.vector.tensor_scalar(valid, rel, float(P), None, ALU.is_lt))
            step(nc.vector.tensor_scalar(slot_f, slot_f, 1.0, None, ALU.add))
            step(nc.vector.tensor_tensor(slot_f, slot_f, valid, ALU.mult))
            step(nc.vector.tensor_scalar(slot_f, slot_f, -1.0, None, ALU.add))
            dve.sem_inc(s("keys"), 1)

        @block.gpsimd
        def _(pool):
            nc.gpsimd.iota(g_no, [[1, G]], base=0, channel_multiplier=0, allow_small_or_imprecise_dtypes=True)
            nc.gpsimd.iota(num, [[0, 1]], base=0, channel_multiplier=1,
                           allow_small_or_imprecise_dtypes=True).then_inc(s("iota"), 1)

        @block.tensor
        def _(pe):
            pe.wait_ge(s("counts"), 1)
            nc.tensor.matmul(m.psC[0:NB, 0, 0:1], counts[:, 0:NB], m.ones[0:EP, 0:1], start=True, stop=True)
            nc.tensor.matmul(m.psC[0:NB, 0, 1:2], counts[:, 1:NB + 1], m.ones[0:EP, 0:1], start=True,
                             stop=True).then_inc(s("sums"), 1)
            pe.wait_ge(s("ng"), 1)
            nc.tensor.matmul(m.psC[0:NB, 0, 2:3], m.upper[:, :], ng, start=True, stop=True).then_inc(s("sums"), 1)
            pe.wait_ge(s("masks"), 1)
            nc.tensor.matmul(m.psC[0:1, 0, 0:G], m.ones[0:NB, 0:1], val, start=True, stop=True)
            nc.tensor.matmul(m.psC[0:1, 0, G:2 * G], m.ones[0:NB, 0:1], mask, start=True, stop=True)
            nc.tensor.matmul(m.psC[:, 1, 0:G], bcol, mask, start=True, stop=True).then_inc(s("sums"), 1)

        def loads(eng, name, pairs):
            def body(g):
                start = eng.value_load(start_i[0:1, bass.ds(g, 1)], min_val=0, max_val=E)
                for dst, src in pairs:
                    eng.dma_start(dst[:, bass.ds(g, 1), :].rearrange("p a k -> p (a k)"),
                                  src[bass.ds(start, GE)].rearrange("(p k) -> p k", k=K)).then_inc(s(name), 16)
            eng.wait_ge(s("starts"), 1)
            with eng.Fori(0, G, 1) as g:
                body(g)

        @block.sync
        def _(sp):
            sp.dma_start(dst_i, a["dst"][0:E].rearrange("(p f) -> p f", p=EP)).then_inc(s("dst"), 16)
            loads(sp, "slot_sp", ((slot_dst, a["dst"]), (m.src_i, a["src"])))
            sp.wait_ge(s("keys"), 1)
            sp.dma_start(m.key_d[1:SL + 1].rearrange("(g p k) -> p g k", p=P, k=K), slot_f).then_inc(s("out"), 16)
            sp.dma_start(m.key_d[0:1].rearrange("(a k) -> a k", a=1), m.guard[:, :]).then_inc(s("out"), 16)
            sp.dma_start(m.key_d[SL + 1:SL + 2].rearrange("(a k) -> a k", a=1), m.guard[:, :]).then_inc(s("out"), 16)
            sp.wait_ge(s("out"), 48)

        @block.scalar
        def _(act):
            loads(act, "slot_act", ((slot_et, a["edge_type_86"]),))

    prev, own, nxt_k, f1, f2 = (b[:, n * RUN:(n + 1) * RUN] for n in range(5))
    with ExitStack() as ctx:
        s = Stage(nc, "runs")
        block = ctx.enter_context(nc.Block())

        @block.sync
        def _(sp):
            for n, t in enumerate((prev, own, nxt_k)):
                sp.dma_start(t, m.key_d[n:n + SL].rearrange("(p f) -> p f", p=P)).then_inc(s("keys"), 16)
            sp.wait_ge(s("flags"), 1)
            for t, d in ((f1, m.first_d), (f2, m.last_d)):
                sp.dma_start(d.rearrange("(p f) -> p f", p=P), t).then_inc(s("out"), 16)
            sp.wait_ge(s("out"), 32)
            for t, d in ((m.first_t, m.first_d), (m.last_t, m.last_d)):
                sp.dma_start(t[:, :, :], d.rearrange("(g p k) -> p g k", p=P, k=K)).then_inc(s("in"), 16)
            sp.wait_ge(s("in"), 32)

        @block.vector
        def _(dve):
            dve.wait_ge(s("keys"), 48)
            nc.vector.tensor_tensor(f1, own, prev, ALU.not_equal)
            nc.vector.tensor_tensor(f2, own, nxt_k, ALU.not_equal).then_inc(s("flags"), 1)
            dve.wait_ge(s("flags"), 1)
            nc.vector.tensor_scalar(m.new_seg[:, :], f1, -BIG, None, ALU.mult)
            nc.vector.tensor_scalar(m.end_seg[:, :], f2, -BIG, None, ALU.mult)



def transposed(nc, m, name):
    with ExitStack() as ctx:
        s = Stage(nc, f"xt_{name}")
        block = ctx.enter_context(nc.Block())
        steps = [range(b, min(b + 4, NB)) for b in range(0, NB, 4)]

        @block.tensor
        def _(pe):
            for n, bs in enumerate(steps):
                need(pe, s("copied"), n - 1)
                for b in bs:
                    ins = nc.tensor.transpose(m.psT[0:D, n % 2, (b - bs[0]) * P:(b - bs[0] + 1) * P], m.X[:, b, :],
                                              m.ident[:, :])
                ins.then_inc(s("turned"), 1)

        @block.scalar
        def _(act):
            for n, bs in enumerate(steps):
                act.wait_ge(s("turned"), n + 1)
                nc.scalar.copy(m.XT[0:D, bs[0] * P:(bs[-1] + 1) * P], m.psT[0:D, n % 2, 0:len(bs) * P]
                               ).then_inc(s("copied"), 1)


def tables(nc, m, name, weights, keep, width, tab, side, linear=None):
    w = m.table_d[name].shape[1]
    out = m.big[:, 0:NB * w].rearrange("p (b w) -> p b w", b=NB)
    rows = D + 1 if keep else D
    with ExitStack() as ctx:
        s = Stage(nc, f"tab_{name}")
        block = ctx.enter_context(nc.Block())

        @block.tensor
        def _(pe):
            for b in range(NB):
                need(pe, s("side"), b - 1)
                ins = nc.tensor.matmul(m.psA[:, b % 2, 0:width], m.XT[0:rows, b * P:(b + 1) * P], weights,
                                       start=True, stop=True)
                if linear is not None:
                    ins = nc.tensor.matmul(m.psA[:, b % 2, width:width + 2 * H3], m.XT[0:rows, b * P:(b + 1) * P],
                                           linear, start=True, stop=True)
                ins.then_inc(s("made"), 1)

        @block.scalar
        def _(act):
            for b in range(NB):
                act.wait_ge(s("made"), b + 1)
                tab(out[:, b, :], m.psA[:, b % 2, :]).then_inc(s("tab"), 1)

        @block.vector
        def _(dve):
            if w > W3 or name == "r":
                lo = W3 if w > W3 else 0
                nc.vector.tensor_copy(out[:, :, lo:lo + D], m.X[:, :, :]).then_inc(s("x"), 1)
            else:
                dve.sem_inc(s("x"), 1)
            for b in range(NB):
                dve.wait_ge(s("tab"), b + 1)
                side(b, m.psA[:, b % 2, :]).then_inc(s("side"), 1)

        @block.sync
        def _(sp):
            sp.wait_ge(s("x"), 1)
            sp.wait_ge(s("tab"), NB)
            sp.dma_start(m.table_d[name].rearrange("(b p) w -> p b w", p=P), out).then_inc(s("out"), 16)
            sp.wait_ge(s("out"), 16)



def normalised(nc, m, tag, addends, relu=False):
    with ExitStack() as ctx:
        s = Stage(nc, f"ln_{tag}")
        block = ctx.enter_context(nc.Block())
        mean, var = m.line[:, 0, :], m.line[:, 1, :]
        wide = [P, NB, D]

        @block.vector
        def _(dve):
            n = [0]

            def step(ins):
                n[0] += 1
                ins.then_inc(s("v"), 1)
                dve.wait_ge(s("v"), n[0])
            total = addends[0]
            for t in addends[1:]:
                step(nc.vector.tensor_tensor(m.Z[:, :, :], total[:, :, :], t[:, :, :], ALU.add))
                total = m.Z
            step(nc.vector.tensor_reduce(mean, m.Z[:, :, :], AX.X, ALU.add))
            step(nc.vector.tensor_scalar(mean, mean, 1.0 / D, None, ALU.mult))
            step(nc.vector.tensor_tensor(m.Z[:, :, :], m.Z[:, :, :], mean.unsqueeze(2).to_broadcast(wide),
                                         ALU.subtract))
            step(nc.vector.tensor_tensor(m.X[:, :, :], m.Z[:, :, :], m.Z[:, :, :], ALU.mult))
            step(nc.vector.tensor_reduce(var, m.X[:, :, :], AX.X, ALU.add))
            dve.sem_inc(s("var"), 1)
            dve.wait_ge(s("root"), 1)
            step(nc.vector.reciprocal(var, var))
            nc.vector.tensor_tensor(m.X[:, :, :], m.Z[:, :, :], var.unsqueeze(2).to_broadcast(wide), ALU.mult)

        @block.scalar
        def _(act):
            act.wait_ge(s("var"), 1)
            nc.scalar.activation(var, var, ACT.Sqrt, bias=m.eps[:, 0:1], scale=1.0 / D).then_inc(s("root"), 1)



def gather(nc, m, s, pool, table, w, used, stored=False, index=None, tiles=G * K):
    def indices(g, slot):
        at = m.src_i[:, bass.ds(g, 1), :].rearrange("p a k -> p (a k)") if index is None else \
            index[:, bass.ds(g * K, K)]
        nc.gpsimd.tensor_copy(m.gi[:, slot, :], at).then_inc(s("indices"), 1)

    def body(i, u):
        g = i * RING + u
        ahead = (u + 1) % RING
        need(pool, s(f"rows{ahead}"), 16 * K * (i if ahead else i + 1))
        indices(g + 1, ahead)
        need(pool, used, g - RING + 1)
        if stored:
            need(pool, s(f"xs{u}"), 16 * i)
        pool.wait_ge(s("indices"), g + 1)
        pool.sem_inc(s("ticket"), 1)
        for k in range(K):
            pool.indirect_dma_start(m.gx[:, u, k, 0:w], None, table,
                                    bass.IndirectOffsetOnAxis(m.gi[:, u, k:k + 1].bitcast(U32), 0)
                                    ).then_inc(s(f"rows{u}"), 16)
    indices(0, 0)
    groups(pool, body, tiles // (K * RING))


def one_hot(nc, m, g, slot, half_width=False):
    to, pattern = (m.oh_b, m.iota_b) if half_width else (m.oh, m.iota_row)
    return nc.vector.tensor_tensor(
        to[:, slot, :, :], pattern[:, :].unsqueeze(1).to_broadcast([P, K, P]),
        m.rel[:, bass.ds(g, 1), :].rearrange("p a k -> p (a k)").unsqueeze(2).to_broadcast([P, K, P]),
        ALU.is_equal)


def add_up(nc, m, dve, g, w, ps, s):
    blk = dve.value_load(m.blk_i[0:1, bass.ds(g, 1)], min_val=0, max_val=NB - 1)
    dve.wait_ge(s("added"), g + 1)
    need(dve, s("acc"), g + 1)
    acc = m.big[:, 0:NB * w].rearrange("p (b w) -> p b w", b=NB)[:, bass.ds(blk, 1), :].rearrange(
        "p a w -> p (a w)")
    return nc.vector.tensor_tensor(acc, acc, ps, ALU.add)


def logits(nc, m, name, heads, cols, layer):
    w = m.table_d[name].shape[1]
    dh = cols // heads
    gat = layer is not None
    at = W3 if gat else w - D

    def prod(half):
        return m.work[:, half, 0:K * cols]

    def turned_b(half):
        return m.psT[:, half, 0:K * P // 2].bitcast(BF16)

    with ExitStack() as ctx:
        s = Stage(nc, f"log_{name}")
        block = ctx.enter_context(nc.Block())

        @block.gpsimd
        def _(pool):
            gather(nc, m, s, pool, m.table_d[name], w, s("read"), True)

        @block.vector
        def _(dve):
            def finish(i, u):
                g = i * RING + u
                dve.wait_ge(s("reduced"), g + 1)
                dve.wait_ge(s("read"), g + 1)
                need(dve, s(f"lg{u}"), 16 * i)
                nc.vector.scalar_tensor_tensor(out=m.lg[:, u, 0:K * heads], in0=m.red[:, u % 2, :],
                                               scalar=1.0 - LEAK, in1=m.lin[:, u % 2, :], op0=ALU.mult,
                                               op1=ALU.add).then_inc(s("logits"), 1)

            def reduce(i, u):
                g = i * RING + u
                half = u % 2
                dve.wait_ge(s("products"), g + 1)
                if gat:
                    need(dve, s("logits"), g - 1)
                    nc.vector.tensor_reduce(m.red[:, half, :], prod(half).rearrange("p (k c) -> p k c", c=dh),
                                            AX.X, ALU.add).then_inc(s("reduced"), 1)
                else:
                    need(dve, s(f"lg{u}"), 16 * i)
                    nc.vector.tensor_reduce(m.lg[:, u, 0:K * heads],
                                            prod(half).rearrange("p (k c) -> p k c", c=dh), AX.X, ALU.add
                                            ).then_inc(s("logits"), 1)

            def products(g, slot):
                half = slot % 2
                apart, whole = K - PE_ADDS, K
                tiles = prod(half).rearrange("p (k c) -> p k c", k=K)
                sums = m.psA[:, half, :].rearrange("p (k c) -> p k c", k=K)
                att = m.att3[:, layer, :].unsqueeze(1)
                nc.vector.tensor_tensor(tiles[:, 0:apart, :], m.gx[:, slot, 0:apart, 0:cols], sums[:, 0:apart, :],
                                        ALU.add).then_inc(s("summed"), 1)
                if PE_ADDS:
                    nc.vector.scalar_tensor_tensor(out=tiles[:, apart:whole, :], in0=sums[:, apart:whole, :],
                                                   scalar=0.0, in1=att.to_broadcast([P, PE_ADDS, cols]),
                                                   op0=ALU.max, op1=ALU.mult)
                nc.vector.tensor_tensor(m.lin[:, half, :].rearrange("p (k h) -> p k h", k=K),
                                        m.gx[:, slot, :, W3 + D:TAB3],
                                        m.psC[:, half, 0:K * H3].rearrange("p (k h) -> p k h", k=K), ALU.add
                                        ).then_inc(s("read"), 1)
                dve.wait_ge(s("summed"), g + 1)
                nc.vector.scalar_tensor_tensor(out=tiles[:, 0:apart, :], in0=tiles[:, 0:apart, :], scalar=0.0,
                                               in1=att.to_broadcast([P, apart, cols]), op0=ALU.max,
                                               op1=ALU.mult).then_inc(s("products"), 1)

            def body(i, u):
                g = i * RING + u
                need(dve, s("turned"), g)
                one_hot(nc, m, g + 3, (u + 3) % RING, True).then_inc(s("one_hot"), 1)
                if gat and u > 1:
                    finish(i, u - 2)
                elif gat and (not isinstance(i, int) or i):
                    finish(i - 1, u + RING - 2)
                dve.wait_ge(s(f"rows{u}"), 16 * K * (i + 1))
                dve.wait_ge(s("projected"), g + 1)
                need(dve, s("logits"), g - 1)
                if gat:
                    products(g, u)
                else:
                    nc.vector.tensor_tensor(prod(u % 2).rearrange("p (k c) -> p k c", k=K), m.gx[:, u, :, 0:cols],
                                            m.psA[:, u % 2, 0:K * cols].rearrange("p (k c) -> p k c", k=K),
                                            ALU.mult).then_inc(s("products"), 1)
                    dve.wait_ge(s("products"), g + 1)
                    dve.sem_inc(s("read"), 1)
                if u:
                    reduce(i, u - 1)
                elif not isinstance(i, int) or i:
                    reduce(i - 1, RING - 1)
            for g in range(3):
                one_hot(nc, m, g, g, True).then_inc(s("one_hot"), 1)
            groups(dve, body)
            last = G // RING - 1
            if gat:
                finish(last, RING - 2)
            reduce(last, RING - 1)
            if gat:
                finish(last, RING - 1)

        @block.scalar
        def _(act):
            def turn(g, half):
                act.wait_ge(s("turned"), g + 1)
                need(act, s("projected"), g - 1)
                nc.scalar.copy(m.ohT[:, half, :], turned_b(half)).then_inc(s("ohT"), 1)

            def body(i, u):
                turn(i * RING + u + 2, u % 2)
            for g in range(2):
                turn(g, g)
            groups(act, body)

        @block.tensor
        def _(pe):
            def turn(g, slot):
                pe.wait_ge(s("one_hot"), g + 1)
                need(pe, s("ohT"), g - 1)
                for k in range(K):
                    ins = nc.tensor.transpose(turned_b(slot % 2)[:, k * P:(k + 1) * P], m.oh_b[:, slot, k, :],
                                              m.ident_b[:, :])
                ins.then_inc(s("turned"), 1)

            def project(g, slot, turns_done):
                half = slot % 2
                blk = pe.value_load(m.blk_i[0:1, bass.ds(g, 1)], min_val=0, max_val=NB - 1)
                pe.wait_ge(s("ohT"), g + 1)
                need(pe, s("products" if gat else "read"), g - 1)
                rows = m.R[:, bass.ds(blk, 1), 0:cols].rearrange("p a c -> p (a c)")
                for k in range(K):
                    adds = gat and k >= K - PE_ADDS
                    if adds and k == K - PE_ADDS:
                        pe.wait_ge(s(f"rows{slot}"), 16 * K * turns_done)
                    to, turned = m.psA[:, half, k * cols:(k + 1) * cols], m.ohT[:, half, k * P:(k + 1) * P]
                    ins = nc.tensor.matmul(to, turned, rows, start=True, stop=not adds)
                    if adds:
                        ins = nc.tensor.matmul(to, m.ident[:, :], m.gx[:, slot, k, 0:cols], start=False, stop=True)
                    if gat:
                        ins = nc.tensor.matmul(m.psC[:, half, k * H3:(k + 1) * H3], turned,
                                               m.R[:, bass.ds(blk, 1), W3:ROW3].rearrange("p a c -> p (a c)"),
                                               start=True, stop=True)
                ins.then_inc(s("projected"), 1)

            def body(i, u):
                g = i * RING + u
                if not (isinstance(g, int) and g == G - 1):
                    project(g + 1, (u + 1) % RING, i + 1 if u < RING - 1 else i + 2)
                turn(g + 2, (u + 2) % RING)
            for g in range(2):
                turn(g, g)
            project(0, 0, 1)
            groups(pe, body, G // RING - 1)
            for u in range(RING):
                body(G // RING - 1, u)

        @block.sync
        def _(sp):
            lview = m.logit_d[name].rearrange("(g p k) h -> g p (k h)", p=P, k=K)
            xview = m.xs_d[name].rearrange("(g p k) d -> g p k d", p=P, k=K)

            def store(i, u):
                g = i * RING + u
                sp.wait_ge(s("logits"), g + 1)
                sp.dma_start(lview[bass.ds(g, 1)].rearrange("a p w -> (a p) w"), m.lg[:, u, 0:K * heads]
                             ).then_inc(s(f"lg{u}"), 16)

            def body(i, u):
                g = i * RING + u
                sp.wait_ge(s(f"rows{u}"), 16 * K * (i + 1))
                sp.dma_start(xview[bass.ds(g, 1)].rearrange("a p k d -> (a p) k d"), m.gx[:, u, :, at:at + D]
                             ).then_inc(s(f"xs{u}"), 16)
                if u:
                    store(i, u - 1)
                elif not isinstance(i, int) or i:
                    store(i - 1, RING - 1)
            groups(sp, body)
            store(G // RING - 1, RING - 1)
            for u in range(RING):
                sp.wait_ge(s(f"xs{u}"), 16 * (G // RING))
                sp.wait_ge(s(f"lg{u}"), 16 * (G // RING))


def softmax_parts(nc, m, name, heads):
    wide = RUN * heads
    L, F = m.big[:, 0:wide], m.big[:, wide:2 * wide]
    by_head = [t.rearrange("p (f h) -> p h f", h=heads) for t in (L, F)]
    tail, flag, carry = (m.c8[:, n, 0:heads] for n in range(3))
    tail_r, flag_r, out_r, carry_r = (m.r8[0:heads, n, :] for n in range(4))

    with ExitStack() as ctx:
        s = Stage(nc, f"soft_{name}")
        block = ctx.enter_context(nc.Block())

        @block.sync
        def _(sp):
            sp.dma_start(L, m.logit_d[name].rearrange("(p f) h -> p (f h)", p=P)).then_inc(s("in"), 16)
            outs = 1
            if name in m.max_d and name != "t":
                sp.wait_ge(s("maxima"), 1)
                sp.dma_start(m.max_d[name].rearrange("(p f) h -> p (f h)", p=P), F).then_inc(s("out"), 16)
                outs = 2
            sp.wait_ge(s("exp"), 1)
            sp.dma_start(m.prob_d[name].rearrange("(p f) h -> p (f h)", p=P), L).then_inc(s("out"), 16)
            sp.wait_ge(s("out"), 16 * outs)

        @block.vector
        def _(dve):
            n = [0]

            def step(ins):
                n[0] += 1
                ins.then_inc(s("v"), 1)
                dve.wait_ge(s("v"), n[0])
            dve.wait_ge(s("in"), 16)
            for back in range(2):
                way = slice(None, None, -1) if back else slice(None)
                cuts = m.end_seg if back else m.new_seg
                edge = 0 if back else RUN - 1
                source = by_head[1 if back else 0]
                for h in range(heads):
                    ins = nc.vector.tensor_tensor_scan(by_head[1][:, h, way], cuts[:, way], source[:, h, way],
                                                       -BIG, ALU.add, ALU.max)
                step(ins)
                nc.vector.tensor_copy(tail, by_head[1][:, :, edge])
                step(nc.vector.tensor_reduce(m.c8[:, 3, 0:1], cuts[:, :], AX.X, ALU.min))
                step(nc.vector.tensor_copy(flag, m.c8[:, 3, 0:1].to_broadcast([P, heads])))
                dve.sem_inc(s("tails"), 1)
                dve.wait_ge(s("rows"), back + 1)
                nc.vector.tensor_copy(tail_r, m.psT[0:heads, 0, 0:P])
                step(nc.vector.tensor_copy(flag_r, m.psT[0:heads, 0, P:2 * P]))
                step(nc.vector.tensor_tensor_scan(out_r[:, way], flag_r[:, way], tail_r[:, way], -BIG,
                                                  ALU.add, ALU.max))
                if back:
                    nc.vector.memset(carry_r[:, P - 1:P], -BIG)
                    step(nc.vector.tensor_copy(carry_r[:, 0:P - 1], out_r[:, 1:P]))
                else:
                    nc.vector.memset(carry_r[:, 0:1], -BIG)
                    step(nc.vector.tensor_copy(carry_r[:, 1:P], out_r[:, 0:P - 1]))
                dve.sem_inc(s("carries"), 1)
                dve.wait_ge(s("cols"), back + 1)
                step(nc.vector.tensor_copy(carry, m.psT[:, 1, 0:heads]))
                for h in range(heads):
                    ins = nc.vector.tensor_tensor_scan(by_head[1][:, h, way], cuts[:, way], by_head[1][:, h, way],
                                                       carry[:, h:h + 1], ALU.add, ALU.max)
                step(ins)
            step(nc.vector.tensor_tensor(L, L, F, ALU.subtract))
            dve.sem_inc(s("shifted"), 1)
            if name != "t":
                f3 = F.rearrange("p (f h) -> p f h", h=heads)
                nc.vector.scalar_tensor_tensor(out=f3, in0=m.new_seg[:, :].unsqueeze(2).to_broadcast([P, RUN, heads]),
                                               scalar=-1.0, in1=f3, op0=ALU.is_lt, op1=ALU.mult
                                               ).then_inc(s("maxima"), 1)

        @block.scalar
        def _(act):
            act.wait_ge(s("shifted"), 1)
            nc.scalar.activation(L, L, ACT.Exp).then_inc(s("exp"), 1)

        @block.tensor
        def _(pe):
            for back in range(2):
                pe.wait_ge(s("tails"), back + 1)
                nc.tensor.transpose(m.psT[0:heads, 0, 0:P], tail, m.ident[:, :])
                nc.tensor.transpose(m.psT[0:heads, 0, P:2 * P], flag, m.ident[:, :]).then_inc(s("rows"), 1)
                pe.wait_ge(s("carries"), back + 1)
                nc.tensor.transpose(m.psT[:, 1, 0:heads], carry_r, m.ident[0:heads, 0:heads]).then_inc(s("cols"), 1)


def weighted_sums(nc, m, name, heads, acc_w):
    gat = name != "t"
    cols = heads * D if gat else D
    extras = 3 if gat else 1
    parts, turns = 4, G // RING
    ends = (turns // 10, turns // 3, 2 * turns // 3, turns)
    n_loads = 2 if gat else 1
    w_all = m.probs[:, 0:G * K * heads].rearrange("p (g w) -> p g w", g=G)
    m_all = m.maxima.rearrange("p (g w) -> p g w", g=G)

    def rhs(half):
        return m.work[:, half, 0:K * acc_w].rearrange("p (k w) -> p k w", k=K)

    with ExitStack() as ctx:
        s = Stage(nc, f"sum_{name}")
        block = ctx.enter_context(nc.Block())

        def in_parts(eng, body, load_part=None):
            for n, end in enumerate(ends):
                if load_part is None:
                    eng.wait_ge(s(f"part{n}"), 16 * n_loads)
                elif n + 1 < parts:
                    load_part(n + 1)
                begin = ends[n - 1] if n else 2
                if n == 0:
                    for i in range(2):
                        for u in range(RING):
                            body(i, u)
                with eng.Fori(begin, end, 1) as i:
                    for u in range(RING):
                        body(i, u)

        @block.sync
        def _(sp):
            xview = m.xs_d[name].rearrange("(g p k) d -> g p (k d)", p=P, k=K)

            def body(i, u):
                g = i * RING + u
                need(sp, s("added"), g - RING + 1)
                sp.dma_start(m.xl[:, u, :, :].rearrange("p k d -> p (k d)"),
                             xview[bass.ds(g, 1)].rearrange("a p w -> (a p) w")).then_inc(s(f"in{u}"), 16)

            def load_part(n):
                for to, d in ((w_all, m.prob_d), (m_all, m.max_d))[:n_loads]:
                    view = d[name].rearrange("(g p k) h -> p g (k h)", p=P, k=K)
                    lo, hi = (ends[n - 1] if n else 0) * RING, ends[n] * RING
                    sp.dma_start(to[:, lo:hi, :], view[:, lo:hi, :]).then_inc(s(f"part{n}"), 16)
            load_part(0)
            in_parts(sp, body, load_part)

        @block.vector
        def _(dve):
            def collect(g, half):
                add_up(nc, m, dve, g, acc_w, m.psC[:, half, 0:acc_w], s).then_inc(s("acc"), 1)

            def body(i, u):
                g = i * RING + u
                weights = w_all[:, bass.ds(g, 1), :].rearrange("p a (k h) -> p (a k) h", k=K).unsqueeze(3)
                dve.wait_ge(s(f"in{u}"), 16 * (i + 1))
                need(dve, s("added"), g - 1)
                if gat:
                    shape = [P, K, heads, D]
                    p = weights.to_broadcast(shape)
                    x = m.xl[:, u, :, :].unsqueeze(2).to_broadcast(shape)
                    o = rhs(u % 2)[:, :, 0:cols].rearrange("p k (h c) -> p k h c", h=heads)
                else:
                    shape = [P, K, heads, D // heads]
                    p = weights.to_broadcast(shape)
                    x = m.xl[:, u, :, :].rearrange("p k (h c) -> p k h c", h=heads)
                    o = rhs(u % 2)[:, :, 0:cols].rearrange("p k (h c) -> p k h c", h=heads)
                nc.vector.tensor_tensor(o, p, x, ALU.mult).then_inc(s("rhs"), 1)
                one_hot(nc, m, g, u).then_inc(s("one_hot"), 1)
                if u:
                    collect(g - 1, (u - 1) % 2)
                elif not isinstance(i, int) or i:
                    collect(g - 1, 1)
            nc.vector.memset(m.big[:, 0:NB * acc_w], 0.0).then_inc(s("acc"), 1)
            in_parts(dve, body)
            collect(G - 1, 1)

        @block.scalar
        def _(act):
            def body(i, u):
                g = i * RING + u
                need(act, s("added"), g - 1)
                r = rhs(u % 2)
                for n, source in enumerate((w_all, m_all)[:n_loads]):
                    nc.scalar.copy(r[:, :, cols + n * heads:cols + (n + 1) * heads],
                                   source[:, bass.ds(g, 1), :].rearrange("p a (k h) -> p (a k) h", k=K)
                                   ).then_inc(s("extra"), 1)
                if gat:
                    nc.scalar.copy(r[:, :, cols + 2 * heads:cols + 2 * heads + 1],
                                   m.first_t[:, bass.ds(g, 1), :].rearrange("p a k -> p k a")
                                   ).then_inc(s("extra"), 1)
            in_parts(act, body)

        @block.tensor
        def _(pe):
            def body(i, u):
                g = i * RING + u
                pe.wait_ge(s("one_hot"), g + 1)
                pe.wait_ge(s("rhs"), g + 1)
                pe.wait_ge(s("extra"), extras * (g + 1))
                need(pe, s("acc"), g)
                for k in range(K):
                    ins = nc.tensor.matmul(m.psC[:, u % 2, 0:acc_w], m.oh[:, u, k, :], rhs(u % 2)[:, k, :],
                                           start=(k == 0), stop=(k == K - 1))
                ins.then_inc(s("added"), 1)
            groups(pe, body)


def transformer_out(nc, m):
    acc = m.big[:, 0:NB * ACC0].rearrange("p (b w) -> p b w", b=NB)
    msg = acc[:, :, 0:D].rearrange("p b (h c) -> p b h c", h=H0)
    den = m.small[:, 0, :, 0:H0]
    steps = [range(b, min(b + 4, NB)) for b in range(0, NB, 4)]
    with ExitStack() as ctx:
        s = Stage(nc, "out_t")
        block = ctx.enter_context(nc.Block())

        @block.vector
        def _(dve):
            nc.vector.tensor_scalar(den, acc[:, :, D:D + H0], 1e-16, None, ALU.max).then_inc(s("den"), 1)
            dve.wait_ge(s("den"), 1)
            nc.vector.reciprocal(den, den).then_inc(s("den"), 1)
            dve.wait_ge(s("den"), 2)
            nc.vector.tensor_tensor(msg, msg, den.unsqueeze(3).to_broadcast([P, NB, H0, D // H0]), ALU.mult
                                    ).then_inc(s("msg"), 1)
            for b in range(NB):
                dve.wait_ge(s("made"), b + 1)
                nc.vector.tensor_copy(m.Y[:, b, :], m.psC[:, b % 2, 0:D]).then_inc(s("y"), 1)

        @block.scalar
        def _(act):
            for n, bs in enumerate(steps):
                act.wait_ge(s("turned"), n + 1)
                nc.scalar.copy(m.XT[0:D, bs[0] * P:(bs[-1] + 1) * P], m.psT[0:D, n % 2, 0:len(bs) * P]
                               ).then_inc(s("copied"), 1)

        @block.tensor
        def _(pe):
            pe.wait_ge(s("msg"), 1)
            for n, bs in enumerate(steps):
                need(pe, s("copied"), n - 1)
                for b in bs:
                    ins = nc.tensor.transpose(m.psT[0:D, n % 2, (b - bs[0]) * P:(b - bs[0] + 1) * P],
                                              acc[:, b, 0:D], m.ident[:, :])
                ins.then_inc(s("turned"), 1)
            pe.wait_ge(s("copied"), len(steps))
            for b in range(NB):
                need(pe, s("y"), b - 1)
                nc.tensor.matmul(m.psC[:, b % 2, 0:D], m.XT[0:D, b * P:(b + 1) * P], m.wo0[:, :], start=True,
                                 stop=True).then_inc(s("made"), 1)


def relation_walk(nc, m):
    name = "r"
    wq = D + NBASE

    def xs(u):
        return m.gx[:, u, :, 0:D]

    def outer(half):
        return m.work[:, half, :].rearrange("p (k w) -> p k w", k=K)

    with ExitStack() as ctx:
        s = Stage(nc, "rel")
        block = ctx.enter_context(nc.Block())

        @block.gpsimd
        def _(pool):
            gather(nc, m, s, pool, m.table_d[name], 2 * D, s("rhs"))

        @block.vector
        def _(dve):
            def one_hots(g, slot):
                one_hot(nc, m, g, slot).then_inc(s("one_hot"), 1)
                nc.vector.tensor_tensor(
                    m.typ[:, slot, :, :], m.iota_row[:, 0:NREL].unsqueeze(1).to_broadcast([P, K, NREL]),
                    m.et_f[:, bass.ds(g, 1), :].rearrange("p a k -> p (a k)").unsqueeze(2).to_broadcast([P, K, NREL]),
                    ALU.is_equal).then_inc(s("one_hot"), 1)

            def collect(g, half):
                add_up(nc, m, dve, g, ACC1, m.psA[:, half, 0:ACC1], s).then_inc(s("acc"), 1)

            def body(i, u):
                g = i * RING + u
                half = u % 2
                need(dve, s("added"), g - 1)
                one_hots(g + 2, (u + 2) % RING)
                dve.wait_ge(s(f"rows{u}"), 16 * K * (i + 1))
                dve.wait_ge(s("fetched"), g + 1)
                fetched = m.psC[:, half, 0:K * wq].rearrange("p (k w) -> p k w", k=K)
                dots = m.lx[:, half, :, :]
                nc.vector.tensor_tensor(dots, m.gx[:, u, :, D:2 * D], fetched[:, :, 0:D], ALU.mult
                                        ).then_inc(s("dots"), 1)
                dve.wait_ge(s("dots"), g + 1)
                nc.vector.tensor_reduce(m.a1[:, half, 0, :], dots, AX.X, ALU.add).then_inc(s("score"), 1)
                dve.wait_ge(s("score"), g + 1)
                nc.vector.tensor_scalar(m.a1[:, half, 1, :], m.a1[:, half, 0, :], D ** -0.5, 0.0, ALU.mult, ALU.max
                                        ).then_inc(s("relu"), 1)
                dve.wait_ge(s("tanh"), g + 1)
                nc.vector.tensor_tensor(m.ac[:, half, :, :], fetched[:, :, D:wq],
                                        m.a1[:, half, 2, :].unsqueeze(2).to_broadcast([P, K, NBASE]), ALU.mult
                                        ).then_inc(s("ac"), 1)
                nc.vector.tensor_tensor(m.lx[:, half, :, :], xs(u),
                                        m.last_t[:, bass.ds(g, 1), :].rearrange("p a k -> p (a k)").unsqueeze(2)
                                        .to_broadcast([P, K, D]), ALU.mult).then_inc(s("lastx"), 1)
                dve.wait_ge(s("ac"), g + 1)
                shape = [P, K, NBASE, D]
                nc.vector.tensor_tensor(outer(half).rearrange("p k (b c) -> p k b c", b=NBASE),
                                        m.ac[:, half, :, :].unsqueeze(3).to_broadcast(shape),
                                        xs(u).unsqueeze(2).to_broadcast(shape), ALU.mult).then_inc(s("rhs"), 1)
                if u:
                    collect(g - 1, (u - 1) % 2)
                elif not isinstance(i, int) or i:
                    collect(g - 1, 1)
            nc.vector.memset(m.big[:, 0:NB * ACC1], 0.0).then_inc(s("acc"), 1)
            for g in range(2):
                one_hots(g, g)
            groups(dve, body)
            collect(G - 1, 1)

        @block.scalar
        def _(act):
            def turn(g, half):
                act.wait_ge(s("turned"), g + 1)
                need(act, s("fetched"), g - 1)
                nc.scalar.copy(m.ohT[:, half, :], m.psT[:, 0, :]).then_inc(s("ohT"), 1)
                nc.scalar.copy(m.typT[:, half, :], m.psT[0:NREL, 1, :]).then_inc(s("ohT"), 1)

            def body(i, u):
                g = i * RING + u
                act.wait_ge(s("relu"), g + 1)
                nc.scalar.activation(m.a1[:, u % 2, 2, :], m.a1[:, u % 2, 1, :], ACT.Tanh).then_inc(s("tanh"), 1)
                turn(g + 2, u % 2)
            for g in range(2):
                turn(g, g)
            groups(act, body)

        @block.tensor
        def _(pe):
            def turn(g, slot):
                pe.wait_ge(s("one_hot"), 2 * (g + 1))
                need(pe, s("ohT"), 2 * g)
                for k in range(K):
                    nc.tensor.transpose(m.psT[:, 0, k * P:(k + 1) * P], m.oh[:, slot, k, :], m.ident[:, :])
                    ins = nc.tensor.transpose(m.psT[0:NREL, 1, k * P:(k + 1) * P], m.typ[:, slot, k, :],
                                              m.ident[:, :])
                ins.then_inc(s("turned"), 1)

            def add(g, slot):
                half = slot % 2
                pe.wait_ge(s("rhs"), g + 1)
                pe.wait_ge(s("lastx"), g + 1)
                need(pe, s("acc"), g)
                for k in range(K):
                    nc.tensor.matmul(m.psA[:, half, 0:NBASE * D], m.oh[:, slot, k, :], outer(half)[:, k, :],
                                     start=(k == 0), stop=(k == K - 1))
                    ins = nc.tensor.matmul(m.psA[:, half, NBASE * D:ACC1], m.oh[:, slot, k, :], m.lx[:, half, k, :],
                                           start=(k == 0), stop=(k == K - 1))
                ins.then_inc(s("added"), 1)

            def fetch(g, half):
                blk = pe.value_load(m.blk_i[0:1, bass.ds(g, 1)], min_val=0, max_val=NB - 1)
                pe.wait_ge(s("ohT"), 2 * (g + 1))
                need(pe, s("ac"), g - 1)
                rows = m.Rr[:, bass.ds(blk, 1), :].rearrange("p a c -> p (a c)")
                for k in range(K):
                    to = m.psC[:, half, k * wq:(k + 1) * wq]
                    nc.tensor.matmul(to, m.ohT[:, half, k * P:(k + 1) * P], rows, start=True, stop=False)
                    ins = nc.tensor.matmul(to, m.typT[:, half, k * P:(k + 1) * P], m.relt[:, :], start=False,
                                           stop=True)
                ins.then_inc(s("fetched"), 1)

            def body(i, u):
                g = i * RING + u
                turn(g + 2, (u + 2) % RING)
                fetch(g + 1, (u + 1) % 2)
                add(g, u)
            for g in range(2):
                turn(g, g)
            fetch(0, 0)
            groups(pe, body)


def relational_out(nc, m):
    acc = m.big[:, 0:NB * ACC1].rearrange("p (b w) -> p b w", b=NB)
    nq = NBASE * D // P
    with ExitStack() as ctx:
        s = Stage(nc, "out_r")
        block = ctx.enter_context(nc.Block())

        @block.tensor
        def _(pe):
            def turn(b):
                need(pe, s("copied"), 2 * (b - 1))
                for q in range(nq):
                    nc.tensor.transpose(m.psA[:, b % 2, q * P:(q + 1) * P], acc[:, b, q * P:(q + 1) * P],
                                        m.ident[:, :])
                nc.tensor.transpose(m.psA[0:D, b % 2, 512:512 + P], acc[:, b, NBASE * D:ACC1], m.ident[:, :]
                                    ).then_inc(s("turned"), 1)
            turn(0)
            for b in range(NB):
                if b + 1 < NB:
                    turn(b + 1)
                pe.wait_ge(s("copied"), 2 * (b + 1))
                need(pe, s("y"), b - 1)
                zt = m.work[:, b % 2, :]
                for q in range(nq):
                    nc.tensor.matmul(m.psC[:, b % 2, 0:D], zt[:, q * P:(q + 1) * P], m.w1b[:, q, :], start=(q == 0),
                                     stop=False)
                nc.tensor.matmul(m.psC[:, b % 2, 0:D], zt[0:D, 512:512 + P], m.w1s[:, :], start=False, stop=True
                                 ).then_inc(s("made"), 1)

        @block.scalar
        def _(act):
            for b in range(NB):
                act.wait_ge(s("turned"), b + 1)
                need(act, s("made"), b - 1)
                zt = m.work[:, b % 2, :]
                nc.scalar.copy(zt[:, 0:512], m.psA[:, b % 2, 0:512]).then_inc(s("copied"), 1)
                nc.scalar.copy(zt[0:D, 512:512 + P], m.psA[0:D, b % 2, 512:512 + P]).then_inc(s("copied"), 1)

        @block.vector
        def _(dve):
            for b in range(NB):
                dve.wait_ge(s("made"), b + 1)
                nc.vector.tensor_scalar(m.Y[:, b, :], m.psC[:, b % 2, 0:D], 0.0, None, ALU.max).then_inc(s("y"), 1)


def relational(nc, m):
    transposed(nc, m, "r")

    def side(b, ps):
        return nc.vector.tensor_copy(m.Rr[:, b, 0:D], ps[:, D:2 * D])

    with ExitStack() as ctx:
        block = ctx.enter_context(nc.Block())

        @block.vector
        def _(dve):
            nc.vector.memset(m.Rr[:, :, D:D + NBASE], 0.0)
    tables(nc, m, "r", m.w1[:, :], True, 2 * D, lambda o, ps: nc.scalar.copy(o[:, D:2 * D], ps[:, 0:D]), side)
    relation_walk(nc, m)
    relational_out(nc, m)
    normalised(nc, m, "r", (m.X, m.Y))


def edge_tiles(nc, m, a):
    src_i, low_i, blk_i = (m.big[:, n * TILES:(n + 1) * TILES].bitcast(I32) for n in range(3))
    with ExitStack() as ctx:
        s = Stage(nc, "tiles")
        block = ctx.enter_context(nc.Block())

        @block.sync
        def _(sp):
            for dst, name in ((src_i, "src"), (m.dst_i[:, 0:TILES], "dst"), (m.w_e[:, :], "edge_weight")):
                sp.dma_start(dst, a[name][0:P * TILES].rearrange("(p t) -> p t", p=P)).then_inc(s("in"), 16)
            sp.wait_ge(s("in"), 48)

        @block.vector
        def _(dve):
            nc.vector.memset(m.src_low[:, TILES:TILES + K], -1.0)
            nc.vector.memset(m.dst_i[:, TILES:TILES + K], 0)
            dve.wait_ge(s("in"), 48)
            nc.vector.tensor_scalar(m.dst_i[:, 0:TILES], m.dst_i[:, 0:TILES], N - 1, None, ALU.min)
            nc.vector.tensor_scalar(low_i, src_i, P - 1, None, ALU.bitwise_and).then_inc(s("v"), 1)
            nc.vector.tensor_scalar(blk_i, src_i, P.bit_length() - 1, None, ALU.arith_shift_right
                                    ).then_inc(s("v"), 1)
            dve.wait_ge(s("v"), 2)
            nc.vector.tensor_copy(m.src_low[:, 0:TILES], low_i)
            nc.vector.tensor_copy(m.src_blk[:, :], blk_i)


def smoothing_walk(nc, m, name, source):
    wide = NB * D
    turns = TILES // (K * RING)
    with ExitStack() as ctx:
        s = Stage(nc, f"put_{name}")
        block = ctx.enter_context(nc.Block())

        @block.sync
        def _(sp):
            sp.dma_start(m.table_d[name].rearrange("(b p) d -> p b d", p=P), source[:, :, :]).then_inc(s("out"), 16)
            sp.wait_ge(s("out"), 16)

    def rhs(k):
        return m.big[:, k * wide:(k + 1) * wide]

    with ExitStack() as ctx:
        s = Stage(nc, f"smooth_{name}")
        block = ctx.enter_context(nc.Block())

        @block.gpsimd
        def _(pool):
            gather(nc, m, s, pool, m.table_d[name], D, s("scaled"), index=m.dst_i, tiles=TILES)

        @block.vector
        def _(dve):
            def prepare(i, u, g, slot):
                half = slot % 2
                nc.vector.tensor_tensor(
                    m.oh[:, slot, :, :], m.iota_row[:, :].unsqueeze(1).to_broadcast([P, K, P]),
                    m.src_low[:, bass.ds(g * K, K)].unsqueeze(2).to_broadcast([P, K, P]),
                    ALU.is_equal).then_inc(s("one_hot"), 1)
                nc.vector.tensor_tensor(
                    m.sblk[:, half, :, :], m.iota_row[:, 0:NB].unsqueeze(1).to_broadcast([P, K, NB]),
                    m.src_blk[:, bass.ds(g * K, K)].unsqueeze(2).to_broadcast([P, K, NB]),
                    ALU.is_equal).then_inc(s("blk_hot"), 1)
                dve.wait_ge(s(f"rows{slot}"), 16 * K * (i + 1 if u < RING - 1 else i + 2))
                nc.vector.tensor_tensor(m.lx[:, half, :, :], m.gx[:, slot, :, 0:D],
                                        m.w_e[:, bass.ds(g * K, K)].unsqueeze(2).to_broadcast([P, K, D]), ALU.mult
                                        ).then_inc(s("scaled"), 1)

            def products(g, half):
                dve.wait_ge(s("blk_hot"), g + 1)
                dve.wait_ge(s("scaled"), g + 1)
                for k in range(K):
                    need(dve, s("added"), K * (g - 1) + k + 1)
                    nc.vector.tensor_tensor(
                        rhs(k).rearrange("p (b d) -> p b d", b=NB),
                        m.sblk[:, half, k, :].unsqueeze(2).to_broadcast([P, NB, D]),
                        m.lx[:, half, k, :].unsqueeze(1).to_broadcast([P, NB, D]), ALU.mult).then_inc(s("rhs"), 1)

            def body(i, u):
                g = i * RING + u
                products(g, u % 2)
                need(dve, s("rhs"), K * g)
                prepare(i, u, g + 1, (u + 1) % RING)
            nc.vector.memset(m.zeros[:, :], 0.0).then_inc(s("zeros"), 1)
            prepare(-1, RING - 1, 0, 0)
            groups(dve, body, turns - 1)
            for u in range(RING):
                g = (turns - 1) * RING + u
                if u < RING - 1:
                    body(turns - 1, u)
                else:
                    products(g, u % 2)
            dve.wait_ge(s("total"), 1)
            nc.vector.tensor_copy(m.Y[:, :, :].rearrange("p b d -> p (b d)")[:, 0:512], m.psA[:, 0, 0:512])
            nc.vector.tensor_copy(m.Y[:, :, :].rearrange("p b d -> p (b d)")[:, 512:wide], m.psA[:, 0, 512:wide])

        @block.tensor
        def _(pe):
            cols = ((0, 512), (512, wide))
            pe.wait_ge(s("zeros"), 1)
            for lo, hi in cols:
                nc.tensor.matmul(m.psA[:, 0, lo:hi], m.zeros[:, 0:P], m.zeros[:, 0:hi - lo], start=True, stop=False)

            def body(i, u):
                g = i * RING + u
                pe.wait_ge(s("one_hot"), g + 1)
                for k in range(K):
                    pe.wait_ge(s("rhs"), K * g + k + 1)
                    for lo, hi in cols:
                        ins = nc.tensor.matmul(m.psA[:, 0, lo:hi], m.oh[:, u, k, :], rhs(k)[:, lo:hi],
                                               start=False, stop=False)
                    ins.then_inc(s("added"), 1)
            groups(pe, body, turns)
            for lo, hi in cols:
                ins = nc.tensor.matmul(m.psA[:, 0, lo:hi], m.zeros[:, 0:P], m.zeros[:, 0:hi - lo], start=False,
                                       stop=True)
            ins.then_inc(s("total"), 1)


def smoothing(nc, m, a):
    edge_tiles(nc, m, a)
    smoothing_walk(nc, m, "s0", m.X)
    smoothing_walk(nc, m, "s1", m.Y)
    smoothing_walk(nc, m, "s2", m.Y)
    normalised(nc, m, "s", (m.X, m.Y))


def self_logits(nc, m, l):
    xl = m.big[:, 0:NB * TAB3].rearrange("p (b w) -> p b w", b=NB)
    steps = [range(b, min(b + 4, NB)) for b in range(0, NB, 4)]
    with ExitStack() as ctx:
        s = Stage(nc, f"self{l}")
        block = ctx.enter_context(nc.Block())

        def part(n):
            return m.work[:, n % 2, 0:len(steps[n]) * W3].rearrange("p (b w) -> p b w", w=W3)

        @block.vector
        def _(dve):
            def reduce(n):
                bs = steps[n]
                dve.wait_ge(s("summed"), n + 1)
                nc.vector.scalar_tensor_tensor(out=part(n), in0=part(n), scalar=0.2, in1=part(n), op0=ALU.mult,
                                               op1=ALU.max).then_inc(s("leaky"), 1)
                dve.wait_ge(s("leaky"), n + 1)
                nc.vector.tensor_tensor(part(n), part(n), m.att3[:, l, :].unsqueeze(1)
                                        .to_broadcast([P, len(bs), W3]), ALU.mult).then_inc(s("weighted"), 1)
                dve.wait_ge(s("weighted"), n + 1)
                nc.vector.tensor_reduce(m.self3[:, bs[0]:bs[-1] + 1, :].rearrange("p b h -> p (b h)"),
                                        part(n).rearrange("p b (h c) -> p (b h) c", c=D), AX.X, ALU.add
                                        ).then_inc(s("logits"), 1)
            for n, bs in enumerate(steps):
                need(dve, s("logits"), n - 1)
                nc.vector.tensor_tensor(part(n), xl[:, bs[0]:bs[-1] + 1, 0:W3],
                                        m.R[:, bs[0]:bs[-1] + 1, 0:W3], ALU.add
                                        ).then_inc(s("summed"), 1)
                if n:
                    reduce(n - 1)
            reduce(len(steps) - 1)


def attention_out(nc, m, l):
    acc = m.big[:, 0:NB * ACC3].rearrange("p (b w) -> p b w", b=NB)
    sums = acc[:, :, 0:W3].rearrange("p b (h c) -> p b h c", h=H3)
    own = m.big[:, NB * ACC3:NB * (ACC3 + W3)].rearrange("p (b h c) -> p b h c", b=NB, h=H3)
    den, top, flag = acc[:, :, W3:W3 + H3], acc[:, :, W3 + H3:W3 + 2 * H3], acc[:, :, ACC3 - 1:ACC3]
    most, e_self, e_edge, total, none = (m.small[:, n, :, :] for n in range(5))
    wide = [P, NB, H3, D]
    with ExitStack() as ctx:
        s = Stage(nc, f"out_g{l}")
        block = ctx.enter_context(nc.Block())

        @block.vector
        def _(dve):
            n = [0]

            def step(ins):
                n[0] += 1
                ins.then_inc(s("v"), 1)
                dve.wait_ge(s("v"), n[0])
            step(nc.vector.tensor_scalar(none, flag.to_broadcast([P, NB, H3]), -1.0, BIG, ALU.add, ALU.mult))
            step(nc.vector.tensor_tensor(top, top, none, ALU.add))
            step(nc.vector.tensor_tensor(most, top, m.self3[:, :, :], ALU.max))
            step(nc.vector.tensor_tensor(e_self, m.self3[:, :, :], most, ALU.subtract))
            step(nc.vector.tensor_tensor(e_edge, top, most, ALU.subtract))
            dve.sem_inc(s("shifted"), 1)
            dve.wait_ge(s("exp"), 2)
            step(nc.vector.tensor_tensor(total, den, e_edge, ALU.mult))
            step(nc.vector.tensor_tensor(total, total, e_self, ALU.add))
            step(nc.vector.tensor_scalar(total, total, 1e-16, None, ALU.add))
            step(nc.vector.reciprocal(total, total))
            nc.vector.tensor_tensor(e_self, e_self, total, ALU.mult)
            step(nc.vector.tensor_tensor(e_edge, e_edge, total, ALU.mult))
            step(nc.vector.tensor_tensor(sums, sums, e_edge.unsqueeze(3).to_broadcast(wide), ALU.mult))
            step(nc.vector.tensor_tensor(own, m.X[:, :, :].unsqueeze(2).to_broadcast(wide),
                                         e_self.unsqueeze(3).to_broadcast(wide), ALU.mult))
            step(nc.vector.tensor_tensor(sums, sums, own, ALU.add))
            dve.sem_inc(s("sums"), 1)
            for b in range(NB):
                dve.wait_ge(s("made"), b + 1)
                nc.vector.tensor_copy(m.Z[:, b, :], m.psC[:, b % 2, 0:D]).then_inc(s("z"), 1)

        @block.scalar
        def _(act):
            act.wait_ge(s("shifted"), 1)
            nc.scalar.activation(e_self, e_self, ACT.Exp).then_inc(s("exp"), 1)
            nc.scalar.activation(e_edge, e_edge, ACT.Exp).then_inc(s("exp"), 1)
            for b in range(NB):
                act.wait_ge(s("turned"), b + 1)
                need(act, s("made"), b - 1)
                nc.scalar.copy(m.work[:, b % 2, 0:W3], m.psT[:, b % 2, 0:W3]).then_inc(s("copied"), 1)

        @block.tensor
        def _(pe):
            def turn(b):
                need(pe, s("copied"), b - 1)
                nc.tensor.transpose(m.psT[:, b % 2, 0:P], acc[:, b, 0:P], m.ident[:, :])
                nc.tensor.transpose(m.psT[:, b % 2, P:2 * P], acc[:, b, P:2 * P], m.ident[:, :]
                                    ).then_inc(s("turned"), 1)
            pe.wait_ge(s("sums"), 1)
            turn(0)
            for b in range(NB):
                if b + 1 < NB:
                    turn(b + 1)
                pe.wait_ge(s("copied"), b + 1)
                need(pe, s("z"), b - 1)
                to = m.psC[:, b % 2, 0:D]
                for q in range(2):
                    nc.tensor.matmul(to, m.work[:, b % 2, q * P:(q + 1) * P], m.w3o[:, l, q, :], start=(q == 0),
                                     stop=False)
                nc.tensor.matmul(to, m.ones[0:1, :], m.brow[:, l, W3:W3 + D], start=False, stop=True
                                 ).then_inc(s("made"), 1)


def batch_normalised(nc, m, l, tag, leaky):
    mean, var, scale = (m.bnv[:, n, :] for n in range(3))
    wide = [P, NB, D]
    with ExitStack() as ctx:
        s = Stage(nc, f"bn{tag}")
        block = ctx.enter_context(nc.Block())

        def over_nodes(t):
            return t.unsqueeze(1).to_broadcast(wide)

        @block.vector
        def _(dve):
            n = [0]

            def step(ins):
                n[0] += 1
                ins.then_inc(s("v"), 1)
                dve.wait_ge(s("v"), n[0])
            if leaky:
                step(nc.vector.scalar_tensor_tensor(out=m.Z[:, :, :], in0=m.Z[:, :, :], scalar=0.01,
                                                    in1=m.Z[:, :, :], op0=ALU.mult, op1=ALU.max))
            step(nc.vector.tensor_tensor(m.X[:, :, :], m.Z[:, :, :], m.X[:, :, :], ALU.add))
            dve.sem_inc(s("ready"), 1)
            dve.wait_ge(s("sums"), 1)
            step(nc.vector.tensor_scalar(mean, m.psC[:, 0, 0:D], 1.0 / N, None, ALU.mult))
            step(nc.vector.tensor_tensor(m.X[:, :, :], m.X[:, :, :], over_nodes(mean), ALU.subtract))
            step(nc.vector.tensor_tensor(m.Z[:, :, :], m.X[:, :, :], m.X[:, :, :], ALU.mult))
            dve.sem_inc(s("ready"), 1)
            dve.wait_ge(s("root"), 1)
            step(nc.vector.reciprocal(scale, var))
            step(nc.vector.tensor_tensor(scale, scale, m.bn[:, l, 0, :], ALU.mult))
            step(nc.vector.tensor_tensor(m.X[:, :, :], m.X[:, :, :], over_nodes(scale), ALU.mult))
            nc.vector.tensor_tensor(m.X[:, :, :], m.X[:, :, :], over_nodes(m.bn[:, l, 1, :]), ALU.add)

        @block.tensor
        def _(pe):
            for n, t in enumerate((m.X, m.Z)):
                pe.wait_ge(s("ready"), n + 1)
                for b in range(NB):
                    rows = P if b < NB - 1 else TAIL
                    ins = nc.tensor.matmul(m.psC[:, n, 0:D], m.ones[0:rows, :], t[0:rows, b, :], start=(b == 0),
                                           stop=(b == NB - 1))
                ins.then_inc(s("sums"), 1)

        @block.scalar
        def _(act):
            act.wait_ge(s("sums"), 2)
            nc.scalar.activation(var, m.psC[:, 1, 0:D], ACT.Sqrt, bias=m.eps[:, 0:1], scale=1.0 / N
                                 ).then_inc(s("root"), 1)


def attention(nc, m):
    with ExitStack() as ctx:
        block = ctx.enter_context(nc.Block())

        @block.vector
        def _(dve):
            nc.vector.tensor_copy(m.Y[:, :, :], m.X[:, :, :])
    for l in range(3):
        name = f"g{l}"
        with nc.cleanup_on_exit():
            transposed(nc, m, name)
            tables(nc, m, name, m.w3[:, l, :], True, 2 * W3,
                   lambda o, ps: (nc.scalar.copy(o[:, 0:W3], ps[:, 0:W3]),
                                  nc.scalar.copy(o[:, W3 + D:TAB3], ps[:, 2 * W3 + H3:2 * W3 + 2 * H3]))[1],
                   lambda b, ps: nc.vector.tensor_copy(m.R[:, b, :], ps[:, W3:2 * W3 + H3]),
                   linear=m.w3l[:, l, :])
            self_logits(nc, m, l)
            logits(nc, m, name, H3, W3, l)
            softmax_parts(nc, m, name, H3)
            weighted_sums(nc, m, name, H3, ACC3)
            attention_out(nc, m, l)
            batch_normalised(nc, m, l, name, l < 2)
    normalised(nc, m, "g", (m.X, m.Y))


def transformer(nc, m):
    transposed(nc, m, "t")
    tables(nc, m, "t", m.w0[:, :], False, 3 * D,
           lambda o, ps: nc.scalar.copy(o, ps[:, 0:2 * D]),
           lambda b, ps: nc.vector.tensor_scalar(m.R[:, b, 0:D], ps[:, 2 * D:3 * D], (D // H0) ** -0.5, None,
                                                 ALU.mult))
    logits(nc, m, "t", H0, D, None)
    softmax_parts(nc, m, "t", H0)
    weighted_sums(nc, m, "t", H0, ACC0)
    transformer_out(nc, m)
    normalised(nc, m, "t", (m.X, m.X, m.Y))


def program(nc, a, out):
    with ExitStack() as ctx:
        m = allocate(nc, ctx)
        with nc.cleanup_on_exit():
            constants(nc, m, a)
            cut(nc, m, a)
        with nc.cleanup_on_exit():
            transformer(nc, m)
        with nc.cleanup_on_exit():
            relational(nc, m)
        with nc.cleanup_on_exit():
            smoothing(nc, m, a)
        attention(nc, m)
        store(nc, m, out)


def store(nc, m, out):
    with ExitStack() as ctx:
        s = Stage(nc, "store")
        block = ctx.enter_context(nc.Block())

        @block.sync
        def _(sp):
            sp.dma_start(out[0:(NB - 1) * P, :].rearrange("(b p) d -> p b d", p=P), m.X[:, 0:NB - 1, :]
                         ).then_inc(s("out"), 16)
            sp.dma_start(out[(NB - 1) * P:N, :], m.X[0:TAIL, NB - 1, :]).then_inc(s("out"), 16)
            sp.wait_ge(s("out"), 32)



_INS = ["x", "src", "dst", "edge_type_86", "edge_weight", "L0_gnn_Wq", "L0_gnn_Wk", "L0_gnn_Wv", "L0_gnn_Wo",
        "L1_gnn_weight", "L1_gnn_w_comp", "L1_gnn_self_loop_weight", "L1_gnn_A1_w", "L1_gnn_A1_b", "L1_gnn_A2_w",
        "L1_gnn_A2_b", "L1_gnn_rel_emb", "L3_gnn_Wl", "L3_gnn_bl", "L3_gnn_Wr", "L3_gnn_br", "L3_gnn_att",
        "L3_gnn_conv_bias", "L3_gnn_bn_gamma", "L3_gnn_bn_beta"]
_PAD = {"src": 0, "dst": 1 << 20, "edge_type_86": 0, "edge_weight": 0}


def kernel(**inputs):
    import numpy as _np
    import concourse.bacc as _bacc
    from concourse import mybir as _mybir
    from concourse.bass_utils import run_bass_kernel_spmd as _run

    nc = _bacc.Bacc("TRN2", target_bir_lowering=False, num_devices=1)
    arrays, args = {}, {}
    for name in _INS:
        x = _np.ascontiguousarray(inputs[name])
        if name in _PAD:
            x = _np.concatenate([x, _np.full(GE, _PAD[name], x.dtype)])
        arrays[f"in_{name}_dram"] = x
        args[name] = nc.dram_tensor(f"in_{name}_dram", x.shape, _mybir.dt.from_np(x.dtype), kind="ExternalInput").ap()
    out = nc.dram_tensor("out_0_dram", (N, D), F32, kind="ExternalOutput").ap()
    program(nc, args, out)
    r = _run(nc, [arrays], core_ids=[0])
    return r.results[0]["out_0_dram"]
```

```python
from contextlib import ExitStack

import concourse.bass as bass
from concourse import mybir

F32 = mybir.dt.float32
BF16 = mybir.dt.bfloat16
F16 = mybir.dt.float16
I32 = mybir.dt.int32
U32 = mybir.dt.uint32
ALU = mybir.AluOpType
ACT = mybir.ActivationFunctionType
AX = mybir.AxisListType

P = 128
D = 32
N, E = 3125, 100000
K = 4
GE = K * P
NB = -(-N // P)
NP = NB * P
TAIL = N - (NB - 1) * P
RING = 4
G = -(-((E + NB * (GE - 1)) // GE) // RING) * RING
SL = G * GE
RUN = SL // P
EP = 125
EF = E // EP
NREL, NBASE = 86, 16
Q = 4
QUADS = -(-N // Q)
QP = NP // Q
TILES = -(-E // (P * K * RING)) * K * RING
TYPE_W = D + NBASE
H0 = 4
H3 = 8
W3 = H3 * D
TAB3 = W3 + D + H3
ROW3 = W3 + H3
LEAK = 0.2
PE_ADDS = 1
ACC0 = D + H0
ACC1 = NBASE * D + D
ACC3 = W3 + 2 * H3 + 1
BIG = 1e30
LN_EPS = 1e-5
assert EP * EF == E and RUN * P == SL and EF == RUN - 80


class Stage:

    def __init__(self, nc, tag):
        self.nc, self.tag, self.made = nc, tag, {}

    def __call__(self, name):
        if name not in self.made:
            self.made[name] = self.nc.alloc_semaphore(name=f"{self.tag}_{name}")
        return self.made[name]


def need(eng, sem, value):
    if not isinstance(value, int) or value > 0:
        eng.wait_ge(sem, value)


def groups(eng, body, turns=G // RING):
    for i in range(2):
        for u in range(RING):
            body(i, u)
    with eng.Fori(2, turns, 1) as i:
        for u in range(RING):
            body(i, u)


class Mem:
    pass


def allocate(nc, ctx):
    m = Mem()

    def sb(name, shape, dt=F32):
        t = ctx.enter_context(nc.sbuf_tensor(name, shape, dt))
        return t

    m.ident = sb("ident", [P, P])
    m.ident_b = sb("ident_b", [P, P], BF16)
    m.iota_b = sb("iota_b", [P, P], BF16)
    m.iota_row = sb("iota_row", [P, P])
    m.ones = sb("ones", [P, P])
    m.upper = sb("upper", [NB, NB])
    m.src_i = sb("src_i", [P, G + 2 * RING, K], I32)
    m.rel = sb("rel", [P, G + 3, K])
    m.et_f = sb("et_f", [P, G + 2, K])
    m.first_t = sb("first_t", [P, G, K])
    m.last_t = sb("last_t", [P, G, K])
    m.new_seg = sb("new_seg", [P, RUN])
    m.end_seg = sb("end_seg", [P, RUN])
    m.blk_i = sb("blk_i", [1, G + 1], I32)
    m.X = sb("X", [P, NB, D])
    m.Y = sb("Y", [P, NB, D])
    m.Z = sb("Z", [P, NB, D])
    m.XT = sb("XT", [D + 1, NP])
    rows = sb("rows", [P, max(NB * ROW3, G * K * H3)])
    m.rows = rows
    m.probs = rows[:, 0:G * K * H3]
    m.R = rows[:, 0:NB * ROW3].rearrange("p (b w) -> p b w", b=NB)
    m.Rr = rows[:, 0:NB * D].rearrange("p (b w) -> p b w", b=NB)
    at = NB * D
    m.type_in = rows[:, at:at + RING * K * TYPE_W].rearrange("p (n k w) -> p n k w", n=RING, k=K)
    at += RING * K * TYPE_W
    m.node_b = rows[:, at:at + K * P].bitcast(BF16).rearrange("p (n k q) -> p n k q", n=2, k=K)
    m.big = sb("big", [P, 2 * RUN * H3])
    m.maxima = m.big[:, NB * ACC3:NB * ACC3 + G * K * H3]
    m.cols_hot = m.big[:, 0:K * QP].bitcast(BF16).rearrange("p (n k c) -> p n k c", n=2, k=K)
    at = K * QP
    m.quad_w = m.big[:, at:at + TILES * Q].rearrange("p (t q) -> p t q", q=Q)
    at += TILES * Q
    m.dst_i = m.big[:, at:at + TILES + 2 * RING * K].bitcast(I32)
    at += TILES + 2 * RING * K
    m.src_col = m.big[:, at:at + TILES]
    at += TILES
    m.tile_tmp = m.big[:, at:at + 4 * TILES].rearrange("p (n t) -> p n t", n=4)
    m.gx = sb("gx", [P, RING, K, TAB3])
    m.gi = sb("gi", [P, 2, RING * K], I32)
    one_hots = sb("oh", [P, RING * K * P])
    m.oh = one_hots[:, :].rearrange("p (n k q) -> p n k q", n=RING, k=K)
    m.oh_b = one_hots[:, 0:RING * K * P // 2].bitcast(BF16).rearrange("p (n k q) -> p n k q", n=RING, k=K)
    m.ohT = sb("ohT", [P, 2, K * P])
    m.work = sb("work", [P, 2, K * ACC1])
    m.red = sb("red", [P, 2, K * H3])
    m.lin = sb("lin", [P, 2, K * H3])
    m.lg = sb("lg", [P, RING, K * H3])
    m.xl = sb("xl", [P, RING, K, D])
    m.a1 = sb("a1", [P, 2, 4, K])
    m.typ = m.work[:, :, 512:512 + K * NREL // 2].bitcast(BF16).rearrange("p n (k r) -> p n k r", k=K)
    m.typT = m.work[0:NREL, :, 1024:1024 + K * P]
    m.type_out = m.work[:, :, 1536:1536 + K * TYPE_W]
    m.zeros = m.ohT[:, 0, :]
    m.iota_h = m.ohT[:, 1, 0:QP // 2].bitcast(F16)
    wide = K * Q * D
    m.msg = m.work[:, :, 0:wide]
    m.rest = m.work[:, :, wide:2 * wide]
    m.parts = m.work[:, :, 2 * wide:2 * wide + 3 * wide // 2].bitcast(BF16).rearrange(
        "p n (j w) -> p n j w", j=3)
    m.ac = sb("ac", [P, 2, K, NBASE])
    m.lx = sb("lx", [P, 2, K, D])
    m.self3 = sb("self3", [P, NB, H3])
    m.small = sb("small", [P, 5, NB, H3])
    m.line = sb("line", [P, 4, NB])
    m.c8 = sb("c8", [P, 6, H3])
    m.r8 = sb("r8", [H3, 4, P])
    m.bnv = sb("bnv", [P, 4, D])
    m.w3 = sb("w3", [D + 1, 3, 2, ROW3])
    m.w3o = sb("w3o", [P, 3, 2, D])
    m.att3 = sb("att3", [P, 3, W3])
    m.bn = sb("bn", [P, 3, 2, D])
    m.bias3 = sb("bias3", [P, 3, D])
    m.node_rows = sb("node_rows", [P, 1])
    m.sum_in = sb("sum_in", [P, D])
    m.brow = m.work[0:1, 0, 0:3 * (W3 + 2 * D)].rearrange("p (l w) -> p l w", l=3)
    m.w0 = sb("w0", [D, 3 * D])
    m.wo0 = sb("wo0", [D, D])
    m.w1 = sb("w1", [D + 1, 2 * D])
    m.w1b = sb("w1b", [P, 4, D])
    m.w1s = sb("w1s", [D, D])
    m.relt = sb("relt", [NREL, D + NBASE])
    m.col = sb("col", [P, 8])
    m.coli = sb("coli", [P, 1], I32)
    m.eps = sb("eps", [P, 1])
    m.guard = sb("guard", [1, 1])
    m.psA = ctx.enter_context(nc.psum_tensor("psA", [P, 2, 1024], F32))
    m.psT = ctx.enter_context(nc.psum_tensor("psT", [P, 2, 512], F32))
    m.psC = ctx.enter_context(nc.psum_tensor("psC", [P, 2, 512], F32))

    def dram(name, shape):
        return nc.dram_tensor(name, shape, F32, kind="Internal").ap()

    m.key_d = dram("key_d", [SL + 2])
    m.first_d = dram("first_d", [SL])
    m.last_d = dram("last_d", [SL])
    m.type_d = dram("type_d", [SL, TYPE_W])
    m.table_d = {n: dram(f"table_{n}", [NP, w]) for n, w in
                 (("t", 2 * D), ("r", 2 * D), ("s0", D), ("s1", D), ("s2", D), ("s3", D), ("g0", TAB3), ("g1", TAB3), ("g2", TAB3))}
    soft = (("t", H0), ("g0", H3), ("g1", H3), ("g2", H3))
    m.xs_d = {n: dram(f"xs_{n}", [SL, D]) for n, _ in soft}
    m.logit_d = {n: dram(f"logit_{n}", [SL, h]) for n, h in soft}
    m.prob_d = {n: dram(f"prob_{n}", [SL, h]) for n, h in soft}
    m.max_d = {n: dram(f"max_{n}", [SL, h]) for n, h in soft}
    return m



def edge_counts(m):
    b = m.big
    dst_i, dst_f = b[0:EP, 0:EF].bitcast(I32), b[0:EP, EF:2 * EF]
    below = [b[0:EP, (2 + n) * EF:(3 + n) * EF] for n in range(2)]
    return dst_i, dst_f, below, b[0:EP, 4 * EF:4 * EF + NB + 1]


def constants(nc, m, a):
    with ExitStack() as ctx:
        s = Stage(nc, "const")
        block = ctx.enter_context(nc.Block())
        LOADS = []
        bias = D
        LOADS.append((m.X[:, 0:NB - 1, :], a["x"][0:(NB - 1) * P, :].rearrange("(b p) d -> p b d", p=P)))
        LOADS.append((m.X[0:TAIL, NB - 1, :], a["x"][(NB - 1) * P:N, :]))
        for n, w in enumerate(("L0_gnn_Wk", "L0_gnn_Wv", "L0_gnn_Wq")):
            LOADS.append((m.w0[:, n * D:(n + 1) * D], a[w]))
        LOADS.append((m.wo0[:, :], a["L0_gnn_Wo"]))
        for n, (w, b) in enumerate((("L1_gnn_A1_w", "L1_gnn_A1_b"), ("L1_gnn_A2_w", "L1_gnn_A2_b"))):
            LOADS.append((m.w1[0:D, n * D:(n + 1) * D], a[w].rearrange("o i -> i o")))
            LOADS.append((m.w1[bias:bias + 1, n * D:(n + 1) * D], a[b].rearrange("(a o) -> a o", a=1)))
        LOADS.append((m.w1b[:, :, :], a["L1_gnn_weight"].rearrange("(t q) i o -> (q i) t o", q=4)))
        LOADS.append((m.w1s[:, :], a["L1_gnn_self_loop_weight"]))
        LOADS.append((m.relt[:, 0:D], a["L1_gnn_rel_emb"]))
        LOADS.append((m.relt[:, D:D + NBASE], a["L1_gnn_w_comp"]))
        for l in range(3):
            for n, (w, b) in enumerate((("L3_gnn_Wl", "L3_gnn_bl"), ("L3_gnn_Wr", "L3_gnn_br"))):
                LOADS.append((m.w3[0:D, l, n, 0:W3], a[w][l]))
                LOADS.append((m.w3[bias:bias + 1, l, n, 0:W3], a[b][l:l + 1]))
            for h in range(H3):
                LOADS.append((m.w3o[(h % 4) * D:(h % 4 + 1) * D, l, h // 4, :],
                              a["L3_gnn_Wl"][l, :, h * D:(h + 1) * D]))
            LOADS.append((m.att3[:, l, :], a["L3_gnn_att"][l].rearrange("(a h) c -> a (h c)", a=1).to_broadcast([P, W3])))
            for n, w in enumerate(("L3_gnn_bn_gamma", "L3_gnn_bn_beta")):
                LOADS.append((m.bn[:, l, n, :], a[w][l:l + 1].to_broadcast([P, D])))
            LOADS.append((m.brow[:, l, 0:W3], a["L3_gnn_bl"][l:l + 1]))
            LOADS.append((m.brow[:, l, W3:W3 + D], a["L3_gnn_conv_bias"][l:l + 1]))

        @block.vector
        def _(dve):
            nc.vector.memset(m.X[:, NB - 1, :], 0.0).then_inc(s("xzero"), 1)
            nc.vector.memset(m.ones[:, :], 1.0).then_inc(s("ones"), 1)
            nc.vector.memset(m.XT[D:D + 1, :], 1.0)
            nc.vector.memset(m.rel[:, G:G + 3, :], -1.0)
            nc.vector.memset(m.et_f[:, G:G + 2, :], -1.0)
            nc.vector.memset(m.eps[:, :], LN_EPS)
            nc.vector.memset(m.guard[:, :], -5.0)
            dve.wait_ge(s("dst"), 16)
            dst_i, dst_f, below, counts = edge_counts(m)
            nc.vector.tensor_copy(dst_f, dst_i).then_inc(s("dst_f"), 1)
            dve.wait_ge(s("dst_f"), 1)
            for j in range(NB + 1):
                need(dve, s("counts"), j - 1)
                nc.vector.tensor_scalar(below[j % 2], dst_f, float(j * P), None, ALU.is_lt).then_inc(s("below"), 1)
                if j:
                    dve.wait_ge(s("below"), j)
                    nc.vector.tensor_reduce(counts[:, j - 1:j], below[(j - 1) % 2], AX.X, ALU.add
                                            ).then_inc(s("counts"), 1)
            dve.wait_ge(s("below"), NB + 1)
            nc.vector.tensor_reduce(counts[:, NB:NB + 1], below[NB % 2], AX.X, ALU.add)
            dve.wait_ge(s("loads"), 16 * len(LOADS))
            weighted = m.rows[0:D + 1, 0:3 * 2 * W3].rearrange("p (l n w) -> p l n w", l=3, n=2)
            nc.vector.tensor_tensor(weighted, m.w3[:, :, :, 0:W3],
                                    m.att3[0:D + 1, :, :].unsqueeze(2).to_broadcast([D + 1, 3, 2, W3]), ALU.mult
                                    ).then_inc(s("weighted"), 1)
            dve.wait_ge(s("weighted"), 1)
            for n in range(2):
                nc.vector.tensor_reduce(m.w3[:, :, n, W3:ROW3],
                                        weighted[:, :, n, :].rearrange("p l (h c) -> p l h c", h=H3), AX.X, ALU.add
                                        ).then_inc(s("weighted"), 1)
            dve.wait_ge(s("weighted"), 3)
            nc.vector.tensor_scalar(m.w3[:, :, :, W3:ROW3], m.w3[:, :, :, W3:ROW3], LEAK, None, ALU.mult)
            nc.vector.tensor_scalar(m.w3o[:, :, :, :], m.w3o[:, :, :, :], 1.0 / H3, None, ALU.mult)
            nc.vector.tensor_reduce(m.brow[:, :, W3 + D:W3 + 2 * D],
                                    m.brow[:, :, 0:W3].rearrange("p l (h c) -> p l c h", h=H3), AX.X, ALU.add
                                    ).then_inc(s("brow"), 1)
            dve.wait_ge(s("brow"), 1)
            nc.vector.tensor_scalar(m.brow[:, :, 0:D], m.brow[:, :, W3 + D:W3 + 2 * D], 1.0 / H3, None,
                                    ALU.mult).then_inc(s("brow"), 1)
            dve.wait_ge(s("brow"), 2)
            nc.vector.tensor_tensor(m.brow[:, :, W3:W3 + D], m.brow[:, :, W3:W3 + D], m.brow[:, :, 0:D], ALU.add).then_inc(s("brow"), 1)
            dve.wait_ge(s("spread"), 1)
            nc.vector.tensor_copy(m.bias3[:, :, :], m.psC[:, 0, 0:3 * D].rearrange("p (l d) -> p l d", l=3))

        @block.tensor
        def _(pe):
            pe.wait_ge(s("ones"), 1)
            pe.wait_ge(s("brow"), 3)
            nc.tensor.matmul(m.psC[:, 0, 0:3 * D], m.ones[0:1, :], m.brow[:, :, W3:W3 + D], start=True, stop=True
                             ).then_inc(s("spread"), 1)

        @block.gpsimd
        def _(pool):
            pool.wait_ge(s("ones"), 1)
            nc.gpsimd.affine_select(out=m.ident[:, :], in_=m.ones[:, :], compare_op=ALU.is_equal, fill=0.0,
                                    base=0, pattern=[[-1, P]], channel_multiplier=1).then_inc(s("ident"), 1)
            nc.gpsimd.affine_select(out=m.upper[:, :], in_=m.ones[0:NB, 0:NB], compare_op=ALU.is_gt, fill=0.0,
                                    base=0, pattern=[[1, NB]], channel_multiplier=-1)
            nc.gpsimd.affine_select(out=m.node_rows[:, :], in_=m.ones[:, 0:1], compare_op=ALU.is_gt, fill=0.0,
                                    base=TAIL, pattern=[[0, 1]], channel_multiplier=-1)
            nc.gpsimd.iota(m.iota_row[:, :], [[1, P]], base=0, channel_multiplier=0,
                           allow_small_or_imprecise_dtypes=True).then_inc(s("iota"), 1)
            pool.wait_ge(s("ident"), 1)
            pool.wait_ge(s("iota"), 1)
            nc.gpsimd.tensor_copy(m.iota_b[:, :], m.iota_row[:, :])
            nc.gpsimd.tensor_copy(m.ident_b[:, :], m.ident[:, :])
            nc.gpsimd.memset(m.src_i[:, G:G + 2 * RING, :], 0)
            nc.gpsimd.memset(m.blk_i[:, G:G + 1], 0)

        @block.sync
        def _(sp):
            sp.dma_start(edge_counts(m)[0], a["dst"][0:E].rearrange("(p f) -> p f", p=EP)).then_inc(s("dst"), 16)
            sp.wait_ge(s("xzero"), 1)
            for n, (dst, src) in enumerate(LOADS):
                sp.dma_start(dst, src, allow_slow_non_contiguous=True).then_inc(s("loads"), 16)
            sp.wait_ge(s("loads"), 16 * len(LOADS))


def cut(nc, m, a):
    b = m.big
    counts = edge_counts(m)[3]
    at = 4 * EF + 32
    g_no, mask, val = (b[0:NB, at + n * G:at + (n + 1) * G] for n in range(3))
    at += 3 * G
    blk128 = b[:, at:at + G]
    row1 = b[0:1, at + G:at + 2 * G]
    row2 = b[0:1, at + 2 * G:at + 3 * G]
    start_i = b[0:1, at + 3 * G:at + 4 * G].bitcast(I32)
    at += 4 * G

    def slots(n, w=1):
        return b[:, at + n * G * K:at + (n + w) * G * K].rearrange("p (g k) -> p g k", k=w * K)
    slot_edges, slot_f, valid = slots(0, 3).bitcast(I32), slots(3), slots(4)
    slot_src, slot_dst, slot_et = (slot_edges.rearrange("p g (k n) -> p g k n", n=3)[:, :, :, n] for n in range(3))
    col = m.col
    first, nxt, t1, ng, g0, g1, off, num = (col[0:NB, n:n + 1] for n in range(8))
    bcol = b[0:NB, at + 5 * G * K:at + 5 * G * K + P]

    with ExitStack() as ctx:
        s = Stage(nc, "cut")
        block = ctx.enter_context(nc.Block())
        AT_ONCE = 11
        QUEUES = (("sp", (0, 3, 6, 9)), ("act", (1, 4, 7, 10)), ("pool", (2, 5, 8)))

        def loads(eng, queue):
            numbers = dict(QUEUES)[queue]
            eng.wait_ge(s("starts"), 1)
            with eng.Fori(0, G // AT_ONCE, 1) as i:
                gs = [i * AT_ONCE + n for n in numbers]
                starts = [eng.value_load(start_i[0:1, bass.ds(g, 1)], min_val=0, max_val=E) for g in gs]
                for g, start in zip(gs, starts):
                    eng.dma_start(slot_edges[:, bass.ds(g, 1), :].rearrange("p a w -> p (a w)"),
                                  a["edges"][bass.ds(start, GE), :].rearrange("(p k) n -> p (k n)", k=K)
                                  ).then_inc(s(f"slots_{queue}"), 16)

        @block.vector
        def _(dve):
            n = [0]

            def step(ins):
                n[0] += 1
                ins.then_inc(s("v"), 1)
                dve.wait_ge(s("v"), n[0])
            dve.wait_ge(s("sums"), 1)
            nc.vector.tensor_copy(first, m.psC[0:NB, 0, 0:1])
            step(nc.vector.tensor_copy(nxt, m.psC[0:NB, 0, 1:2]))
            step(nc.vector.tensor_tensor(t1, nxt, first, ALU.subtract))
            step(nc.vector.tensor_scalar(t1, t1, float(GE - 1), None, ALU.add))
            step(nc.vector.tensor_copy(m.coli[0:NB, :], t1))
            step(nc.vector.tensor_scalar(m.coli[0:NB, :], m.coli[0:NB, :], GE.bit_length() - 1, None,
                                         ALU.arith_shift_right))
            step(nc.vector.tensor_copy(ng, m.coli[0:NB, :]))
            dve.sem_inc(s("ng"), 1)
            dve.wait_ge(s("sums"), 2)
            step(nc.vector.tensor_copy(g0, m.psC[0:NB, 0, 2:3]))
            step(nc.vector.tensor_tensor(g1, g0, ng, ALU.add))
            step(nc.vector.tensor_scalar(off, g0, float(-GE), None, ALU.mult))
            step(nc.vector.tensor_tensor(off, off, first, ALU.add))
            dve.wait_ge(s("iota"), 1)
            step(nc.vector.tensor_scalar(mask, g_no, g1, None, ALU.is_lt))
            step(nc.vector.tensor_scalar(val, g_no, g0, None, ALU.is_ge))
            step(nc.vector.tensor_tensor(mask, mask, val, ALU.mult))
            step(nc.vector.tensor_scalar(val, g_no, float(GE), off, ALU.mult, ALU.add))
            step(nc.vector.tensor_tensor(val, val, mask, ALU.mult))
            step(nc.vector.tensor_scalar(bcol, m.ones[0:NB, :], num, None, ALU.mult))
            dve.sem_inc(s("masks"), 1)
            dve.wait_ge(s("sums"), 3)
            step(nc.vector.tensor_scalar(row1, m.psC[0:1, 0, G:2 * G], float(-E), float(E), ALU.mult, ALU.add))
            step(nc.vector.tensor_tensor(row1, row1, m.psC[0:1, 0, 0:G], ALU.add))
            nc.vector.tensor_copy(start_i, row1).then_inc(s("starts"), 1)
            step(nc.vector.tensor_copy(m.blk_i[:, 0:G], m.psC[0:1, 1, 0:G]))
            step(nc.vector.tensor_scalar(blk128, m.psC[:, 1, 0:G], float(P), None, ALU.mult))
            for queue, numbers in QUEUES:
                dve.wait_ge(s(f"slots_{queue}"), 16 * len(numbers) * (G // AT_ONCE))
            nc.vector.tensor_copy(m.src_i[:, 0:G, :], slot_src)
            nc.vector.tensor_copy(m.et_f[:, 0:G, :], slot_et)
            step(nc.vector.tensor_copy(slot_f, slot_dst))
            rel = m.rel[:, 0:G, :]
            step(nc.vector.tensor_tensor(rel, slot_f, blk128.unsqueeze(2).to_broadcast([P, G, K]), ALU.subtract))
            step(nc.vector.tensor_scalar(valid, rel, float(P), None, ALU.is_lt))
            step(nc.vector.tensor_scalar(slot_f, slot_f, 1.0, None, ALU.add))
            step(nc.vector.tensor_tensor(slot_f, slot_f, valid, ALU.mult))
            step(nc.vector.tensor_scalar(slot_f, slot_f, -1.0, None, ALU.add))
            dve.sem_inc(s("keys"), 1)

        @block.gpsimd
        def _(pool):
            nc.gpsimd.iota(g_no, [[1, G]], base=0, channel_multiplier=0, allow_small_or_imprecise_dtypes=True)
            nc.gpsimd.iota(num, [[0, 1]], base=0, channel_multiplier=1,
                           allow_small_or_imprecise_dtypes=True).then_inc(s("iota"), 1)
            loads(pool, "pool")

        @block.tensor
        def _(pe):
            nc.tensor.matmul(m.psC[0:NB, 0, 0:1], counts[:, 0:NB], m.ones[0:EP, 0:1], start=True, stop=True)
            nc.tensor.matmul(m.psC[0:NB, 0, 1:2], counts[:, 1:NB + 1], m.ones[0:EP, 0:1], start=True,
                             stop=True).then_inc(s("sums"), 1)
            pe.wait_ge(s("ng"), 1)
            nc.tensor.matmul(m.psC[0:NB, 0, 2:3], m.upper[:, :], ng, start=True, stop=True).then_inc(s("sums"), 1)
            pe.wait_ge(s("masks"), 1)
            nc.tensor.matmul(m.psC[0:1, 0, 0:G], m.ones[0:NB, 0:1], val, start=True, stop=True)
            nc.tensor.matmul(m.psC[0:1, 0, G:2 * G], m.ones[0:NB, 0:1], mask, start=True, stop=True)
            nc.tensor.matmul(m.psC[:, 1, 0:G], bcol, mask, start=True, stop=True).then_inc(s("sums"), 1)

        @block.sync
        def _(sp):
            loads(sp, "sp")
            sp.wait_ge(s("keys"), 1)
            sp.dma_start(m.key_d[1:SL + 1].rearrange("(g p k) -> p g k", p=P, k=K), slot_f).then_inc(s("out"), 16)
            sp.dma_start(m.key_d[0:1].rearrange("(a k) -> a k", a=1), m.guard[:, :]).then_inc(s("out"), 16)
            sp.dma_start(m.key_d[SL + 1:SL + 2].rearrange("(a k) -> a k", a=1), m.guard[:, :]).then_inc(s("out"), 16)
            sp.wait_ge(s("out"), 48)

        @block.scalar
        def _(act):
            loads(act, "act")

    prev, own, nxt_k, f1, f2 = (b[:, n * RUN:(n + 1) * RUN] for n in range(5))
    with ExitStack() as ctx:
        s = Stage(nc, "runs")
        block = ctx.enter_context(nc.Block())

        @block.sync
        def _(sp):
            for n, t in enumerate((prev, own, nxt_k)):
                sp.dma_start(t, m.key_d[n:n + SL].rearrange("(p f) -> p f", p=P)).then_inc(s("keys"), 16)
            sp.wait_ge(s("flags"), 1)
            for t, d in ((f1, m.first_d), (f2, m.last_d)):
                sp.dma_start(d.rearrange("(p f) -> p f", p=P), t).then_inc(s("out"), 16)
            sp.wait_ge(s("out"), 32)
            for t, d in ((m.first_t, m.first_d), (m.last_t, m.last_d)):
                sp.dma_start(t[:, :, :], d.rearrange("(g p k) -> p g k", p=P, k=K)).then_inc(s("in"), 16)
            sp.wait_ge(s("in"), 32)

        @block.vector
        def _(dve):
            dve.wait_ge(s("keys"), 48)
            nc.vector.tensor_tensor(f1, own, prev, ALU.not_equal)
            nc.vector.tensor_tensor(f2, own, nxt_k, ALU.not_equal).then_inc(s("flags"), 1)
            dve.wait_ge(s("flags"), 1)
            nc.vector.tensor_scalar(m.new_seg[:, :], f1, -BIG, None, ALU.mult)
            nc.vector.tensor_scalar(m.end_seg[:, :], f2, -BIG, None, ALU.mult)



def tables(nc, m, name, sources, dests, tab, side, layer=None):
    gat = layer is not None
    w = m.table_d[name].shape[1]
    out = m.big[:, 0:NB * w].rearrange("p (b w) -> p b w", b=NB)
    rows = sources.shape[0]
    steps = [range(b, min(b + 4, NB)) for b in range(0, NB, 4)]
    parts = 4
    ends = [(n + 1) * NB // parts for n in range(parts)]

    def bank(b, n):
        return m.psA[:, b % 2, n * 512:n * 512 + (sources, dests)[n].shape[1]]

    with ExitStack() as ctx:
        s = Stage(nc, f"tab_{name}")
        block = ctx.enter_context(nc.Block())

        @block.tensor
        def _(pe):
            def turn(n):
                need(pe, s("copied"), n - 1)
                for b in steps[n]:
                    at = (b - steps[n][0]) * P
                    ins = nc.tensor.transpose(m.psT[0:D, n % 2, at:at + P], m.X[:, b, :], m.ident[:, :])
                ins.then_inc(s("turned"), 1)
            turn(0)
            for b in range(NB):
                if b % 4 == 0 and b // 4 + 1 < len(steps):
                    turn(b // 4 + 1)
                pe.wait_ge(s("copied"), b // 4 + 1)
                for n, (weights, read) in enumerate(((sources, "tab"), (dests, "side"))):
                    need(pe, s(read), b - 1)
                    nc.tensor.matmul(bank(b, n), m.XT[0:rows, b * P:(b + 1) * P], weights, start=True,
                                     stop=True).then_inc(s(f"made_{read}"), 1)

        @block.scalar
        def _(act):
            def copy_turned(n):
                bs = steps[n]
                act.wait_ge(s("turned"), n + 1)
                nc.scalar.copy(m.XT[0:D, bs[0] * P:(bs[-1] + 1) * P], m.psT[0:D, n % 2, 0:len(bs) * P]
                               ).then_inc(s("copied"), 1)
            copy_turned(0)
            for b in range(NB):
                if b % 4 == 0 and b // 4 + 1 < len(steps):
                    copy_turned(b // 4 + 1)
                act.wait_ge(s("made_tab"), b + 1)
                tab(out[:, b, :], bank(b, 0)).then_inc(s("tab"), 1)
                if gat:
                    act.wait_ge(s("made_side"), b + 1)
                    side(b, bank(b, 1)).then_inc(s("side"), 1)

        @block.vector
        def _(dve):
            if w > W3 or name == "r":
                lo = W3 + H3 if w > W3 else 0
                nc.vector.tensor_copy(out[:, :, lo:lo + D], m.X[:, :, :]).then_inc(s("x"), 1)
            else:
                dve.sem_inc(s("x"), 1)
            if gat:
                self_logits(nc, m, s, dve, layer)
            for b in range(0 if gat else NB):
                dve.wait_ge(s("made_side"), b + 1)
                side(b, bank(b, 1)).then_inc(s("side"), 1)

        @block.sync
        def _(sp):
            view = m.table_d[name].rearrange("(b p) w -> p b w", p=P)
            sp.wait_ge(s("x"), 1)
            for lo, hi in zip([0] + ends, ends):
                sp.wait_ge(s("tab"), hi)
                sp.dma_start(view[:, lo:hi, :], out[:, lo:hi, :]).then_inc(s("out"), 16)
            sp.wait_ge(s("out"), 16 * parts)


def normalised(nc, m, tag, addends):
    with ExitStack() as ctx:
        s = Stage(nc, f"ln_{tag}")
        block = ctx.enter_context(nc.Block())
        mean, var = m.line[:, 0, :], m.line[:, 1, :]
        wide = [P, NB, D]

        @block.vector
        def _(dve):
            n = [0]

            def step(ins):
                n[0] += 1
                ins.then_inc(s("v"), 1)
                dve.wait_ge(s("v"), n[0])
            total = addends[0]
            for t in addends[1:]:
                step(nc.vector.tensor_tensor(m.Z[:, :, :], total[:, :, :], t[:, :, :], ALU.add))
                total = m.Z
            step(nc.vector.tensor_reduce(mean, m.Z[:, :, :], AX.X, ALU.add))
            step(nc.vector.tensor_scalar(mean, mean, 1.0 / D, None, ALU.mult))
            step(nc.vector.tensor_tensor(m.Z[:, :, :], m.Z[:, :, :], mean.unsqueeze(2).to_broadcast(wide),
                                         ALU.subtract))
            step(nc.vector.tensor_tensor(m.X[:, :, :], m.Z[:, :, :], m.Z[:, :, :], ALU.mult))
            step(nc.vector.tensor_reduce(var, m.X[:, :, :], AX.X, ALU.add))
            dve.sem_inc(s("var"), 1)
            dve.wait_ge(s("root"), 1)
            step(nc.vector.reciprocal(var, var))
            nc.vector.tensor_tensor(m.X[:, :, :], m.Z[:, :, :], var.unsqueeze(2).to_broadcast(wide), ALU.mult)

        @block.scalar
        def _(act):
            act.wait_ge(s("var"), 1)
            nc.scalar.activation(var, var, ACT.Sqrt, bias=m.eps[:, 0:1], scale=1.0 / D).then_inc(s("root"), 1)



def gather(nc, m, s, pool, table, w, used, stored=False, index=None, tiles=G * K):
    def indices(i, odd):
        at = m.src_i[:, bass.ds(i * RING, RING), :].rearrange("p g k -> p (g k)") if index is None else \
            index[:, bass.ds(i * RING * K, RING * K)]
        nc.gpsimd.tensor_copy(m.gi[:, odd, :], at).then_inc(s("indices"), 1)

    def turn(i, odd):
        for u in range(RING):
            g = i * RING + u
            if u == 1:
                for v in range(RING):
                    need(pool, s(f"rows{v}"), 16 * K * i)
                indices(i + 1, 1 - odd)
            need(pool, used, g - RING + 1)
            if stored:
                need(pool, s(f"xs{u}"), 16 * i)
            pool.wait_ge(s("indices"), i + 1)
            pool.sem_inc(s("ticket"), 1)
            for k in range(K):
                pool.indirect_dma_start(m.gx[:, u, k, 0:w], None, table,
                                        bass.IndirectOffsetOnAxis(
                                            m.gi[:, odd, u * K + k:u * K + k + 1].bitcast(U32), 0)
                                        ).then_inc(s(f"rows{u}"), 16)
    turns = tiles // (K * RING)
    assert turns % 2 == 1
    indices(0, 0)
    for i in range(3):
        turn(i, i % 2)
    with pool.Fori(3, turns, 2) as i:
        turn(i, 1)
        turn(i + 1, 0)


def one_hot(nc, m, g, slot, half_width=False):
    to, pattern = (m.oh_b, m.iota_b) if half_width else (m.oh, m.iota_row)
    return nc.vector.tensor_tensor(
        to[:, slot, :, :], pattern[:, :].unsqueeze(1).to_broadcast([P, K, P]),
        m.rel[:, bass.ds(g, 1), :].rearrange("p a k -> p (a k)").unsqueeze(2).to_broadcast([P, K, P]),
        ALU.is_equal)


def block_of(m, dve, g):
    return dve.value_load(m.blk_i[0:1, bass.ds(g, 1)], min_val=0, max_val=NB - 1)


def add_up(nc, m, dve, g, w, ps, s, blk=None):
    if blk is None:
        blk = block_of(m, dve, g)
    dve.wait_ge(s("added"), g + 1)
    need(dve, s("acc"), g + 1)
    acc = m.big[:, 0:NB * w].rearrange("p (b w) -> p b w", b=NB)[:, bass.ds(blk, 1), :].rearrange(
        "p a w -> p (a w)")
    if len(ps.shape) == 3:
        acc = acc.rearrange("p (n w) -> p n w", n=2)
    return nc.vector.tensor_tensor(acc, acc, ps, ALU.add)


def logits(nc, m, name, heads, cols, layer):
    w = m.table_d[name].shape[1]
    dh = cols // heads
    gat = layer is not None
    at = w - D

    def prod(half):
        return m.work[:, half, 0:K * cols]

    def turned_b(half):
        return m.psT[:, half, 0:K * P // 2].bitcast(BF16)

    def type_turned():
        return m.psC[0:NREL, 0, 0:K * P // 2].bitcast(BF16)

    with ExitStack() as ctx:
        s = Stage(nc, f"log_{name}")
        block = ctx.enter_context(nc.Block())

        @block.gpsimd
        def _(pool):
            gather(nc, m, s, pool, m.table_d[name], w, s("read"), True)

        @block.vector
        def _(dve):
            def finish(i, u):
                g = i * RING + u
                dve.wait_ge(s("reduced"), g + 1)
                dve.wait_ge(s("read"), g + 1)
                need(dve, s(f"lg{u}"), 16 * i)
                nc.vector.scalar_tensor_tensor(out=m.lg[:, u, 0:K * heads], in0=m.red[:, u % 2, :],
                                               scalar=1.0 - LEAK, in1=m.lin[:, u % 2, :], op0=ALU.mult,
                                               op1=ALU.add).then_inc(s("logits"), 1)

            def reduce(i, u):
                g = i * RING + u
                half = u % 2
                dve.wait_ge(s("products"), g + 1)
                if gat:
                    need(dve, s("logits"), g - 1)
                    nc.vector.tensor_reduce(m.red[:, half, :], prod(half).rearrange("p (k c) -> p k c", c=dh),
                                            AX.X, ALU.add).then_inc(s("reduced"), 1)
                else:
                    need(dve, s(f"lg{u}"), 16 * i)
                    nc.vector.tensor_reduce(m.lg[:, u, 0:K * heads],
                                            prod(half).rearrange("p (k c) -> p k c", c=dh), AX.X, ALU.add
                                            ).then_inc(s("logits"), 1)

            def products(g, slot):
                half = slot % 2
                apart, whole = K - PE_ADDS, K
                tiles = prod(half).rearrange("p (k c) -> p k c", k=K)
                sums = m.psA[:, half, :].rearrange("p (k c) -> p k c", k=K)
                att = m.att3[:, layer, :].unsqueeze(1)
                nc.vector.tensor_tensor(tiles[:, 0:apart, :], m.gx[:, slot, 0:apart, 0:cols], sums[:, 0:apart, :],
                                        ALU.add).then_inc(s("summed"), 1)
                if PE_ADDS:
                    nc.vector.scalar_tensor_tensor(out=tiles[:, apart:whole, :], in0=sums[:, apart:whole, :],
                                                   scalar=0.0, in1=att.to_broadcast([P, PE_ADDS, cols]),
                                                   op0=ALU.max, op1=ALU.mult)
                nc.vector.tensor_tensor(m.lin[:, half, :].rearrange("p (k h) -> p k h", k=K),
                                        m.gx[:, slot, :, W3:ROW3],
                                        m.psC[:, half, 0:K * H3].rearrange("p (k h) -> p k h", k=K), ALU.add
                                        ).then_inc(s("read"), 1)
                dve.wait_ge(s("summed"), g + 1)
                nc.vector.scalar_tensor_tensor(out=tiles[:, 0:apart, :], in0=tiles[:, 0:apart, :], scalar=0.0,
                                               in1=att.to_broadcast([P, apart, cols]), op0=ALU.max,
                                               op1=ALU.mult).then_inc(s("products"), 1)

            def body(i, u):
                g = i * RING + u
                need(dve, s("turned"), g)
                one_hot(nc, m, g + 3, (u + 3) % RING, True).then_inc(s("one_hot"), 1)
                if not gat:
                    need(dve, s("type_turned"), g - 1)
                    nc.vector.tensor_tensor(
                        m.typ[:, u % 2, :, :], m.iota_b[:, 0:NREL].unsqueeze(1).to_broadcast([P, K, NREL]),
                        m.et_f[:, bass.ds(g, 1), :].rearrange("p a k -> p (a k)").unsqueeze(2)
                        .to_broadcast([P, K, NREL]), ALU.is_equal).then_inc(s("type_hot"), 1)
                if gat and u > 1:
                    finish(i, u - 2)
                elif gat and (not isinstance(i, int) or i):
                    finish(i - 1, u + RING - 2)
                dve.wait_ge(s(f"rows{u}"), 16 * K * (i + 1))
                dve.wait_ge(s("projected"), g + 1)
                need(dve, s("logits"), g - 1)
                if gat:
                    products(g, u)
                else:
                    nc.vector.tensor_tensor(prod(u % 2).rearrange("p (k c) -> p k c", k=K), m.gx[:, u, :, 0:cols],
                                            m.psA[:, u % 2, 0:K * cols].rearrange("p (k c) -> p k c", k=K),
                                            ALU.mult).then_inc(s("products"), 1)
                    dve.wait_ge(s("products"), g + 1)
                    dve.sem_inc(s("read"), 1)
                if u:
                    reduce(i, u - 1)
                elif not isinstance(i, int) or i:
                    reduce(i - 1, RING - 1)
            for g in range(3):
                one_hot(nc, m, g, g, True).then_inc(s("one_hot"), 1)
            groups(dve, body)
            last = G // RING - 1
            if gat:
                finish(last, RING - 2)
            reduce(last, RING - 1)
            if gat:
                finish(last, RING - 1)

        @block.scalar
        def _(act):
            def turn(g, half):
                act.wait_ge(s("turned"), g + 1)
                need(act, s("projected"), g - 1)
                nc.scalar.copy(m.ohT[:, half, :], turned_b(half)).then_inc(s("ohT"), 1)

            def type_turn(g, half):
                act.wait_ge(s("type_turned"), g + 1)
                need(act, s("type_rows"), g - 1)
                nc.scalar.copy(m.typT[:, half, :], type_turned()).then_inc(s("typT"), 1)

            def type_out(i, u):
                g = i * RING + u
                act.wait_ge(s("type_rows"), g + 1)
                need(act, s(f"type_stored{u % 2}"), 16 * (2 * i + u // 2))
                nc.scalar.copy(m.type_out[:, u % 2, :], m.psC[:, 1, 0:K * TYPE_W]).then_inc(s("type_out"), 1)

            def body(i, u):
                turn(i * RING + u + 2, u % 2)
                if not gat:
                    type_turn(i * RING + u, u % 2)
                    if u:
                        type_out(i, u - 1)
                    elif not isinstance(i, int) or i:
                        type_out(i - 1, RING - 1)
            for g in range(2):
                turn(g, g)
            groups(act, body)
            if not gat:
                type_out(G // RING - 1, RING - 1)

        @block.tensor
        def _(pe):
            def turn(g, slot):
                pe.wait_ge(s("one_hot"), g + 1)
                need(pe, s("ohT"), g - 1)
                for k in range(K):
                    ins = nc.tensor.transpose(turned_b(slot % 2)[:, k * P:(k + 1) * P], m.oh_b[:, slot, k, :],
                                              m.ident_b[:, :])
                ins.then_inc(s("turned"), 1)

            def project(g, slot, turns_done):
                half = slot % 2
                blk = pe.value_load(m.blk_i[0:1, bass.ds(g, 1)], min_val=0, max_val=NB - 1)
                pe.wait_ge(s("ohT"), g + 1)
                need(pe, s("products" if gat else "read"), g - 1)
                rows = m.R[:, bass.ds(blk, 1), 0:cols].rearrange("p a c -> p (a c)")
                for k in range(K):
                    adds = gat and k >= K - PE_ADDS
                    if adds and k == K - PE_ADDS:
                        pe.wait_ge(s(f"rows{slot}"), 16 * K * turns_done)
                    to, turned = m.psA[:, half, k * cols:(k + 1) * cols], m.ohT[:, half, k * P:(k + 1) * P]
                    ins = nc.tensor.matmul(to, turned, rows, start=True, stop=not adds)
                    if adds:
                        ins = nc.tensor.matmul(to, m.ident[:, :], m.gx[:, slot, k, 0:cols], start=False, stop=True)
                    if gat:
                        ins = nc.tensor.matmul(m.psC[:, half, k * H3:(k + 1) * H3], turned,
                                               m.R[:, bass.ds(blk, 1), W3:ROW3].rearrange("p a c -> p (a c)"),
                                               start=True, stop=True)
                ins.then_inc(s("projected"), 1)

            def type_turn(g, half):
                pe.wait_ge(s("type_hot"), g + 1)
                need(pe, s("typT"), g)
                for k in range(K):
                    ins = nc.tensor.transpose(type_turned()[:, k * P:(k + 1) * P], m.typ[:, half, k, :],
                                              m.ident_b[:, :])
                ins.then_inc(s("type_turned"), 1)

            def type_rows(g, half):
                pe.wait_ge(s("typT"), g + 1)
                need(pe, s("type_out"), g)
                for k in range(K):
                    ins = nc.tensor.matmul(m.psC[:, 1, k * TYPE_W:(k + 1) * TYPE_W],
                                           m.typT[:, half, k * P:(k + 1) * P], m.relt[:, :], start=True, stop=True)
                ins.then_inc(s("type_rows"), 1)

            def body(i, u):
                g = i * RING + u
                if not (isinstance(g, int) and g == G - 1):
                    project(g + 1, (u + 1) % RING, i + 1 if u < RING - 1 else i + 2)
                turn(g + 2, (u + 2) % RING)
                if not gat:
                    type_turn(g, u % 2)
                    if u or not isinstance(i, int) or i:
                        type_rows(g - 1, (u + 1) % 2)
            for g in range(2):
                turn(g, g)
            project(0, 0, 1)
            groups(pe, body, G // RING - 1)
            for u in range(RING):
                body(G // RING - 1, u)
            if not gat:
                type_rows(G - 1, 1)

        @block.sync
        def _(sp):
            tview = m.type_d.rearrange("(g p k) w -> g p (k w)", p=P, k=K)
            lview = m.logit_d[name].rearrange("(g p k) h -> g p (k h)", p=P, k=K)
            xview = m.xs_d[name].rearrange("(g p k) d -> g p k d", p=P, k=K)

            def store_types(g, half):
                sp.wait_ge(s("type_out"), g + 1)
                sp.dma_start(tview[bass.ds(g, 1)].rearrange("a p w -> (a p) w"), m.type_out[:, half, :]
                             ).then_inc(s(f"type_stored{half}"), 16)

            def store(i, u):
                g = i * RING + u
                sp.wait_ge(s("logits"), g + 1)
                sp.dma_start(lview[bass.ds(g, 1)].rearrange("a p w -> (a p) w"), m.lg[:, u, 0:K * heads]
                             ).then_inc(s(f"lg{u}"), 16)

            def body(i, u):
                g = i * RING + u
                sp.wait_ge(s(f"rows{u}"), 16 * K * (i + 1))
                sp.dma_start(xview[bass.ds(g, 1)].rearrange("a p k d -> (a p) k d"), m.gx[:, u, :, at:at + D]
                             ).then_inc(s(f"xs{u}"), 16)
                if u:
                    store(i, u - 1)
                elif not isinstance(i, int) or i:
                    store(i - 1, RING - 1)
                if not gat and (u or not isinstance(i, int) or i):
                    store_types(g - 1, (u + 1) % 2)
            groups(sp, body)
            if not gat:
                store_types(G - 1, 1)
            store(G // RING - 1, RING - 1)
            for u in range(RING):
                sp.wait_ge(s(f"xs{u}"), 16 * (G // RING))
                sp.wait_ge(s(f"lg{u}"), 16 * (G // RING))
            for half in range(0 if gat else 2):
                sp.wait_ge(s(f"type_stored{half}"), 16 * (G // 2))


def softmax_parts(nc, m, name, heads):
    wide = RUN * heads
    L, F = m.big[:, 0:wide], m.big[:, wide:2 * wide]
    by_head = [t.rearrange("p (f h) -> p h f", h=heads) for t in (L, F)]
    gat = name != "t"
    PARTS = 4

    def cut(t, c):
        return t[:, c * wide // PARTS:(c + 1) * wide // PARTS]
    tail, flag, carry = (m.c8[:, n, 0:heads] for n in range(3))
    tail_r, flag_r, out_r, carry_r = (m.r8[0:heads, n, :] for n in range(4))

    with ExitStack() as ctx:
        s = Stage(nc, f"soft_{name}")
        block = ctx.enter_context(nc.Block())

        @block.sync
        def _(sp):
            sp.dma_start(L, m.logit_d[name].rearrange("(p f) h -> p (f h)", p=P)).then_inc(s("in"), 16)
            for c in range(PARTS):
                for ready, d, source in (("exp", m.prob_d, L), ("maxima", m.max_d, F))[:1 + gat]:
                    sp.wait_ge(s(ready), c + 1)
                    sp.dma_start(cut(d[name].rearrange("(p f) h -> p (f h)", p=P), c), cut(source, c)
                                 ).then_inc(s("out"), 16)
            sp.wait_ge(s("out"), 16 * PARTS * (1 + gat))

        @block.vector
        def _(dve):
            n = [0]

            def step(ins):
                n[0] += 1
                ins.then_inc(s("v"), 1)
                dve.wait_ge(s("v"), n[0])
            dve.wait_ge(s("in"), 16)
            for back in range(2):
                way = slice(None, None, -1) if back else slice(None)
                cuts = m.end_seg if back else m.new_seg
                edge = 0 if back else RUN - 1
                source = by_head[1 if back else 0]
                for h in range(heads):
                    ins = nc.vector.tensor_tensor_scan(by_head[1][:, h, way], cuts[:, way], source[:, h, way],
                                                       -BIG, ALU.add, ALU.max)
                step(ins)
                nc.vector.tensor_copy(tail, by_head[1][:, :, edge])
                step(nc.vector.tensor_reduce(m.c8[:, 3, 0:1], cuts[:, :], AX.X, ALU.min))
                step(nc.vector.tensor_copy(flag, m.c8[:, 3, 0:1].to_broadcast([P, heads])))
                dve.sem_inc(s("tails"), 1)
                dve.wait_ge(s("rows"), back + 1)
                nc.vector.tensor_copy(tail_r, m.psT[0:heads, 0, 0:P])
                step(nc.vector.tensor_copy(flag_r, m.psT[0:heads, 0, P:2 * P]))
                step(nc.vector.tensor_tensor_scan(out_r[:, way], flag_r[:, way], tail_r[:, way], -BIG,
                                                  ALU.add, ALU.max))
                if back:
                    nc.vector.memset(carry_r[:, P - 1:P], -BIG)
                    step(nc.vector.tensor_copy(carry_r[:, 0:P - 1], out_r[:, 1:P]))
                else:
                    nc.vector.memset(carry_r[:, 0:1], -BIG)
                    step(nc.vector.tensor_copy(carry_r[:, 1:P], out_r[:, 0:P - 1]))
                dve.sem_inc(s("carries"), 1)
                dve.wait_ge(s("cols"), back + 1)
                step(nc.vector.tensor_copy(carry, m.psT[:, 1, 0:heads]))
                for h in range(heads):
                    ins = nc.vector.tensor_tensor_scan(by_head[1][:, h, way], cuts[:, way], by_head[1][:, h, way],
                                                       carry[:, h:h + 1], ALU.add, ALU.max)
                step(ins)
            for c in range(PARTS):
                nc.vector.tensor_tensor(cut(L, c), cut(L, c), cut(F, c), ALU.subtract).then_inc(s("shifted"), 1)
                if gat:
                    f3 = cut(F, c).rearrange("p (f h) -> p f h", h=heads)
                    new = m.new_seg[:, c * RUN // PARTS:(c + 1) * RUN // PARTS]
                    dve.wait_ge(s("shifted"), c + 1)
                    nc.vector.scalar_tensor_tensor(out=f3, in0=new.unsqueeze(2).to_broadcast([P, RUN // PARTS, heads]),
                                                   scalar=-1.0, in1=f3, op0=ALU.is_lt, op1=ALU.mult
                                                   ).then_inc(s("maxima"), 1)

        @block.scalar
        def _(act):
            for c in range(PARTS):
                act.wait_ge(s("shifted"), c + 1)
                nc.scalar.activation(cut(L, c), cut(L, c), ACT.Exp).then_inc(s("exp"), 1)

        @block.tensor
        def _(pe):
            for back in range(2):
                pe.wait_ge(s("tails"), back + 1)
                nc.tensor.transpose(m.psT[0:heads, 0, 0:P], tail, m.ident[:, :])
                nc.tensor.transpose(m.psT[0:heads, 0, P:2 * P], flag, m.ident[:, :]).then_inc(s("rows"), 1)
                pe.wait_ge(s("carries"), back + 1)
                nc.tensor.transpose(m.psT[:, 1, 0:heads], carry_r, m.ident[0:heads, 0:heads]).then_inc(s("cols"), 1)


def weighted_sums(nc, m, name, heads, acc_w):
    gat = name != "t"
    cols = heads * D if gat else D
    extras = 3 if gat else 1
    parts, turns = 4, G // RING
    ends = (turns // 10, turns // 3, 2 * turns // 3, turns)
    n_loads = 2 if gat else 1
    w_all = m.probs[:, 0:G * K * heads].rearrange("p (g w) -> p g w", g=G)
    m_all = m.maxima.rearrange("p (g w) -> p g w", g=G)

    def rhs(half):
        return m.work[:, half, 0:K * acc_w].rearrange("p (k w) -> p k w", k=K)

    def sums(u):
        return (m.psC, m.psT)[u // 2][:, u % 2, 0:acc_w]

    with ExitStack() as ctx:
        s = Stage(nc, f"sum_{name}")
        block = ctx.enter_context(nc.Block())

        def in_parts(eng, body, load_part=None):
            for n, end in enumerate(ends):
                if load_part is None:
                    eng.wait_ge(s(f"part{n}"), 16 * n_loads)
                begin = ends[n - 1] if n else 2
                if n == 0:
                    for i in range(2):
                        for u in range(RING):
                            body(i, u)
                if load_part is not None and n + 1 < parts:
                    load_part(n + 1)
                with eng.Fori(begin, end, 1) as i:
                    for u in range(RING):
                        body(i, u)

        @block.sync
        def _(sp):
            xview = m.xs_d[name].rearrange("(g p k) d -> g p (k d)", p=P, k=K)

            def body(i, u):
                g = i * RING + u
                need(sp, s("added"), g - RING + 1)
                sp.dma_start(m.xl[:, u, :, :].rearrange("p k d -> p (k d)"),
                             xview[bass.ds(g, 1)].rearrange("a p w -> (a p) w")).then_inc(s(f"in{u}"), 16)

            def load_part(n):
                for to, d in ((w_all, m.prob_d), (m_all, m.max_d))[:n_loads]:
                    view = d[name].rearrange("(g p k) h -> p g (k h)", p=P, k=K)
                    lo, hi = (ends[n - 1] if n else 0) * RING, ends[n] * RING
                    sp.dma_start(to[:, lo:hi, :], view[:, lo:hi, :]).then_inc(s(f"part{n}"), 16)
            load_part(0)
            in_parts(sp, body, load_part)

        @block.gpsimd
        def _(pool):
            nc.gpsimd.memset(m.big[:, 0:NB * acc_w], 0.0).then_inc(s("acc"), 1)

        @block.vector
        def _(dve):
            def collect(i, u):
                add_up(nc, m, dve, i * RING + u, acc_w, sums(u), s).then_inc(s("acc"), 1)

            def body(i, u):
                g = i * RING + u
                weights = w_all[:, bass.ds(g, 1), :].rearrange("p a (k h) -> p (a k) h", k=K).unsqueeze(3)
                dve.wait_ge(s(f"in{u}"), 16 * (i + 1))
                need(dve, s("added"), g - 1)
                if gat:
                    shape = [P, K, heads, D]
                    p = weights.to_broadcast(shape)
                    x = m.xl[:, u, :, :].unsqueeze(2).to_broadcast(shape)
                    o = rhs(u % 2)[:, :, 0:cols].rearrange("p k (h c) -> p k h c", h=heads)
                else:
                    shape = [P, K, heads, D // heads]
                    p = weights.to_broadcast(shape)
                    x = m.xl[:, u, :, :].rearrange("p k (h c) -> p k h c", h=heads)
                    o = rhs(u % 2)[:, :, 0:cols].rearrange("p k (h c) -> p k h c", h=heads)
                nc.vector.tensor_tensor(o, p, x, ALU.mult).then_inc(s("rhs"), 1)
                one_hot(nc, m, g, u).then_inc(s("one_hot"), 1)
                if u > 1:
                    collect(i, u - 2)
                elif not isinstance(i, int) or i:
                    collect(i - 1, u + RING - 2)
            in_parts(dve, body)
            for u in (RING - 2, RING - 1):
                collect(turns - 1, u)

        @block.scalar
        def _(act):
            def body(i, u):
                g = i * RING + u
                need(act, s("added"), g - 1)
                r = rhs(u % 2)
                for n, source in enumerate((w_all, m_all)[:n_loads]):
                    nc.scalar.copy(r[:, :, cols + n * heads:cols + (n + 1) * heads],
                                   source[:, bass.ds(g, 1), :].rearrange("p a (k h) -> p (a k) h", k=K)
                                   ).then_inc(s("extra"), 1)
                if gat:
                    nc.scalar.copy(r[:, :, cols + 2 * heads:cols + 2 * heads + 1],
                                   m.first_t[:, bass.ds(g, 1), :].rearrange("p a k -> p k a")
                                   ).then_inc(s("extra"), 1)
            in_parts(act, body)

        @block.tensor
        def _(pe):
            def body(i, u):
                g = i * RING + u
                pe.wait_ge(s("one_hot"), g + 1)
                pe.wait_ge(s("rhs"), g + 1)
                pe.wait_ge(s("extra"), extras * (g + 1))
                need(pe, s("acc"), g - 2)
                for k in range(K):
                    ins = nc.tensor.matmul(sums(u), m.oh[:, u, k, :], rhs(u % 2)[:, k, :],
                                           start=(k == 0), stop=(k == K - 1))
                ins.then_inc(s("added"), 1)
            groups(pe, body)


def transformer_out(nc, m):
    acc = m.big[:, 0:NB * ACC0].rearrange("p (b w) -> p b w", b=NB)
    msg = acc[:, :, 0:D].rearrange("p b (h c) -> p b h c", h=H0)
    den = m.small[:, 0, :, 0:H0]
    steps = [range(b, min(b + 4, NB)) for b in range(0, NB, 4)]
    with ExitStack() as ctx:
        s = Stage(nc, "out_t")
        block = ctx.enter_context(nc.Block())

        @block.vector
        def _(dve):
            nc.vector.tensor_scalar(den, acc[:, :, D:D + H0], 1e-16, None, ALU.max).then_inc(s("den"), 1)
            dve.wait_ge(s("den"), 1)
            nc.vector.reciprocal(den, den).then_inc(s("den"), 1)
            dve.wait_ge(s("den"), 2)
            nc.vector.tensor_tensor(msg, msg, den.unsqueeze(3).to_broadcast([P, NB, H0, D // H0]), ALU.mult
                                    ).then_inc(s("msg"), 1)
            for b in range(NB):
                dve.wait_ge(s("made"), b + 1)
                nc.vector.tensor_copy(m.Y[:, b, :], m.psC[:, b % 2, 0:D]).then_inc(s("y"), 1)

        @block.scalar
        def _(act):
            for n, bs in enumerate(steps):
                act.wait_ge(s("turned"), n + 1)
                nc.scalar.copy(m.XT[0:D, bs[0] * P:(bs[-1] + 1) * P], m.psT[0:D, n % 2, 0:len(bs) * P]
                               ).then_inc(s("copied"), 1)

        @block.tensor
        def _(pe):
            pe.wait_ge(s("msg"), 1)
            for n, bs in enumerate(steps):
                need(pe, s("copied"), n - 1)
                for b in bs:
                    ins = nc.tensor.transpose(m.psT[0:D, n % 2, (b - bs[0]) * P:(b - bs[0] + 1) * P],
                                              acc[:, b, 0:D], m.ident[:, :])
                ins.then_inc(s("turned"), 1)
            pe.wait_ge(s("copied"), len(steps))
            for b in range(NB):
                need(pe, s("y"), b - 1)
                nc.tensor.matmul(m.psC[:, b % 2, 0:D], m.XT[0:D, b * P:(b + 1) * P], m.wo0[:, :], start=True,
                                 stop=True).then_inc(s("made"), 1)


def relation_walk(nc, m):
    name = "r"

    def xs(u):
        return m.gx[:, u, :, 0:D]

    def rhs(half):
        return m.work[:, half, :].rearrange("p (k w) -> p k w", k=K)

    turned = m.psT[:, 0, 0:K * P // 2].bitcast(BF16)

    with ExitStack() as ctx:
        s = Stage(nc, "rel")
        block = ctx.enter_context(nc.Block())

        @block.gpsimd
        def _(pool):
            gather(nc, m, s, pool, m.table_d[name], 2 * D, s("rhs"))

        @block.sync
        def _(sp):
            view = m.type_d.rearrange("(g p k) w -> g p (k w)", p=P, k=K)

            def body(i, u):
                g = i * RING + u
                need(sp, s("ac"), g - RING + 1)
                sp.dma_start(m.type_in[:, u, :, :].rearrange("p k w -> p (k w)"),
                             view[bass.ds(g, 1)].rearrange("a p w -> (a p) w")).then_inc(s(f"types{u}"), 16)
            groups(sp, body)

        @block.vector
        def _(dve):
            def node_hot(g, slot):
                one_hot(nc, m, g, slot).then_inc(s("node_hot"), 1)

            def collect(g, half, blk=None):
                add_up(nc, m, dve, g, ACC1, m.psA[:, half, :].rearrange("p (n w) -> p n w", n=2)[:, :, 0:ACC1 // 2],
                       s, blk).then_inc(s("acc"), 1)

            def dots(g, slot, turns_done):
                half = slot % 2
                y = m.lx[:, half, :, :]
                dve.wait_ge(s("fetched"), g + 1)
                dve.wait_ge(s(f"types{slot}"), 16 * turns_done)
                dve.wait_ge(s(f"rows{slot}"), 16 * K * turns_done)
                nc.vector.tensor_tensor(y, m.psC[:, half, 0:K * D].rearrange("p (k w) -> p k w", k=K),
                                        m.type_in[:, slot, :, 0:D], ALU.add).then_inc(s("y_hat"), 1)
                nc.vector.tensor_tensor(rhs(half)[:, :, NBASE * D:ACC1], xs(slot),
                                        m.last_t[:, bass.ds(g, 1), :].rearrange("p a k -> p (a k)").unsqueeze(2)
                                        .to_broadcast([P, K, D]), ALU.mult).then_inc(s("lastx"), 1)
                dve.wait_ge(s("y_hat"), g + 1)
                nc.vector.tensor_tensor(y, m.gx[:, slot, :, D:2 * D], y, ALU.mult).then_inc(s("dots"), 1)

            def score(g, half):
                dve.wait_ge(s("dots"), g + 1)
                nc.vector.tensor_reduce(m.a1[:, half, 0, :], m.lx[:, half, :, :], AX.X, ALU.add
                                        ).then_inc(s("score"), 1)

            def scaled(g, slot):
                half = slot % 2
                dve.wait_ge(s("tanh"), g + 1)
                need(dve, s("rhs"), g - 1)
                nc.vector.tensor_tensor(m.ac[:, half, :, :], m.type_in[:, slot, :, D:TYPE_W],
                                        m.a1[:, half, 2, :].unsqueeze(2).to_broadcast([P, K, NBASE]), ALU.mult
                                        ).then_inc(s("ac"), 1)

            def outer(g, slot):
                half = slot % 2
                dve.wait_ge(s("ac"), g + 1)
                shape = [P, K, NBASE, D]
                nc.vector.tensor_tensor(rhs(half)[:, :, 0:NBASE * D].rearrange("p k (b c) -> p k b c", b=NBASE),
                                        m.ac[:, half, :, :].unsqueeze(3).to_broadcast(shape),
                                        xs(slot).unsqueeze(2).to_broadcast(shape), ALU.mult).then_inc(s("rhs"), 1)

            def body(i, u, last=False):
                g = i * RING + u
                need(dve, s("added"), g - 1)
                outer(g, u)
                any_before = u or not isinstance(i, int) or i
                blk = block_of(m, dve, g - 1) if any_before else None
                need(dve, s("added"), g)
                if not last:
                    dots(g + 1, (u + 1) % RING, i + 1 if u < RING - 1 else i + 2)
                if any_before:
                    collect(g - 1, (u + 1) % 2, blk)
                if not last:
                    score(g + 1, (u + 1) % 2)
                    node_hot(g + 3, (u + 3) % RING)
                    scaled(g + 1, (u + 1) % RING)
            nc.vector.memset(m.big[:, 0:NB * ACC1], 0.0).then_inc(s("acc"), 1)
            for g in range(3):
                node_hot(g, g)
            dots(0, 0, 1)
            score(0, 0)
            scaled(0, 0)
            groups(dve, body, G // RING - 1)
            for u in range(RING):
                body(G // RING - 1, u, last=u == RING - 1)
            collect(G - 1, 1)

        @block.scalar
        def _(act):
            def narrow(g, slot):
                act.wait_ge(s("node_hot"), g + 1)
                need(act, s("turned"), g - 1)
                nc.scalar.copy(m.node_b[:, slot % 2, :, :], m.oh[:, slot, :, :]).then_inc(s("node_b"), 1)

            def turn(g, half):
                act.wait_ge(s("turned"), g + 1)
                need(act, s("fetched"), g - 1)
                nc.scalar.copy(m.ohT[:, half, :], turned).then_inc(s("ohT"), 1)

            def tanh(g, half):
                act.wait_ge(s("score"), g + 1)
                nc.scalar.activation(m.a1[:, half, 1, :], m.a1[:, half, 0, :], ACT.Relu, scale=D ** -0.5
                                     ).then_inc(s("relu"), 1)
                act.wait_ge(s("relu"), g + 1)
                nc.scalar.activation(m.a1[:, half, 2, :], m.a1[:, half, 1, :], ACT.Tanh).then_inc(s("tanh"), 1)

            def body(i, u, last=False):
                g = i * RING + u
                narrow(g + 2, (u + 2) % RING)
                turn(g + 2, u % 2)
                if not last:
                    tanh(g + 1, (u + 1) % 2)
            for g in range(2):
                narrow(g, g)
                turn(g, g)
            tanh(0, 0)
            groups(act, body, G // RING - 1)
            for u in range(RING):
                body(G // RING - 1, u, last=u == RING - 1)

        @block.tensor
        def _(pe):
            def turn(g, slot):
                pe.wait_ge(s("node_b"), g + 1)
                need(pe, s("ohT"), g)
                for k in range(K):
                    ins = nc.tensor.transpose(turned[:, k * P:(k + 1) * P], m.node_b[:, slot % 2, k, :],
                                              m.ident_b[:, :])
                ins.then_inc(s("turned"), 1)

            def add(g, slot):
                half = slot % 2
                pe.wait_ge(s("rhs"), g + 1)
                pe.wait_ge(s("lastx"), g + 1)
                need(pe, s("acc"), g)
                for n in range(2):
                    for k in range(K):
                        ins = nc.tensor.matmul(m.psA[:, half, n * 512:n * 512 + ACC1 // 2], m.oh[:, slot, k, :],
                                               rhs(half)[:, k, n * ACC1 // 2:(n + 1) * ACC1 // 2],
                                               start=(k == 0), stop=(k == K - 1))
                ins.then_inc(s("added"), 1)

            def fetch(g, half):
                blk = pe.value_load(m.blk_i[0:1, bass.ds(g, 1)], min_val=0, max_val=NB - 1)
                pe.wait_ge(s("ohT"), g + 1)
                need(pe, s("y_hat"), g - 1)
                rows = m.Rr[:, bass.ds(blk, 1), :].rearrange("p a c -> p (a c)")
                for k in range(K):
                    ins = nc.tensor.matmul(m.psC[:, half, k * D:(k + 1) * D], m.ohT[:, half, k * P:(k + 1) * P],
                                           rows, start=True, stop=True)
                ins.then_inc(s("fetched"), 1)

            def body(i, u):
                g = i * RING + u
                fetch(g + 1, (u + 1) % 2)
                turn(g + 2, (u + 2) % RING)
                add(g, u)
            for g in range(2):
                turn(g, g)
            fetch(0, 0)
            groups(pe, body)


def relational_out(nc, m):
    acc = m.big[:, 0:NB * ACC1].rearrange("p (b w) -> p b w", b=NB)
    nq = NBASE * D // P
    with ExitStack() as ctx:
        s = Stage(nc, "out_r")
        block = ctx.enter_context(nc.Block())

        @block.tensor
        def _(pe):
            def turn(b):
                need(pe, s("copied"), 2 * (b - 1))
                for q in range(nq):
                    nc.tensor.transpose(m.psA[:, b % 2, q * P:(q + 1) * P], acc[:, b, q * P:(q + 1) * P],
                                        m.ident[:, :])
                nc.tensor.transpose(m.psA[0:D, b % 2, 512:512 + P], acc[:, b, NBASE * D:ACC1], m.ident[:, :]
                                    ).then_inc(s("turned"), 1)
            turn(0)
            for b in range(NB):
                if b + 1 < NB:
                    turn(b + 1)
                pe.wait_ge(s("copied"), 2 * (b + 1))
                need(pe, s("y"), b - 1)
                zt = m.work[:, b % 2, :]
                for q in range(nq):
                    nc.tensor.matmul(m.psC[:, b % 2, 0:D], zt[:, q * P:(q + 1) * P], m.w1b[:, q, :], start=(q == 0),
                                     stop=False)
                nc.tensor.matmul(m.psC[:, b % 2, 0:D], zt[0:D, 512:512 + P], m.w1s[:, :], start=False, stop=True
                                 ).then_inc(s("made"), 1)

        @block.scalar
        def _(act):
            for b in range(NB):
                act.wait_ge(s("turned"), b + 1)
                need(act, s("made"), b - 1)
                zt = m.work[:, b % 2, :]
                nc.scalar.copy(zt[:, 0:512], m.psA[:, b % 2, 0:512]).then_inc(s("copied"), 1)
                nc.scalar.copy(zt[0:D, 512:512 + P], m.psA[0:D, b % 2, 512:512 + P]).then_inc(s("copied"), 1)

        @block.vector
        def _(dve):
            for b in range(NB):
                dve.wait_ge(s("made"), b + 1)
                nc.vector.tensor_scalar(m.Y[:, b, :], m.psC[:, b % 2, 0:D], 0.0, None, ALU.max).then_inc(s("y"), 1)


def relational(nc, m):

    def side(b, ps):
        return nc.vector.tensor_copy(m.Rr[:, b, :], ps)

    tables(nc, m, "r", m.w1[:, 0:D], m.w1[:, D:2 * D], lambda o, ps: nc.scalar.copy(o[:, D:2 * D], ps), side)
    relation_walk(nc, m)
    relational_out(nc, m)
    normalised(nc, m, "r", (m.X, m.Y))


def edge_tiles(nc, m, a):
    src_i, w_e = m.tile_tmp[:, 0, :].bitcast(I32), m.tile_tmp[:, 1, :]
    low_i, low = m.tile_tmp[:, 2, :].bitcast(I32), m.tile_tmp[:, 3, :]
    iota = m.work[:, 0, 0:QP]
    with ExitStack() as ctx:
        s = Stage(nc, "tiles")
        block = ctx.enter_context(nc.Block())

        @block.sync
        def _(sp):
            for dst, name in ((src_i, "src"), (m.dst_i[:, 0:TILES], "dst"), (w_e, "edge_weight")):
                sp.dma_start(dst, a[name][0:P * TILES].rearrange("(p t) -> p t", p=P)).then_inc(s("in"), 16)
            sp.dma_start(m.table_d["s0"].rearrange("(b p) d -> p b d", p=P), m.X[:, :, :]).then_inc(s("out"), 16)
            sp.wait_ge(s("in"), 48)
            sp.wait_ge(s("out"), 16)

        @block.gpsimd
        def _(pool):
            nc.gpsimd.iota(iota, [[1, QP]], base=0, channel_multiplier=0,
                           allow_small_or_imprecise_dtypes=True).then_inc(s("iota"), 1)

        @block.vector
        def _(dve):
            nc.vector.memset(m.dst_i[:, TILES:TILES + 2 * RING * K], 0)
            nc.vector.memset(m.zeros[:, :], 0.0)
            dve.wait_ge(s("iota"), 1)
            nc.vector.tensor_copy(m.iota_h[:, :], iota)
            dve.wait_ge(s("in"), 48)
            nc.vector.tensor_scalar(m.dst_i[:, 0:TILES], m.dst_i[:, 0:TILES], N - 1, None, ALU.min)
            nc.vector.tensor_scalar(low_i, src_i, Q - 1, None, ALU.bitwise_and).then_inc(s("v"), 1)
            nc.vector.tensor_scalar(src_i, src_i, Q.bit_length() - 1, None, ALU.arith_shift_right
                                    ).then_inc(s("v"), 1)
            dve.wait_ge(s("v"), 2)
            nc.vector.tensor_copy(low, low_i).then_inc(s("v"), 1)
            nc.vector.tensor_copy(m.src_col[:, :], src_i)
            dve.wait_ge(s("v"), 3)
            for q in range(Q):
                nc.vector.scalar_tensor_tensor(out=m.quad_w[:, :, q], in0=low, scalar=float(q), in1=w_e,
                                               op0=ALU.is_equal, op1=ALU.mult)


def smoothing_walk(nc, m, n):
    name = f"s{n}"
    turns = TILES // (K * RING)
    cols = ((0, 512), (512, QP))
    chunks = -(-QP // P)
    whole = QP // P
    out = m.work[:, 0, 0:chunks * P].rearrange("p (c w) -> p c w", w=P)

    with ExitStack() as ctx:
        s = Stage(nc, f"smooth_{name}")
        block = ctx.enter_context(nc.Block())

        @block.gpsimd
        def _(pool):
            gather(nc, m, s, pool, m.table_d[name], D, s("message"), index=m.dst_i, tiles=TILES)

        @block.vector
        def _(dve):
            def column_hots(g, half, ks):
                for k in ks:
                    ins = nc.vector.tensor_scalar(m.cols_hot[:, half, k, 0:QUADS], m.iota_h[:, 0:QUADS],
                                                  m.src_col[:, bass.ds(g * K + k, 1)], None, ALU.is_equal)
                return ins

            def body(i, u):
                g = i * RING + u
                half = u % 2
                dve.wait_ge(s(f"rows{u}"), 16 * K * (i + 1))
                need(dve, s("low"), g - 1)
                shape = [P, K, Q, D]
                nc.vector.tensor_tensor(m.msg[:, half, :].rearrange("p (k q d) -> p k q d", k=K, q=Q),
                                        m.quad_w[:, bass.ds(g * K, K), :].unsqueeze(3).to_broadcast(shape),
                                        m.gx[:, u, :, 0:D].unsqueeze(2).to_broadcast(shape), ALU.mult
                                        ).then_inc(s("message"), 1)
                need(dve, s("added"), g - 1)
                column_hots(g, half, range(K // 2))
                dve.wait_ge(s("high"), g + 1)
                dve.wait_ge(s("message"), g + 1)
                nc.vector.tensor_tensor(m.rest[:, half, :], m.msg[:, half, :], m.parts[:, half, 0, :], ALU.subtract
                                        ).then_inc(s("rest"), 1)
                column_hots(g, half, range(K // 2, K)).then_inc(s("col_hot"), 1)
                dve.wait_ge(s("middle"), g + 1)
                dve.wait_ge(s("rest"), g + 1)
                nc.vector.tensor_tensor(m.parts[:, half, 2, :], m.rest[:, half, :], m.parts[:, half, 1, :],
                                        ALU.subtract).then_inc(s("low"), 1)
            groups(dve, body, turns)
            dve.wait_ge(s("total"), 1)
            nc.vector.tensor_copy(m.big[:, 0:QP], m.psA[:, 0, 0:QP]).then_inc(s("sums"), 1)
            for bank in range(2):
                dve.wait_ge(s("turned"), bank + 1)
                c0, c1 = (0, 4) if bank == 0 else (4, whole)
                ins = nc.vector.tensor_copy(out[:, c0:c1, :].rearrange("p c w -> p (c w)"),
                                            m.psT[:, bank, 0:(c1 - c0) * P])
                if bank and chunks > whole:
                    ins = nc.vector.tensor_copy(out[0:QP - whole * P, whole, :],
                                                m.psT[0:QP - whole * P, bank, (whole - 4) * P:(chunks - 4) * P])
                ins.then_inc(s("out"), 1)

        @block.scalar
        def _(act):
            def body(i, u):
                g = i * RING + u
                half = u % 2
                need(act, s("added"), g - 1)
                act.wait_ge(s("message"), g + 1)
                nc.scalar.copy(m.parts[:, half, 0, :], m.msg[:, half, :]).then_inc(s("high"), 1)
                act.wait_ge(s("rest"), g + 1)
                nc.scalar.copy(m.parts[:, half, 1, :], m.rest[:, half, :]).then_inc(s("middle"), 1)
            groups(act, body, turns)

        @block.tensor
        def _(pe):
            for lo, hi in cols:
                nc.tensor.matmul(m.psA[:, 0, lo:hi], m.zeros[:, 0:P], m.zeros[:, 0:hi - lo], start=True, stop=False)

            def body(i, u):
                g = i * RING + u
                half = u % 2
                for part in ("col_hot", "high", "middle", "low"):
                    pe.wait_ge(s(part), g + 1)
                for k in range(K):
                    for j in range(3):
                        for lo, hi in ((0, 512), (512, QUADS)):
                            ins = nc.tensor.matmul(m.psA[:, 0, lo:hi], m.parts[:, half, j, k * P:(k + 1) * P],
                                                   m.cols_hot[:, half, k, lo:hi], start=False, stop=False)
                ins.then_inc(s("added"), 1)
            groups(pe, body, turns)
            for lo, hi in cols:
                ins = nc.tensor.matmul(m.psA[:, 0, lo:hi], m.zeros[:, 0:P], m.zeros[:, 0:hi - lo], start=False,
                                       stop=True)
            ins.then_inc(s("total"), 1)
            pe.wait_ge(s("sums"), 1)
            for c in range(chunks):
                width = min(P, QP - c * P)
                ins = nc.tensor.transpose(m.psT[0:width, c // 4, (c % 4) * P:(c % 4 + 1) * P],
                                          m.big[:, c * P:c * P + width], m.ident[:, :])
                if c in (3, chunks - 1):
                    ins.then_inc(s("turned"), 1)

        @block.sync
        def _(sp):
            rows = m.table_d[f"s{n + 1}"].rearrange("(r q) d -> r (q d)", q=Q)
            sp.wait_ge(s("out"), 2)
            sp.dma_start(rows[0:whole * P].rearrange("(c p) w -> p c w", p=P), out[:, 0:whole, :]
                         ).then_inc(s("stored"), 16)
            sp.dma_start(rows[whole * P:QP], out[0:QP - whole * P, whole, :]).then_inc(s("stored"), 16)
            sp.wait_ge(s("stored"), 32)


def smoothing(nc, m, a):
    edge_tiles(nc, m, a)
    for n in range(3):
        smoothing_walk(nc, m, n)
    with ExitStack() as ctx:
        s = Stage(nc, "smoothed")
        block = ctx.enter_context(nc.Block())

        @block.sync
        def _(sp):
            sp.dma_start(m.Y[:, :, :], m.table_d["s3"].rearrange("(b p) d -> p b d", p=P)).then_inc(s("in"), 16)
            sp.wait_ge(s("in"), 16)
    normalised(nc, m, "s", (m.X, m.Y))


def self_logits(nc, m, s, dve, l):
    xl = m.big[:, 0:NB * TAB3].rearrange("p (b w) -> p b w", b=NB)
    steps = [range(b, min(b + 4, NB)) for b in range(0, NB, 4)]

    def part(n):
        return m.work[:, n % 2, 0:len(steps[n]) * W3].rearrange("p (b w) -> p b w", w=W3)

    def reduce(n):
        bs = steps[n]
        dve.wait_ge(s("self_summed"), n + 1)
        nc.vector.scalar_tensor_tensor(out=part(n), in0=part(n), scalar=LEAK, in1=part(n), op0=ALU.mult,
                                       op1=ALU.max).then_inc(s("self_leaky"), 1)
        dve.wait_ge(s("self_leaky"), n + 1)
        nc.vector.tensor_tensor(part(n), part(n), m.att3[:, l, :].unsqueeze(1)
                                .to_broadcast([P, len(bs), W3]), ALU.mult).then_inc(s("self_weighted"), 1)
        dve.wait_ge(s("self_weighted"), n + 1)
        nc.vector.tensor_reduce(m.self3[:, bs[0]:bs[-1] + 1, :].rearrange("p b h -> p (b h)"),
                                part(n).rearrange("p b (h c) -> p (b h) c", c=D), AX.X, ALU.add
                                ).then_inc(s("self_logits"), 1)

    for n, bs in enumerate(steps):
        dve.wait_ge(s("tab"), bs[-1] + 1)
        dve.wait_ge(s("side"), bs[-1] + 1)
        need(dve, s("self_logits"), n - 1)
        nc.vector.tensor_tensor(part(n), xl[:, bs[0]:bs[-1] + 1, 0:W3], m.R[:, bs[0]:bs[-1] + 1, 0:W3], ALU.add
                                ).then_inc(s("self_summed"), 1)
        if n:
            reduce(n - 1)
    reduce(len(steps) - 1)


def attention_out(nc, m, l):
    acc = m.big[:, 0:NB * ACC3].rearrange("p (b w) -> p b w", b=NB)
    sums = acc[:, :, 0:W3].rearrange("p b (h c) -> p b h c", h=H3)
    own = m.big[:, NB * ACC3:NB * (ACC3 + W3)].rearrange("p (b h c) -> p b h c", b=NB, h=H3)
    den, top, flag = acc[:, :, W3:W3 + H3], acc[:, :, W3 + H3:W3 + 2 * H3], acc[:, :, ACC3 - 1:ACC3]
    most, e_self, e_edge, total, none = (m.small[:, n, :, :] for n in range(5))
    pairs = [range(b, min(b + 2, NB)) for b in range(0, NB, 2)]
    ends = (6, 12, 18, NB)
    with ExitStack() as ctx:
        s = Stage(nc, f"out_g{l}")
        block = ctx.enter_context(nc.Block())

        @block.vector
        def _(dve):
            n = [0]

            def step(ins):
                n[0] += 1
                ins.then_inc(s("v"), 1)
                dve.wait_ge(s("v"), n[0])
            step(nc.vector.tensor_scalar(none, flag.to_broadcast([P, NB, H3]), -1.0, BIG, ALU.add, ALU.mult))
            step(nc.vector.tensor_tensor(top, top, none, ALU.add))
            step(nc.vector.tensor_tensor(most, top, m.self3[:, :, :], ALU.max))
            step(nc.vector.tensor_tensor(e_self, m.self3[:, :, :], most, ALU.subtract))
            step(nc.vector.tensor_tensor(e_edge, top, most, ALU.subtract))
            dve.sem_inc(s("shifted"), 1)
            dve.wait_ge(s("exp"), 2)
            step(nc.vector.tensor_tensor(total, den, e_edge, ALU.mult))
            step(nc.vector.tensor_tensor(total, total, e_self, ALU.add))
            step(nc.vector.tensor_scalar(total, total, 1e-16, None, ALU.add))
            step(nc.vector.reciprocal(total, total))
            nc.vector.tensor_tensor(e_self, e_self, total, ALU.mult)
            step(nc.vector.tensor_tensor(e_edge, e_edge, total, ALU.mult))
            for lo, hi in zip((0,) + ends, ends):
                wide = [P, hi - lo, H3, D]
                part, self_part = sums[:, lo:hi], own[:, lo:hi]
                nc.vector.tensor_tensor(part, part, e_edge[:, lo:hi].unsqueeze(3).to_broadcast(wide), ALU.mult)
                step(nc.vector.tensor_tensor(self_part, m.X[:, lo:hi, :].unsqueeze(2).to_broadcast(wide),
                                             e_self[:, lo:hi].unsqueeze(3).to_broadcast(wide), ALU.mult))
                nc.vector.tensor_tensor(part, part, self_part, ALU.add).then_inc(s("sums"), 1)

        @block.scalar
        def _(act):
            def copy_out(n):
                bs = pairs[n]
                act.wait_ge(s("made"), n + 1)
                nc.scalar.copy(m.Z[:, bs[0]:bs[-1] + 1, :].rearrange("p b d -> p (b d)"),
                               m.psC[:, n % 2, 0:len(bs) * D]).then_inc(s("z"), 1)

            act.wait_ge(s("shifted"), 1)
            nc.scalar.activation(e_self, e_self, ACT.Exp).then_inc(s("exp"), 1)
            nc.scalar.activation(e_edge, e_edge, ACT.Exp).then_inc(s("exp"), 1)
            for n, bs in enumerate(pairs):
                act.wait_ge(s("turned"), n + 1)
                need(act, s("made"), n - 1)
                nc.scalar.copy(m.work[:, n % 2, 0:len(bs) * W3], m.psT[:, n % 2, 0:len(bs) * W3]
                               ).then_inc(s("copied"), 1)
                if n:
                    copy_out(n - 1)
            copy_out(len(pairs) - 1)

        @block.tensor
        def _(pe):
            def turn(n):
                need(pe, s("copied"), n - 1)
                pe.wait_ge(s("sums"), 1 + sum(end <= pairs[n][-1] for end in ends))
                for j, b in enumerate(pairs[n]):
                    for q in range(2):
                        at = j * W3 + q * P
                        ins = nc.tensor.transpose(m.psT[:, n % 2, at:at + P], acc[:, b, q * P:(q + 1) * P],
                                                  m.ident[:, :])
                ins.then_inc(s("turned"), 1)
            turn(0)
            for n, bs in enumerate(pairs):
                if n + 1 < len(pairs):
                    turn(n + 1)
                pe.wait_ge(s("copied"), n + 1)
                need(pe, s("z"), n - 1)
                for j in range(len(bs)):
                    for q in range(2):
                        at = j * W3 + q * P
                        ins = nc.tensor.matmul(m.psC[:, n % 2, j * D:(j + 1) * D], m.work[:, n % 2, at:at + P],
                                               m.w3o[:, l, q, :], start=(q == 0), stop=(q == 1))
                ins.then_inc(s("made"), 1)


def batch_normalised(nc, m, l, tag, leaky):
    mean, var, scale = (m.bnv[:, n, :] for n in range(3))
    wide = [P, NB, D]
    with ExitStack() as ctx:
        s = Stage(nc, f"bn{tag}")
        block = ctx.enter_context(nc.Block())

        def over_nodes(t):
            return t.unsqueeze(1).to_broadcast(wide)

        @block.vector
        def _(dve):
            n = [0]

            def step(ins):
                n[0] += 1
                ins.then_inc(s("v"), 1)
                dve.wait_ge(s("v"), n[0])

            def over_blocks(t):
                step(nc.vector.tensor_scalar(t[:, NB - 1, :], t[:, NB - 1, :], m.node_rows[:, 0:1], None, ALU.mult))
                nc.vector.tensor_reduce(m.sum_in[:, :], t[:, :, :].rearrange("p b d -> p d b"), AX.X, ALU.add
                                        ).then_inc(s("ready"), 1)
            step(nc.vector.tensor_tensor(m.Z[:, :, :], m.Z[:, :, :], over_nodes(m.bias3[:, l, :]), ALU.add))
            if leaky:
                step(nc.vector.scalar_tensor_tensor(out=m.Z[:, :, :], in0=m.Z[:, :, :], scalar=0.01,
                                                    in1=m.Z[:, :, :], op0=ALU.mult, op1=ALU.max))
            step(nc.vector.tensor_tensor(m.X[:, :, :], m.Z[:, :, :], m.X[:, :, :], ALU.add))
            over_blocks(m.X)
            dve.wait_ge(s("sums"), 1)
            step(nc.vector.tensor_scalar(mean, m.psC[:, 0, 0:D], 1.0 / N, None, ALU.mult))
            step(nc.vector.tensor_tensor(m.X[:, :, :], m.X[:, :, :], over_nodes(mean), ALU.subtract))
            step(nc.vector.tensor_tensor(m.Z[:, :, :], m.X[:, :, :], m.X[:, :, :], ALU.mult))
            over_blocks(m.Z)
            dve.wait_ge(s("root"), 1)
            step(nc.vector.reciprocal(scale, var))
            step(nc.vector.tensor_tensor(scale, scale, m.bn[:, l, 0, :], ALU.mult))
            step(nc.vector.tensor_tensor(m.X[:, :, :], m.X[:, :, :], over_nodes(scale), ALU.mult))
            nc.vector.tensor_tensor(m.X[:, :, :], m.X[:, :, :], over_nodes(m.bn[:, l, 1, :]), ALU.add)

        @block.tensor
        def _(pe):
            for n in range(2):
                pe.wait_ge(s("ready"), n + 1)
                nc.tensor.matmul(m.psC[:, n, 0:D], m.ones[:, :], m.sum_in[:, :], start=True, stop=True
                                 ).then_inc(s("sums"), 1)

        @block.scalar
        def _(act):
            act.wait_ge(s("sums"), 2)
            nc.scalar.activation(var, m.psC[:, 1, 0:D], ACT.Sqrt, bias=m.eps[:, 0:1], scale=1.0 / N
                                 ).then_inc(s("root"), 1)


def attention(nc, m):
    with ExitStack() as ctx:
        block = ctx.enter_context(nc.Block())

        @block.vector
        def _(dve):
            nc.vector.tensor_copy(m.Y[:, :, :], m.X[:, :, :])
    for l in range(3):
        name = f"g{l}"
        with nc.cleanup_on_exit():
            tables(nc, m, name, m.w3[:, l, 0, :], m.w3[:, l, 1, :],
                   lambda o, ps: nc.scalar.copy(o[:, 0:ROW3], ps),
                   lambda b, ps: nc.scalar.copy(m.R[:, b, :], ps), layer=l)
            logits(nc, m, name, H3, W3, l)
            softmax_parts(nc, m, name, H3)
            weighted_sums(nc, m, name, H3, ACC3)
            attention_out(nc, m, l)
            batch_normalised(nc, m, l, name, l < 2)
    normalised(nc, m, "g", (m.X, m.Y))


def transformer(nc, m):
    tables(nc, m, "t", m.w0[:, 0:2 * D], m.w0[:, 2 * D:3 * D],
           lambda o, ps: nc.scalar.copy(o, ps),
           lambda b, ps: nc.vector.tensor_scalar(m.R[:, b, 0:D], ps, (D // H0) ** -0.5, None, ALU.mult))
    logits(nc, m, "t", H0, D, None)
    softmax_parts(nc, m, "t", H0)
    weighted_sums(nc, m, "t", H0, ACC0)
    transformer_out(nc, m)
    normalised(nc, m, "t", (m.X, m.X, m.Y))


def program(nc, a, out):
    with ExitStack() as ctx:
        m = allocate(nc, ctx)
        with nc.cleanup_on_exit():
            constants(nc, m, a)
            cut(nc, m, a)
        with nc.cleanup_on_exit():
            transformer(nc, m)
        with nc.cleanup_on_exit():
            relational(nc, m)
        with nc.cleanup_on_exit():
            smoothing(nc, m, a)
        attention(nc, m)
        store(nc, m, out)


def store(nc, m, out):
    with ExitStack() as ctx:
        s = Stage(nc, "store")
        block = ctx.enter_context(nc.Block())

        @block.sync
        def _(sp):
            sp.dma_start(out[0:(NB - 1) * P, :].rearrange("(b p) d -> p b d", p=P), m.X[:, 0:NB - 1, :]
                         ).then_inc(s("out"), 16)
            sp.dma_start(out[(NB - 1) * P:N, :], m.X[0:TAIL, NB - 1, :]).then_inc(s("out"), 16)
            sp.wait_ge(s("out"), 32)



_INS = ["x", "src", "dst", "edges", "edge_weight", "L0_gnn_Wq", "L0_gnn_Wk", "L0_gnn_Wv", "L0_gnn_Wo",
        "L1_gnn_weight", "L1_gnn_w_comp", "L1_gnn_self_loop_weight", "L1_gnn_A1_w", "L1_gnn_A1_b", "L1_gnn_A2_w",
        "L1_gnn_A2_b", "L1_gnn_rel_emb", "L3_gnn_Wl", "L3_gnn_bl", "L3_gnn_Wr", "L3_gnn_br", "L3_gnn_att",
        "L3_gnn_conv_bias", "L3_gnn_bn_gamma", "L3_gnn_bn_beta"]
_PAD = {"src": 0, "dst": 1 << 20, "edges": (0, 1 << 20, 0), "edge_weight": 0}


def kernel(**inputs):
    import numpy as _np
    import concourse.bacc as _bacc
    from concourse import mybir as _mybir
    from concourse.bass_utils import run_bass_kernel_spmd as _run

    nc = _bacc.Bacc("TRN2", target_bir_lowering=False, num_devices=1)
    arrays, args = {}, {}
    inputs["edges"] = _np.stack([inputs["src"], inputs["dst"], inputs["edge_type_86"]], axis=1)
    for name in _INS:
        x = _np.ascontiguousarray(inputs[name])
        if name in _PAD:
            x = _np.concatenate([x, _np.full((GE,) + x.shape[1:], _PAD[name], x.dtype)])
        arrays[f"in_{name}_dram"] = x
        args[name] = nc.dram_tensor(f"in_{name}_dram", x.shape, _mybir.dt.from_np(x.dtype), kind="ExternalInput").ap()
    out = nc.dram_tensor("out_0_dram", (N, D), F32, kind="ExternalOutput").ap()
    program(nc, args, out)
    r = _run(nc, [arrays], core_ids=[0])
    return r.results[0]["out_0_dram"]
```
